# Optimizing a Trainium2 kernel written in Bass

```python
import numpy as np
import jax
import jax.numpy as jnp

def _softmax(x, axis=-1):
    return jax.nn.softmax(x, axis=axis)

def _gelu(x):
    return jax.nn.gelu(x, approximate=True)

def _silu(x):
    return jax.nn.silu(x)

def _sigmoid(x):
    return jax.nn.sigmoid(x)

def _layernorm(x, axis=-1, eps=1e-05):
    m = jnp.mean(x, axis=axis, keepdims=True)
    v = jnp.var(x, axis=axis, keepdims=True)
    return (x - m) / jnp.sqrt(v + eps)

def _scatter_add(tgt, idx, src, axis=0):
    return tgt.at[idx].add(src)

def _segment_sum(src, seg, n):
    return jax.ops.segment_sum(src, seg, n)
kernel_name = 'mk_adaln_d1_jaxref_r8_049148'

def setup_inputs(seed: int=0):
    np.random.seed(seed)
    _w = jnp.asarray

    def _L0_attn_setup():
        import jax, jax.numpy as jnp
        import numpy as np
        H = 16
        NOPE = 64
        ROPE = 64
        QK = NOPE + ROPE
        VD = 128
        QR = 682
        KVR = 32
        D = 256
        THETA = 128000.0
        EPS = 1e-06

        def rmsnorm(x, w):
            var = jnp.mean(jnp.square(x.astype(jnp.float32)), axis=-1, keepdims=True)
            return (x * jax.lax.rsqrt(var + EPS)).astype(x.dtype) * w

        def _pair_permute(t):
            b, h, s, d = t.shape
            return t.reshape(b, h, s, d // 2, 2).swapaxes(-1, -2).reshape(b, h, s, d)

        def _rotate_half(t):
            t1, t2 = jnp.split(t, 2, axis=-1)
            return jnp.concatenate([-t2, t1], axis=-1)

        def _rope(q_pe, k_pe, seq_len):
            inv_freq = 1.0 / THETA ** (jnp.arange(0, ROPE, 2, dtype=jnp.float32) / ROPE)
            pos = jnp.arange(seq_len, dtype=jnp.float32)
            freqs = pos[:, None] * inv_freq[None, :]
            emb = jnp.concatenate([freqs, freqs], axis=-1)
            cos = jnp.cos(emb)[None, None]
            sin = jnp.sin(emb)[None, None]
            q_pe = _pair_permute(q_pe)
            k_pe = _pair_permute(k_pe)
            q_pe = q_pe * cos + _rotate_half(q_pe) * sin
            k_pe = k_pe * cos + _rotate_half(k_pe) * sin
            return (q_pe, k_pe)
        key = jax.random.key(seed)
        ks = jax.random.split(key, 8)
        s = 0.02
        return {'x': jax.random.normal(ks[0], (2, 256, D), dtype=jnp.float32), 'q_a_w': jax.random.normal(ks[1], (QR, D), dtype=jnp.float32) * s, 'q_a_ln': jnp.ones((QR,), dtype=jnp.float32), 'q_b_w': jax.random.normal(ks[2], (H * QK, QR), dtype=jnp.float32) * s, 'kv_a_w': jax.random.normal(ks[3], (KVR + ROPE, D), dtype=jnp.float32) * s, 'kv_a_ln': jnp.ones((KVR,), dtype=jnp.float32), 'kv_b_w': jax.random.normal(ks[4], (H * (NOPE + VD), KVR), dtype=jnp.float32) * s, 'o_w': jax.random.normal(ks[5], (D, H * VD), dtype=jnp.float32) * s}
    _L0_attn_in = _L0_attn_setup()

    def _L0_ffn_setup():
        import jax, jax.numpy as jnp
        import numpy as np
        NUM_EXPERTS = 32
        TOP_K = 6
        N_GROUPS = 4
        N_LIMITED_GROUPS = 2
        key = jax.random.key(seed)
        ks = jax.random.split(key, 8)
        H, M = (256, 176)
        SH = 2 * M
        s = 0.02
        return {'hidden_states': jax.random.normal(ks[0], (4, 256, H), jnp.float32), 'gate_w': jax.random.normal(ks[1], (H, NUM_EXPERTS), jnp.float32) * s, 'w_gate': jax.random.normal(ks[2], (NUM_EXPERTS, H, M), jnp.float32) * s, 'w_up': jax.random.normal(ks[3], (NUM_EXPERTS, H, M), jnp.float32) * s, 'w_down': jax.random.normal(ks[4], (NUM_EXPERTS, M, H), jnp.float32) * s, 'sw_gate': jax.random.normal(ks[5], (H, SH), jnp.float32) * s, 'sw_up': jax.random.normal(ks[6], (H, SH), jnp.float32) * s, 'sw_down': jax.random.normal(ks[7], (SH, H), jnp.float32) * s}
    _L0_ffn_in = _L0_ffn_setup()
    _L0_c = _w((lambda *s: np.random.randn(*s).astype(np.float32) * 0.05)(1, 256))
    _L0_wmod = _w((lambda *s: np.random.randn(*s).astype(np.float32) * 0.05)(256, 6 * 256) * 256 ** (-0.5))
    _d = {'L0_attn_x': _L0_attn_in['x'], 'L0_attn_q_a_w': _L0_attn_in['q_a_w'], 'L0_attn_q_a_ln': _L0_attn_in['q_a_ln'], 'L0_attn_q_b_w': _L0_attn_in['q_b_w'], 'L0_attn_kv_a_w': _L0_attn_in['kv_a_w'], 'L0_attn_kv_a_ln': _L0_attn_in['kv_a_ln'], 'L0_attn_kv_b_w': _L0_attn_in['kv_b_w'], 'L0_attn_o_w': _L0_attn_in['o_w'], 'L0_ffn_gate_w': _L0_ffn_in['gate_w'], 'L0_ffn_w_gate': _L0_ffn_in['w_gate'], 'L0_ffn_w_up': _L0_ffn_in['w_up'], 'L0_ffn_w_down': _L0_ffn_in['w_down'], 'L0_ffn_sw_gate': _L0_ffn_in['sw_gate'], 'L0_ffn_sw_up': _L0_ffn_in['sw_up'], 'L0_ffn_sw_down': _L0_ffn_in['sw_down'], 'L0_c': _L0_c, 'L0_wmod': _L0_wmod}
    _x0 = _d['L0_attn_x']
    _d['L0_attn_x'] = jax.random.normal(jax.random.fold_in(jax.random.key(seed), 1), (1, 2048, 256), dtype=_x0.dtype)
    del _x0
    return _d

def reference(L0_attn_x, L0_attn_q_a_w, L0_attn_q_a_ln, L0_attn_q_b_w, L0_attn_kv_a_w, L0_attn_kv_a_ln, L0_attn_kv_b_w, L0_attn_o_w, L0_ffn_gate_w, L0_ffn_w_gate, L0_ffn_w_up, L0_ffn_w_down, L0_ffn_sw_gate, L0_ffn_sw_up, L0_ffn_sw_down, L0_c, L0_wmod):

    def _L0_attn_ref(x, q_a_w, q_a_ln, q_b_w, kv_a_w, kv_a_ln, kv_b_w, o_w):
        import jax, jax.numpy as jnp
        import numpy as np
        H = 16
        NOPE = 64
        ROPE = 64
        QK = NOPE + ROPE
        VD = 128
        QR = 682
        KVR = 32
        D = 256
        THETA = 128000.0
        EPS = 1e-06

        def rmsnorm(x, w):
            var = jnp.mean(jnp.square(x.astype(jnp.float32)), axis=-1, keepdims=True)
            return (x * jax.lax.rsqrt(var + EPS)).astype(x.dtype) * w

        def _pair_permute(t):
            b, h, s, d = t.shape
            return t.reshape(b, h, s, d // 2, 2).swapaxes(-1, -2).reshape(b, h, s, d)

        def _rotate_half(t):
            t1, t2 = jnp.split(t, 2, axis=-1)
            return jnp.concatenate([-t2, t1], axis=-1)

        def _rope(q_pe, k_pe, seq_len):
            inv_freq = 1.0 / THETA ** (jnp.arange(0, ROPE, 2, dtype=jnp.float32) / ROPE)
            pos = jnp.arange(seq_len, dtype=jnp.float32)
            freqs = pos[:, None] * inv_freq[None, :]
            emb = jnp.concatenate([freqs, freqs], axis=-1)
            cos = jnp.cos(emb)[None, None]
            sin = jnp.sin(emb)[None, None]
            q_pe = _pair_permute(q_pe)
            k_pe = _pair_permute(k_pe)
            q_pe = q_pe * cos + _rotate_half(q_pe) * sin
            k_pe = k_pe * cos + _rotate_half(k_pe) * sin
            return (q_pe, k_pe)
        B, S, _ = x.shape
        q = rmsnorm(x @ q_a_w.T, q_a_ln) @ q_b_w.T
        q = q.reshape(B, S, H, QK).transpose(0, 2, 1, 3)
        q_nope, q_pe = (q[..., :NOPE], q[..., NOPE:])
        ckv = x @ kv_a_w.T
        c, k_pe = (ckv[..., :KVR], ckv[..., KVR:])
        k_pe = k_pe[:, None, :, :]
        kv = rmsnorm(c, kv_a_ln) @ kv_b_w.T
        kv = kv.reshape(B, S, H, NOPE + VD).transpose(0, 2, 1, 3)
        k_nope, v = (kv[..., :NOPE], kv[..., NOPE:])
        q_pe, k_pe = _rope(q_pe, k_pe, S)
        query = jnp.concatenate([q_nope, q_pe], axis=-1)
        key = jnp.concatenate([k_nope, jnp.broadcast_to(k_pe, (B, H, S, ROPE))], axis=-1)
        scale = 1.0 / jnp.sqrt(jnp.float32(QK))
        scores = jnp.einsum('bhsd,bhtd->bhst', query, key) * scale
        attn = jax.nn.softmax(scores.astype(jnp.float32), axis=-1).astype(query.dtype)
        out = jnp.einsum('bhst,bhtd->bhsd', attn, v)
        out = out.transpose(0, 2, 1, 3).reshape(B, S, H * VD)
        return out @ o_w.T

    def _L0_ffn_ref(hidden_states, gate_w, w_gate, w_up, w_down, sw_gate, sw_up, sw_down):
        import jax, jax.numpy as jnp
        import numpy as np
        NUM_EXPERTS = 32
        TOP_K = 6
        N_GROUPS = 4
        N_LIMITED_GROUPS = 2
        B, S, H = hidden_states.shape
        E, K = (NUM_EXPERTS, TOP_K)
        x = hidden_states.reshape(-1, H)
        T = x.shape[0]
        scores = jax.nn.sigmoid(x @ gate_w)
        original_scores = scores
        epg = E // N_GROUPS
        sg = scores.reshape(T, N_GROUPS, epg)
        group_scores = jnp.max(sg, axis=-1)
        _, top_groups = jax.lax.top_k(group_scores, N_LIMITED_GROUPS)
        mask = jnp.ones((T, N_GROUPS), dtype=bool)
        mask = mask.at[jnp.arange(T)[:, None], top_groups].set(False)
        sg = jnp.where(mask[:, :, None], -jnp.inf, sg)
        masked_scores = sg.reshape(T, E)
        _, selected_experts = jax.lax.top_k(masked_scores, K)
        weights = jnp.take_along_axis(original_scores, selected_experts, axis=-1)
        weights = weights / jnp.sum(weights, axis=-1, keepdims=True)
        sel_flat = selected_experts.ravel()
        x_exp = jnp.repeat(x, K, axis=0)
        sort_idx = jnp.argsort(sel_flat)
        xs = x_exp[sort_idx]
        group_sizes = jnp.bincount(sel_flat, length=E).astype(jnp.int32)
        g = jax.lax.ragged_dot(xs, w_gate, group_sizes)
        u = jax.lax.ragged_dot(xs, w_up, group_sizes)
        d = jax.lax.ragged_dot(jax.nn.silu(g) * u, w_down, group_sizes)
        unsort_idx = jnp.argsort(sort_idx)
        out = d[unsort_idx].reshape(T, K, H)
        expert_out = jnp.sum(out * weights[..., None], axis=1)
        shared = jax.nn.silu(x @ sw_gate) * (x @ sw_up) @ sw_down
        return (expert_out + shared).reshape(B, S, H)
    x = L0_attn_x
    mod = (_silu(L0_c) @ L0_wmod).reshape(L0_c.shape[0], 6, 1, -1)
    sa, ca, ga, sb, cb, gb = (mod[:, 0], mod[:, 1], mod[:, 2], mod[:, 3], mod[:, 4], mod[:, 5])
    ga = (2 * (ga >= 0) - 1) * jnp.maximum(jnp.abs(ga), 0.25)
    gb = (2 * (gb >= 0) - 1) * jnp.maximum(jnp.abs(gb), 0.25)
    h = _layernorm(x, axis=-1) * (1 + ca) + sa
    x = x + ga * _L0_attn_ref(h, L0_attn_q_a_w, L0_attn_q_a_ln, L0_attn_q_b_w, L0_attn_kv_a_w, L0_attn_kv_a_ln, L0_attn_kv_b_w, L0_attn_o_w)
    h = _layernorm(x, axis=-1) * (1 + cb) + sb
    x = x + gb * _L0_ffn_ref(h, L0_ffn_gate_w, L0_ffn_w_gate, L0_ffn_w_up, L0_ffn_w_down, L0_ffn_sw_gate, L0_ffn_sw_up, L0_ffn_sw_down)
    return x

_drawn_inputs = setup_inputs


def setup_inputs(seed=0):
    import zlib

    import numpy as np

    out = dict(_drawn_inputs(seed))
    spreads = {'L0_attn_q_a_ln': (1.0, 0.6), 'L0_attn_kv_a_ln': (1.0, 0.6)}
    factors = {'L0_attn_q_a_w': 8.0,
     'L0_attn_q_b_w': 8.0,
     'L0_attn_kv_a_w': 8.0,
     'L0_attn_kv_b_w': 8.0,
     'L0_attn_o_w': 8.0,
     'L0_ffn_gate_w': 8.0,
     'L0_ffn_w_gate': 8.0,
     'L0_ffn_w_up': 8.0,
     'L0_ffn_w_down': 8.0,
     'L0_ffn_sw_gate': 8.0,
     'L0_ffn_sw_up': 8.0,
     'L0_ffn_sw_down': 8.0,
     'L0_c': 8.0,
     'L0_wmod': 8.0}
    for name, (base, spread) in spreads.items():
        noise = np.random.default_rng([zlib.crc32(name.encode()), seed]).standard_normal(out[name].shape)
        drawn = base * np.exp(spread * noise) if base else spread * noise
        out[name] = jnp.asarray(drawn.astype(out[name].dtype))
    for name, factor in factors.items():
        out[name] = (out[name] * factor).astype(out[name].dtype)
    return out
```

```python
from contextlib import ExitStack

import numpy as np

import concourse.bass as bass
from concourse import mybir

F32 = mybir.dt.float32
F32R = mybir.dt.float32r
I32 = mybir.dt.int32
U32 = mybir.dt.uint32
ALU = mybir.AluOpType
ACT = mybir.ActivationFunctionType
AX = mybir.AxisListType
ds = bass.ds

P = 128
S = 2048
D = 256
T = S // P
DK = D // P
H = 16
ROPE = 64
HALF = ROPE // 2
C = 32
QK = 128
V = 128
KA = ROPE + C
KS = KA + 1
QR = 682
RT = -(-QR // P)
RL = QR - (RT - 1) * P
HC = H * C
QC = 512
E = 32
TOPK = 6
GROUPS = 4
EPG = E // GROUPS
M = 176
MH = M // 2
SH = 2 * M
SLOT_TILES = S * TOPK // P + E
TILES = SLOT_TILES + 2 * T
STEPS_V = 4 * 4 + 2
SCALE = float(1.0 / np.sqrt(np.float32(QK)))
STEPS = 32
CP = 64


class Chain:

    def __init__(self, engine, semaphore):
        self.engine, self.semaphore, self.before, self.now = engine, semaphore, 0, 0

    def __call__(self, instruction):
        instruction.then_inc(self.semaphore, 1)
        self.now += 1
        self.engine.wait_ge(self.semaphore, self.before + self.now)

    def enter(self, i, each):
        self.start, self.each = self.before + self.now, each
        self.before, self.now = self.start + i * each, 0

    def leave(self, end, unit=1):
        assert self.now == self.each * unit, (self.now, self.each, unit)
        self.before, self.now = self.start + end * self.each, 0


def program(nc, a, out):
    top = ExitStack()
    with top:
        def sb(stack, name, cols, dt=F32, parts=P):
            return stack.enter_context(nc.sbuf_tensor(name, [parts, cols], dt))

        x = sb(top, "x", T * D)
        ident = sb(top, "ident", P)
        ones = sb(top, "ones", P)
        mod = sb(top, "mod", 6 * D)
        wov = sb(top, "wov", 4 * D)
        cbar = sb(top, "cbar", T * HC)
        slots_dram = nc.dram_tensor("expert_rows", [SLOT_TILES * P + S, D], F32, kind="Internal").ap()
        done_dram = nc.dram_tensor("expert_out", [TILES * P, D], F32, kind="Internal").ap()

        att = ExitStack()
        with att:
            hT = sb(att, "hT", DK * S)
            weff = sb(att, "weff", DK * H * KA)
            caug = sb(att, "caug", T * CP)
            cosq = sb(att, "cosq", S)
            sinq = sb(att, "sinq", S)
            k_hi = sb(att, "k_hi", S, F32R)
            k_lo = sb(att, "k_lo", S, F32R)
            mods_and_weights(nc, a, x, ident, ones, mod, wov, hT, weff, caug, cosq, sinq, k_hi, k_lo, slots_dram, cbar)
            attention(nc, hT, weff, caug, cosq, sinq, k_hi, k_lo, ident, cbar)
        ffn(nc, a, x, ident, mod, wov, cbar, slots_dram, done_dram, out)


def mods_and_weights(nc, a, x, ident, ones, mod, wov, hT, weff, caug, cosq, sinq, k_hi, k_lo, slots_dram, cbar):
    st = ExitStack()
    with st:
        def sb(name, cols, dt=F32):
            return st.enter_context(nc.sbuf_tensor(name, [P, cols], dt))

        def pb(name, banks=1):
            return st.enter_context(nc.psum_tensor(name, [P, 512 * banks], F32))

        def sem(name):
            return st.enter_context(nc.semaphore(name))

        ccol = sb("ccol", 3 * DK)
        cwide = sb("cwide", DK * P)
        gate_sign = sb("gate_sign", D)
        wqaT = sb("wqaT", DK * QR)
        wqa = sb("wqa", RT * D)
        lnq = sb("lnq", RT)
        wkvT = sb("wkvT", DK * KA)
        lnkv = sb("lnkv", C)
        fold = sb("fold", H * KA)
        wv = cbar[:, H * D:H * D + H * C]
        woT = cbar[:, 0:H * D]
        wqb = sb("wqb", 2 * QR)
        afold = sb("afold", RT * H * KA)
        wmod = afold[:, 0:DK * 6 * D]
        hbuf = sb("hbuf", 2 * D)
        hTb = sb("hTb", 2 * D)
        stats = sb("stats", T * 6)
        mv = sb("mv", T * 2)
        rstd = sb("rstd", T)
        ckv = cbar[:, 5120:5120 + T * KA]
        junk = sb("junk", 512)
        ssq = sb("ssq", T * 3)
        rq = sb("rq", T)
        rc = sb("rc", T)
        tmp16 = sb("tmp16", T * 4)
        diag = sb("diag", 2 * P)
        kbuf = sb("kbuf", 4 * KA)
        rot_a = sb("rot_a", QC)
        rot_b = sb("rot_b", QC)
        kraw = sb("kraw", QC)
        zeros = cbar[:, 7168:7168 + 2 * D]

        pw = [pb("pw0", 2), pb("pw1", 2)]
        pt = [pb("pt0"), pb("pt1")]
        pk = [pb("pk0"), pb("pk1")]

        ld_x = sem("ld_x")
        ld_mod = sem("ld_mod")
        ld_w = sem("ld_w")
        ld_qb = [sem("ld_qb0"), sem("ld_qb1")]
        zeroed = sem("zeroed")
        consts = sem("consts")
        exp_c = sem("exp_c")
        silu_c = sem("silu_c")
        mod_mm = sem("mod_mm")
        mod_used = sem("mod_used")
        mod_copied = sem("mod_copied")
        dve = sem("dve")
        pool = sem("pool")
        var_ready = sem("var_ready")
        stats_ready = sem("stats_ready")
        rstd_ready = sem("rstd_ready")
        h_ready = sem("h_ready")
        ht_mm = sem("ht_mm")
        ht_ready = sem("ht_ready")
        kv_mm = sem("kv_mm")
        kv_ready = sem("kv_ready")
        squares_ready = sem("squares_ready")
        sums_ready = sem("sums_ready")
        roots_ready = sem("roots_ready")
        k_ready = sem("k_ready")
        k_mm = sem("k_mm")
        k_used = sem("k_used")
        diag_ready = sem("diag_ready")
        rq_mm = sem("rq_mm")
        rq_used = sem("rq_used")
        fold_ready = sem("fold_ready")
        a_mm = sem("a_mm")
        a_used = sem("a_used")
        w_mm = sem("w_mm")
        w_used = sem("w_used")
        ov_mm = sem("ov_mm")
        ov_used = sem("ov_used")

        block = st.enter_context(nc.Block())

        NLW = 9

        @block.sync
        def _(sp):
            sp.sem_inc(a_mm, 2)
            sp.dma_start(x[:, :].rearrange("p (t d) -> p t d", t=T),
                         a["x"].rearrange("(t p) d -> p t d", p=P)).then_inc(ld_x, 16)
            sp.dma_start(ccol[:, 0:DK], a["c"]).then_inc(ld_mod, 16)
            sp.dma_start(wmod.rearrange("p (k n) -> p k n", k=DK),
                         a["wmod"].rearrange("(k p) n -> p k n", p=P)).then_inc(ld_mod, 16)
            sp.dma_start(wqaT[:, :].rearrange("p (k n) -> p k n", k=DK),
                         a["wqaT"].rearrange("(k p) n -> p k n", p=P)).then_inc(ld_w, 16)
            sp.dma_start(wkvT[:, :].rearrange("p (k n) -> p k n", k=DK),
                         a["wkvT"].rearrange("(k p) n -> p k n", p=P)).then_inc(ld_w, 16)
            sp.dma_start(lnkv[:, :], a["lnkv"]).then_inc(ld_w, 16)
            sp.dma_start(cosq[0:ROPE, :], a["cos"]).then_inc(ld_w, 16)
            sp.dma_start(sinq[0:ROPE, :], a["sin"]).then_inc(ld_w, 16)
            sp.dma_start(wqa[:, 0:(RT - 1) * D].rearrange("p (k n) -> p k n", n=D),
                         a["wqa"][0:(RT - 1) * P, :].rearrange("(k p) n -> p k n", p=P)).then_inc(ld_w, 16)
            sp.dma_start(wqa[0:RL, (RT - 1) * D:RT * D], a["wqa"][(RT - 1) * P:QR, :]).then_inc(ld_w, 16)
            sp.dma_start(lnq[:, :], a["lnq"]).then_inc(ld_w, 16)
            sp.dma_start(woT, a["woT"]).then_inc(ld_w, 16)
            sp.dma_start(wv, a["wv"]).then_inc(fold_ready, 16)
            sp.wait_ge(consts, 4)
            sp.dma_start(fold[ROPE:P, :].rearrange("p (h n) -> p h n", h=H)[:, :, ROPE:KA],
                         a["wk"].rearrange("p (h n) -> p h n", h=H)).then_inc(fold_ready, 16)
            with sp.Fori(0, H // 2) as trip_no:
                h = trip_no * 2
                for u in range(2):
                    sp.wait_ge(a_mm, h + u + 1)
                    sp.dma_start(wqb[:, u * QR:(u + 1) * QR],
                                 a["wqb"][:, ds((h + u) * QR, QR)]).then_inc(ld_qb[u], 16)

        @block.gpsimd
        def _(gp):
            step = Chain(gp, pool)
            step(gp.memset(ident[:, :], 0.0))
            step(gp.affine_select(out=ident[:, :], in_=ident[:, :], compare_op=ALU.not_equal, fill=1.0,
                                  base=0, pattern=[[-1, P]], channel_multiplier=1))
            step(gp.memset(ones[:, :], 1.0))
            step(gp.memset(zeros, 0.0))
            step(gp.memset(k_hi[KA:KS, :].bitcast(F32), 1.0))
            step(gp.memset(k_lo[KA:KS, :].bitcast(F32), 0.0))
            step(gp.memset(fold[:, :], 0.0))
            step(gp.memset(caug[:, :], 0.0))
            step(gp.memset(caug[:, :].rearrange("p (t n) -> p t n", t=T)[:, :, C:C + 1], 1.0))
            step(gp.tensor_copy(fold[0:ROPE, :].rearrange("p (h n) -> p h n", h=H)[:, :, 0:ROPE],
                                ident[0:ROPE, 0:ROPE].rearrange("p (h n) -> p h n", h=1).to_broadcast([ROPE, H, ROPE])))
            gp.sem_inc(consts, 4)
            rows = slots_dram.rearrange("(n p r) d -> n p (r d)", p=P, r=2)
            with gp.Fori(0, SLOT_TILES // 2) as n:
                gp.dma_start(rows[ds(n, 1), :, :].rearrange("a p n -> (a p) n"), zeros).then_inc(zeroed, 16)
            gp.wait_ge(zeroed, 16 * (SLOT_TILES // 2))

        @block.scalar
        def _(act):
            act.wait_ge(ld_mod, 32)
            act.activation(ccol[:, DK:2 * DK], ccol[:, 0:DK], ACT.Exp, scale=-1.0).then_inc(exp_c, 1)
            act.wait_ge(var_ready, 1)
            act.activation(rstd[:, :], tmp16[:, 0:T], ACT.Sqrt).then_inc(rstd_ready, 1)
            with act.Fori(0, T // 2) as trip_no:
                t = trip_no * 2
                for u in range(2):
                    act.wait_ge(ht_mm, t + u + 3)
                    act.wait_ge(kv_mm, t + u + 1)
                    act.copy(hTb[:, u * D:(u + 1) * D], pt[u][:, 0:D]).then_inc(ht_ready, 1)
                    act.copy(hT[:, :].rearrange("p (k s) -> p k s", k=DK)[:, :, ds((t + u) * P, P)],
                             pt[u][:, 0:D].rearrange("p (k s) -> p k s", k=DK)).then_inc(ht_ready, 1)
                    act.wait_ge(kv_mm, t + u + 3)
                    for c in range(2):
                        act.activation(pw[u][:, c * 512:c * 512 + 341], pw[u][:, c * 512:c * 512 + 341], ACT.Square,
                                       accum_out=ssq[:, ds((t + u) * 3 + c, 1)])
                    act.wait_ge(kv_ready, t + u + 3)
                    act.activation(junk[:, ds((t + u) * C, C)], ckv[:, ds((t + u) * KA + ROPE, C)], ACT.Square,
                                   accum_out=ssq[:, ds((t + u) * 3 + 2, 1)]).then_inc(squares_ready, 1)
            act.wait_ge(sums_ready, 2)
            act.activation(rq[:, :], tmp16[:, 0:T], ACT.Sqrt).then_inc(roots_ready, 1)
            act.activation(rc[:, :], tmp16[:, T:2 * T], ACT.Sqrt).then_inc(roots_ready, 1)

        @block.vector
        def _(v):
            step = Chain(v, dve)
            v.wait_ge(exp_c, 1)
            v.wait_ge(consts, 4)
            step(v.tensor_scalar(ccol[:, DK:2 * DK], ccol[:, DK:2 * DK], 1.0, None, ALU.add))
            step(v.reciprocal(ccol[:, 2 * DK:3 * DK], ccol[:, DK:2 * DK]))
            step(v.tensor_tensor(ccol[:, 2 * DK:3 * DK], ccol[:, 2 * DK:3 * DK], ccol[:, 0:DK], ALU.mult))
            for k in range(DK):
                v.tensor_scalar(cwide[:, k * P:(k + 1) * P], ones[:, :], ccol[:, 2 * DK + k:2 * DK + k + 1], None,
                                ALU.mult).then_inc(silu_c, 1)
            v.wait_ge(ld_x, 16)
            with v.Fori(0, T) as t:
                v.bn_stats(stats[:, ds(t * 6, 6)], x[:, ds(t * D, D)]).then_inc(stats_ready, 1)
            v.wait_ge(stats_ready, T)
            for t in range(T):
                last = v.bn_aggr(mv[:, t * 2:(t + 1) * 2], stats[:, t * 6:(t + 1) * 6])
            step(last)
            var = mv[:, :].rearrange("p (t n) -> p t n", n=2)[:, :, 1]
            v.tensor_scalar(tmp16[:, 0:T], var, 1e-5, None, ALU.add).then_inc(var_ready, 1)
            for c in range(3):
                v.wait_ge(mod_mm, c + 1)
                v.tensor_copy(mod[:, c * 512:(c + 1) * 512], pw[c % 2][:, 0:512]).then_inc(mod_used, 1)
            v.wait_ge(mod_used, 3)
            for part in (1, 4):
                step(v.tensor_scalar(mod[:, part * D:(part + 1) * D], mod[:, part * D:(part + 1) * D], 1.0, None,
                                     ALU.add))
            for part in (2, 5):
                g = mod[:, part * D:(part + 1) * D]
                step(v.tensor_scalar(gate_sign[:, :], g, 0.0, 2.0, ALU.is_ge, ALU.mult))
                step(v.tensor_scalar(gate_sign[:, :], gate_sign[:, :], -1.0, None, ALU.add))
                step(v.tensor_tensor(g, g, gate_sign[:, :], ALU.mult))
                step(v.scalar_tensor_tensor(out=g, in0=g, scalar=0.25, in1=gate_sign[:, :], op0=ALU.max,
                                            op1=ALU.mult))
            v.wait_ge(rstd_ready, 1)
            step(v.reciprocal(rstd[:, :], rstd[:, :]))
            with v.Fori(0, T // 2) as trip_no:
                t = trip_no * 2
                step.enter(t, 2)
                for u in range(2):
                    hb = hbuf[:, u * D:(u + 1) * D]
                    v.wait_ge(ht_mm, t + u + 1)
                    step(v.tensor_scalar(hb, x[:, ds((t + u) * D, D)], mv[:, ds((t + u) * 2, 1)],
                                         rstd[:, ds(t + u, 1)], ALU.subtract, ALU.mult))
                    step(v.tensor_tensor(hb, hb, mod[:, D:2 * D], ALU.mult))
                    v.tensor_tensor(hb, hb, mod[:, 0:D], ALU.add).then_inc(h_ready, 1)
                for u in range(2):
                    v.wait_ge(kv_mm, t + u + 3)
                    v.tensor_copy(ckv[:, ds((t + u) * KA, KA)], pk[u][:, 0:KA]).then_inc(kv_ready, 1)
            step.leave(T, 2)
            v.wait_ge(squares_ready, T + 2)
            s3 = ssq[:, :].rearrange("p (t n) -> p t n", n=3)
            step(v.tensor_tensor(tmp16[:, 0:T], s3[:, :, 0], s3[:, :, 1], ALU.add))
            v.tensor_scalar(tmp16[:, 0:T], tmp16[:, 0:T], 1.0 / QR, 1e-6, ALU.mult, ALU.add).then_inc(sums_ready, 1)
            v.tensor_scalar(tmp16[:, T:2 * T], s3[:, :, 2], 1.0 / C, 1e-6, ALU.mult, ALU.add).then_inc(sums_ready, 1)
            v.wait_ge(roots_ready, 2)
            step(v.reciprocal(rq[:, :], rq[:, :]))
            step(v.reciprocal(rc[:, :], rc[:, :]))
            v.wait_ge(ld_w, 16 * NLW)
            v.wait_ge(kv_ready, T + 2)
            with v.Fori(0, T // 4) as q:
                step.enter(q, 6)
                for j in range(4):
                    t = q * 4 + j
                    if j == 0:
                        v.wait_ge(k_used, q + 1)
                    v.tensor_copy(kbuf[:, j * KA:j * KA + ROPE], ckv[:, ds(t * KA, ROPE)]).then_inc(k_ready, 1)
                    v.scalar_tensor_tensor(out=kbuf[:, j * KA + ROPE:(j + 1) * KA], in0=ckv[:, ds(t * KA + ROPE, C)],
                                           scalar=rc[:, ds(t, 1)], in1=lnkv[:, :], op0=ALU.mult,
                                           op1=ALU.mult).then_inc(k_ready, 1)
                    v.scalar_tensor_tensor(out=caug[:, ds(t * CP, C)], in0=ckv[:, ds(t * KA + ROPE, C)],
                                           scalar=rc[:, ds(t, 1)], in1=lnkv[:, :], op0=ALU.mult,
                                           op1=ALU.mult).then_inc(k_ready, 1)
                v.wait_ge(k_mm, q + 1)
                step(v.tensor_tensor(rot_a[0:ROPE, :], pk[0][0:ROPE, :], cosq[0:ROPE, ds(q * QC, QC)], ALU.mult))
                step(v.tensor_tensor(rot_b[HALF:ROPE, :], pk[0][0:HALF, :], sinq[0:HALF, ds(q * QC, QC)], ALU.mult))
                step(v.tensor_tensor(rot_b[0:HALF, :], pk[0][HALF:ROPE, :], sinq[HALF:ROPE, ds(q * QC, QC)], ALU.mult))
                step(v.tensor_tensor(kraw[0:ROPE, :], rot_a[0:ROPE, :], rot_b[0:ROPE, :], ALU.add))
                step(v.tensor_copy(kraw[ROPE:KA, :], pk[0][ROPE:KA, :]))
                step(v.tensor_copy(k_hi[0:KA, ds(q * QC, QC)], kraw[0:KA, :]))
                v.tensor_tensor(k_lo[0:KA, ds(q * QC, QC)], kraw[0:KA, :],
                                k_hi[0:KA, ds(q * QC, QC)].bitcast(F32), ALU.subtract).then_inc(k_used, 1)
                v.wait_ge(k_used, q + 2)
            step.leave(T // 4)
            with v.Fori(0, T // 2) as trip_no:
                t = trip_no * 2
                for u in range(2):
                    v.wait_ge(rq_used, t + u + 1)
                    v.tensor_scalar(diag[:, u * P:(u + 1) * P], ident[:, :], rq[:, ds(t + u, 1)], None,
                                    ALU.mult).then_inc(diag_ready, 1)
                for u in range(2):
                    v.wait_ge(rq_mm, t + u + 1)
                    tok = ds((t + u) * P, P)
                    v.tensor_tensor(cosq[0:ROPE, tok], cosq[0:ROPE, tok], pt[u][0:ROPE, 0:P], ALU.mult)
                    v.tensor_tensor(sinq[0:ROPE, tok], sinq[0:ROPE, tok], pt[u][0:ROPE, 0:P], ALU.mult)
                    v.tensor_copy(cosq[ROPE:KA, tok], pt[u][ROPE:KA, 0:P]).then_inc(rq_used, 1)
            with v.Fori(0, H // 2) as trip_no:
                h = trip_no * 2
                for u in range(2):
                    v.wait_ge(a_mm, h + u + 3)
                    for r in range(RT):
                        n = P if r < RT - 1 else RL
                        src = pw[u][0:n, (r // 3) * 512 + (r % 3) * KA:(r // 3) * 512 + (r % 3 + 1) * KA]
                        last = v.tensor_scalar(afold[0:n, ds((h + u) * KA + r * H * KA, KA)], src, lnq[0:n, r:r + 1],
                                               None, ALU.mult)
                    last.then_inc(a_used, 1)
            for c in range(3):
                for k in range(DK):
                    n = c * DK + k
                    v.wait_ge(w_mm, n + 1)
                    v.tensor_copy(weff[:, k * H * KA + c * 512:k * H * KA + (c + 1) * 512],
                                  pt[n % 2][:, :]).then_inc(w_used, 1)
            for g in range(4):
                v.wait_ge(ov_mm, g + 1)
                v.tensor_copy(wov[:, g * D:(g + 1) * D], pk[g % 2][:, 0:D]).then_inc(ov_used, 1)

        @block.tensor
        def _(pe):
            pe.wait_ge(silu_c, DK)
            for c in range(3):
                if c == 2:
                    pe.wait_ge(mod_used, 1)
                for k in range(DK):
                    last = pe.matmul(pw[c % 2][:, 0:512], cwide[:, k * P:(k + 1) * P],
                                     wmod[:, k * 6 * D + c * 512:k * 6 * D + (c + 1) * 512],
                                     start=(k == 0), stop=(k == DK - 1))
                last.then_inc(mod_mm, 1)
            pe.wait_ge(mod_used, 3)
            pe.wait_ge(ld_w, 16 * NLW)
            for s in (ht_mm, kv_mm, squares_ready, kv_ready):
                pe.sem_inc(s, 2)
            with pe.Fori(0, T // 2) as trip_no:
                t = trip_no * 2
                for u in range(2):
                    pe.wait_ge(h_ready, t + u + 1)
                    for k in range(DK):
                        last = pe.transpose(pt[u][:, k * P:(k + 1) * P], hbuf[:, u * D + k * P:u * D + (k + 1) * P],
                                            ident[:, :])
                    last.then_inc(ht_mm, 1)
                    pe.wait_ge(ht_ready, 2 * (t + u) + 2)
                    pe.wait_ge(squares_ready, t + u + 1)
                    pe.wait_ge(kv_ready, t + u + 1)
                    for c in range(2):
                        for k in range(DK):
                            last = pe.matmul(pw[u][:, c * 512:c * 512 + 341], hTb[:, u * D + k * P:u * D + (k + 1) * P],
                                             wqaT[:, k * QR + c * 341:k * QR + (c + 1) * 341],
                                             start=(k == 0), stop=(k == DK - 1))
                    for k in range(DK):
                        last = pe.matmul(pk[u][:, 0:KA], hTb[:, u * D + k * P:u * D + (k + 1) * P],
                                         wkvT[:, k * KA:(k + 1) * KA], start=(k == 0), stop=(k == DK - 1))
                    last.then_inc(kv_mm, 1)
            pe.wait_ge(kv_ready, T + 2)
            pe.wait_ge(squares_ready, T + 2)
            pe.sem_inc(k_used, 1)
            with pe.Fori(0, T // 4) as q:
                pe.wait_ge(k_ready, 12 * q + 12)
                pe.wait_ge(k_used, q + 1)
                for j in range(4):
                    last = pe.transpose(pk[0][0:KA, j * P:(j + 1) * P], kbuf[:, j * KA:(j + 1) * KA], ident[:, :])
                last.then_inc(k_mm, 1)
            pe.sem_inc(rq_used, 2)
            with pe.Fori(0, T // 2) as trip_no:
                t = trip_no * 2
                for u in range(2):
                    pe.wait_ge(diag_ready, t + u + 1)
                    pe.wait_ge(rq_used, t + u + 1)
                    pe.matmul(pt[u][:, 0:P], ones[:, :], diag[:, u * P:(u + 1) * P], start=True,
                              stop=True).then_inc(rq_mm, 1)
            pe.wait_ge(rq_used, T + 2)
            pe.sem_inc(a_used, 2)
            pe.wait_ge(fold_ready, 32)
            with pe.Fori(0, H // 2) as trip_no:
                h = trip_no * 2
                for u in range(2):
                    pe.wait_ge(ld_qb[u], 8 * h + 16)
                    pe.wait_ge(a_used, h + u + 1)
                    for r in range(RT):
                        n = P if r < RT - 1 else RL
                        last = pe.matmul(pw[u][0:n, (r // 3) * 512 + (r % 3) * KA:(r // 3) * 512 + (r % 3 + 1) * KA],
                                         wqb[:, u * QR + r * P:u * QR + r * P + n],
                                         fold[:, ds((h + u) * KA, KA)], start=(r % 3 == 0), stop=True,
                                         skip_group_check=True)
                    last.then_inc(a_mm, 1)
            pe.wait_ge(a_used, H + 2)
            for c in range(3):
                for k in range(DK):
                    n = c * DK + k
                    if n >= 2:
                        pe.wait_ge(w_used, n - 1)
                    for r in range(RT):
                        m = P if r < RT - 1 else RL
                        last = pe.matmul(pt[n % 2][:, :], wqa[0:m, r * D + k * P:r * D + (k + 1) * P],
                                         afold[0:m, r * H * KA + c * 512:r * H * KA + (c + 1) * 512],
                                         start=(r == 0), stop=(r == RT - 1))
                    last.then_inc(w_mm, 1)
            pe.wait_ge(k_used, T // 4 + 1)
            for g in range(4):
                if g >= 2:
                    pe.wait_ge(ov_used, g - 1)
                for j in range(4):
                    h = 4 * g + j
                    last = pe.matmul(pk[g % 2][C * j:C * (j + 1), 0:D], wv[:, h * C:(h + 1) * C],
                                     woT[:, h * D:(h + 1) * D], start=True, stop=True)
                last.then_inc(ov_mm, 1)


def attention(nc, hT, weff, caug, cosq, sinq, k_hi, k_lo, ident, cbar):
    st = ExitStack()
    with st:
        def sb(name, cols, dt=F32):
            return st.enter_context(nc.sbuf_tensor(name, [P, cols], dt))

        def pb(name, cols=QC):
            return st.enter_context(nc.psum_tensor(name, [P, cols], F32))

        def sem(name):
            return st.enter_context(nc.semaphore(name))

        q_hi = [sb("q_hi0", S, F32R), sb("q_hi1", S, F32R)]
        q_lo = [sb("q_lo0", S, F32R), sb("q_lo1", S, F32R)]
        wq = [sb("wq0", DK * KA), sb("wq1", DK * KA)]
        prob = [sb(f"prob{n}", 2 * QC) for n in range(4)]
        q_raw = sb("q_raw", QC)
        rot = sb("rot", QC)
        maxes = sb("maxes", 4 * T)
        maxneg = sb("maxneg", T)
        att_t = sb("att_t", QC)
        recip = sb("recip", 8)

        p_s = [pb("p_s0", 2 * QC), pb("p_s1", 2 * QC)]
        p_m = [pb("p_m0"), pb("p_m1")]
        p_o = pb("p_o")
        p_x = pb("p_x")

        wq_ready = sem("wq_ready")
        x_mm = sem("x_mm")
        x_used = sem("x_used")
        q_ready = sem("q_ready")
        max_mm = sem("max_mm")
        max_used = sem("max_used")
        neg_ready = sem("neg_ready")
        s_mm = sem("s_mm")
        p_ready = sem("p_ready")
        o_mm = sem("o_mm")
        o_copied = sem("o_copied")
        zero_rows = sem("zero_rows")
        vec = sem("vec")

        def beside(first, last):
            at = {s: [] for s in range(STEPS)}
            if not first:
                at[0].append(("copy", 1))
                at[1].append(("turn", 1))
            at[16].append(("copy", 0))
            at[17].append(("turn", 0))
            if not last:
                for c in range(4):
                    at[2 + c].append(("project", c))
                    at[28 + c].append(("row", c))
                for n in range(4 * T):
                    at[6 + (n * 22) // (4 * T)].append(("max", n))
            for s, todo in at.items():
                maxima = [what for what in todo if what[0] == "max"]
                copies = [what for what in todo if what[0] == "copy"]
                others = [what for what in todo if what[0] not in ("max", "copy")]
                at[s] = maxima[:2] + copies + maxima[2:] + others
            return at

        ALONE = [("project", c) for c in range(4)] + [("max", n) for n in range(4 * T)] + [("row", c) for c in range(4)]

        def x_use(h, what, last=False):
            kind, c = what
            if h is None:
                return {"project": 0, "row": 4}[kind] + c
            if last:
                return 10 * h + {1: 7, 0: 8}[c]
            return 10 * h + {"turn": {1: 7, 0: 12}.get(c), "project": 8 + c, "row": 13 + c}[kind]

        block = st.enter_context(nc.Block())

        @block.gpsimd
        def _(gp):
            for u in range(2):
                gp.memset(q_lo[u][KA:KS, :].bitcast(F32), 0.0).then_inc(zero_rows, 1)
                gp.wait_ge(zero_rows, u + 1)
            w3 = weff[:, :].rearrange("p (k n) -> p k n", k=DK)
            with gp.Fori(0, H // 2) as trip_no:
                h = trip_no * 2
                for u in range(2):
                    gp.wait_ge(q_ready, 4 * (h + u) + 1)
                    gp.tensor_copy(wq[u][:, :].rearrange("p (k n) -> p k n", k=DK),
                                   w3[:, :, ds((h + u) * KA, KA)]).then_inc(wq_ready, 1)

        @block.scalar
        def _(act):
            act.preload_act_table(ACT.Exp)
            with act.Fori(0, H) as h:
                for s in range(STEPS):
                    n = h * STEPS + s
                    act.wait_ge(s_mm, n + 1)
                    act.wait_ge(o_mm, n + 1)
                    act.activation(prob[s % 4][:, :], p_s[s % 2][:, :], ACT.Exp, scale=SCALE).then_inc(p_ready, 1)

        @block.vector
        def _(v):
            step = Chain(v, vec)

            def project(c, g, u, use):
                tok = slice(c * QC, (c + 1) * QC)
                v.wait_ge(x_mm, use + 1)
                v.wait_ge(q_ready, 4 * g + c + 5)
                step(v.tensor_tensor(q_raw[0:KA, :], p_x[0:KA, :], cosq[0:KA, tok], ALU.mult))
                step(v.tensor_tensor(rot[HALF:ROPE, :], p_x[0:HALF, :], sinq[0:HALF, tok], ALU.mult))
                v.tensor_tensor(rot[0:HALF, :], p_x[HALF:ROPE, :], sinq[HALF:ROPE, tok], ALU.mult).then_inc(x_used, 1)
                v.wait_ge(x_used, use + 2)
                step(v.tensor_tensor(q_raw[0:ROPE, :], q_raw[0:ROPE, :], rot[0:ROPE, :], ALU.add))
                step(v.tensor_copy(q_hi[u][0:KA, tok], q_raw[0:KA, :]))
                v.tensor_tensor(q_lo[u][0:KA, tok], q_raw[0:KA, :], q_hi[u][0:KA, tok].bitcast(F32),
                                ALU.subtract).then_inc(q_ready, 1)

            def maximum(n, g):
                v.wait_ge(max_mm, 64 * g + n + 1)
                v.tensor_reduce(maxes[:, n:n + 1], p_m[n % 2][:, :], AX.X, ALU.max).then_inc(max_used, 1)
                if n == 4 * T - 1:
                    v.wait_ge(max_used, 64 * g + n + 3)
                    v.tensor_reduce(maxneg[:, :], maxes[:, :].rearrange("p (t c) -> p t c", c=4), AX.X, ALU.max,
                                    negate=True).then_inc(neg_ready, 1)
                    v.wait_ge(neg_ready, g + 1)

            def row(c, u, use):
                v.wait_ge(x_mm, use + 1)
                v.tensor_copy(q_hi[u][KA:KS, c * QC:(c + 1) * QC], p_x[KA:KS, :]).then_inc(x_used, 1)

            def copy_out(half, h):
                v.wait_ge(o_mm, STEPS * h + 16 * half + 16 + 4)
                v.tensor_copy(att_t[:, :], p_o[:, :]).then_inc(o_copied, 1)

            def turn(half, h, use):
                v.wait_ge(x_mm, use + 1)
                src = p_x[:, :].rearrange("p (b s n) -> p b s n", b=4, s=2)
                r = recip[:, :].rearrange("p (b s n) -> p b s n", b=4, s=2)
                step(v.reciprocal(r, src[:, :, :, C:C + 1]))
                dst = cbar[:, half * 8 * HC:(half + 1) * 8 * HC].rearrange("p (s b n) -> p b s n", s=2, b=4)
                v.tensor_tensor(dst[:, :, :, ds(h * C, C)], src[:, :, :, 0:C], r.to_broadcast([P, 4, 2, C]),
                                ALU.mult).then_inc(x_used, 1)
                v.wait_ge(x_used, use + 2)

            def head(h, u, first=False, last=False):
                for s, todo in beside(first, last).items():
                    for what in todo:
                        kind, c = what
                        if kind == "project":
                            project(c, h + 1, 1 - u, x_use(h, what))
                        elif kind == "max":
                            maximum(c, h + 1)
                        elif kind == "row":
                            row(c, 1 - u, x_use(h, what))
                        elif kind == "copy":
                            copy_out(c, h - c)
                        else:
                            turn(c, h - c, x_use(h, what, last))

            for kind, c in ALONE:
                if kind == "project":
                    project(c, 0, 0, x_use(None, (kind, c)))
                elif kind == "max":
                    maximum(c, 0)
                else:
                    row(c, 0, x_use(None, (kind, c)))
            head(0, 0, first=True)
            start = step.now
            with v.Fori(0, (H - 2) // 2) as trip_no:
                h = 1 + trip_no * 2
                step.before, step.now = start + (h - 1) * STEPS_V, 0
                head(h, 1)
                head(h + 1, 0)
                assert step.now == 2 * STEPS_V
            step.before, step.now = start + (H - 2) * STEPS_V, 0
            head(H - 1, 1, last=True)
            copy_out(1, H - 1)
            turn(1, H - 1, 10 * (H - 1) + 9)

        @block.tensor
        def _(pe):
            for s, n in ((x_used, 1), (q_ready, 5), (max_used, 2), (p_ready, 2), (o_mm, 4), (o_copied, 1)):
                pe.sem_inc(s, n)

            def project(c, g, u, use):
                pe.wait_ge(wq_ready, g + 1)
                pe.wait_ge(x_used, use + 1)
                for k in range(DK):
                    last = pe.matmul(p_x[0:KA, :], wq[u][:, k * KA:(k + 1) * KA],
                                     hT[:, k * S + c * QC:k * S + (c + 1) * QC], start=(k == 0), stop=(k == DK - 1))
                last.then_inc(x_mm, 1)

            def maximum(n, g, u):
                j, kc = n // 4, n % 4
                if kc == 0:
                    pe.wait_ge(q_ready, 4 * g + j // 4 + 6)
                pe.wait_ge(max_used, 64 * g + n + 1)
                pe.matmul(p_m[n % 2][:, :], q_hi[u][0:KA, j * P:(j + 1) * P], k_hi[0:KA, kc * QC:(kc + 1) * QC],
                          start=True, stop=True).then_inc(max_mm, 1)

            def row(c, g, use):
                pe.wait_ge(neg_ready, g + 1)
                pe.wait_ge(x_used, use + 1)
                for j in range(4):
                    last = pe.matmul(p_x[KA:KS, j * P:(j + 1) * P], maxneg[:, 4 * c + j:4 * c + j + 1], ident[:, :],
                                     start=True, stop=True)
                last.then_inc(x_mm, 1)

            def turn(half, h, use):
                pe.wait_ge(o_copied, 2 * h + half + 2)
                pe.wait_ge(x_used, use + 1)
                for b in range(4):
                    last = pe.transpose(p_x[:, b * P:(b + 1) * P], att_t[:, b * P:(b + 1) * P], ident[:, :])
                last.then_inc(x_mm, 1)

            def scores(s, h, u, rows_from, between):
                half, kt = s // 16, s % 16
                n = STEPS * h + s
                if kt == 0:
                    pe.wait_ge(x_used, rows_from + 2 * half + 3)
                pe.wait_ge(p_ready, n + 1)
                keys = slice(kt * P, (kt + 1) * P)
                for part, (kk, qq) in enumerate(((k_hi, q_hi), (k_hi, q_lo), (k_lo, q_hi))):
                    if part and between:
                        between.pop(0)()
                    for j in range(2):
                        c = 2 * half + j
                        last = pe.matmul(p_s[s % 2][:, j * QC:(j + 1) * QC], kk[0:KS, keys],
                                         qq[u][0:KS, c * QC:(c + 1) * QC], start=(part == 0), stop=(part == 2))
                last.then_inc(s_mm, 1)

            def weigh(s, h):
                half, kt = s // 16, s % 16
                n = STEPS * h + s
                pe.wait_ge(p_ready, n + 3)
                if kt == 0:
                    pe.wait_ge(o_copied, 2 * h + half + 1)
                for j in range(2):
                    last = pe.matmul(p_o[j * CP:(j + 1) * CP, :], caug[:, kt * CP:(kt + 1) * CP],
                                     prob[s % 4][:, j * QC:(j + 1) * QC], start=(kt == 0), stop=(kt == 15))
                last.then_inc(o_mm, 1)

            def head(h, u, rows_from, first=False, last=False):
                for s, todo in beside(first, last).items():
                    maxima = [(lambda c=c: maximum(c, h + 1, 1 - u)) for kind, c in todo if kind == "max"]
                    scores(s, h, u, rows_from, maxima)
                    if s:
                        weigh(s - 1, h)
                    elif not first:
                        weigh(STEPS - 1, h - 1)
                    for m in maxima:
                        m()
                    for what in todo:
                        kind, c = what
                        if kind == "project":
                            project(c, h + 1, 1 - u, x_use(h, what))
                        elif kind == "row":
                            row(c, h + 1, x_use(h, what))
                        elif kind == "turn":
                            turn(c, h - c, x_use(h, what, last))

            pe.wait_ge(zero_rows, 2)
            for kind, c in ALONE:
                if kind == "project":
                    project(c, 0, 0, x_use(None, (kind, c)))
                elif kind == "max":
                    maximum(c, 0, 0)
                else:
                    row(c, 0, x_use(None, (kind, c)))
            head(0, 0, 4, first=True)
            with pe.Fori(0, (H - 2) // 2) as trip_no:
                h = 1 + trip_no * 2
                head(h, 1, 10 * h + 3)
                head(h + 1, 0, 10 * h + 13)
            head(H - 1, 1, 10 * (H - 1) + 3, last=True)
            weigh(STEPS - 1, H - 1)
            turn(1, H - 1, 10 * (H - 1) + 9)


def ffn(nc, a, x, ident, mod, wov, cbar, slots_dram, done_dram, out):
    outer = ExitStack()
    with outer:
        def keep(name, cols, dt=F32):
            return outer.enter_context(nc.sbuf_tensor(name, [P, cols], dt))

        hall = keep("hall", T * D)
        mv = keep("mv2", T * 2)
        rstd = keep("rstd2", T)
        weight = keep("weight", T * 8)
        slot = keep("slot", T * 8, U32)
        slot_out = keep("slot_out", T * 8, U32)
        tile_expert = keep("tile_expert", TILES, I32)
        project_out(nc, x, ident, mod, wov, cbar, mv, rstd)
        route(nc, a, x, ident, mod, mv, rstd, hall, weight, slot, slot_out, tile_expert, slots_dram)
        experts(nc, a, ident, hall, slot, tile_expert, slots_dram, done_dram)
        combine(nc, x, mod, weight, slot_out, done_dram, out)


def project_out(nc, x, ident, mod, wov, cbar, mv, rstd):
    st = ExitStack()
    with st:
        def sb(name, cols, dt=F32):
            return st.enter_context(nc.sbuf_tensor(name, [P, cols], dt))

        def sem(name):
            return st.enter_context(nc.semaphore(name))

        cst = [sb("cst0", HC), sb("cst1", HC)]
        ctb = [sb("ctb0", HC), sb("ctb1", HC)]
        gated = sb("gated", D)
        stats = sb("stats2", T * 6)
        var = sb("var2", T)
        p_t = [st.enter_context(nc.psum_tensor(f"p_t{n}", [P, HC], F32)) for n in range(2)]
        p_y = [st.enter_context(nc.psum_tensor(f"p_y{n}", [P, D], F32)) for n in range(2)]
        c_ready = sem("c_ready")
        ct_mm = sem("ct_mm")
        ct_ready = sem("ct_ready")
        y_mm = sem("y_mm")
        y_used = sem("y_used")
        vec = sem("vec2")
        var_ready = sem("var_ready2")
        stats_ready = sem("stats_ready2")
        root_ready = sem("root_ready2")
        block = st.enter_context(nc.Block())

        @block.gpsimd
        def _(gp):
            with gp.Fori(0, T // 2) as trip_no:
                t = trip_no * 2
                for u in range(2):
                    gp.wait_ge(ct_mm, t + u + 1)
                    gp.tensor_copy(cst[u][:, :], cbar[:, ds((t + u) * HC, HC)]).then_inc(c_ready, 1)

        @block.scalar
        def _(act):
            with act.Fori(0, T // 2) as trip_no:
                t = trip_no * 2
                for u in range(2):
                    act.wait_ge(ct_mm, t + u + 3)
                    act.wait_ge(y_mm, t + u + 1)
                    act.copy(ctb[u][:, :], p_t[u][:, :]).then_inc(ct_ready, 1)
            act.wait_ge(var_ready, 1)
            act.activation(rstd[:, :], var[:, :], ACT.Sqrt).then_inc(root_ready, 1)

        @block.vector
        def _(v):
            step = Chain(v, vec)
            with v.Fori(0, T // 2) as trip_no:
                t = trip_no * 2
                step.enter(t, 1)
                for u in range(2):
                    xt = x[:, ds((t + u) * D, D)]
                    v.wait_ge(y_mm, t + u + 3)
                    v.tensor_tensor(gated[:, :], p_y[u][:, :], mod[:, 2 * D:3 * D], ALU.mult).then_inc(y_used, 1)
                    v.wait_ge(y_used, t + u + 3)
                    step(v.tensor_tensor(xt, xt, gated[:, :], ALU.add))
            step.leave(T, 2)
            with v.Fori(0, T) as t:
                v.bn_stats(stats[:, ds(t * 6, 6)], x[:, ds(t * D, D)]).then_inc(stats_ready, 1)
            v.wait_ge(stats_ready, T)
            for t in range(T):
                last = v.bn_aggr(mv[:, t * 2:(t + 1) * 2], stats[:, t * 6:(t + 1) * 6])
            step(last)
            v.tensor_scalar(var[:, :], mv[:, :].rearrange("p (t n) -> p t n", n=2)[:, :, 1], 1e-5, None,
                            ALU.add).then_inc(var_ready, 1)
            v.wait_ge(root_ready, 1)
            step(v.reciprocal(rstd[:, :], rstd[:, :]))

        @block.tensor
        def _(pe):
            for s in (ct_mm, ct_ready, y_mm, y_used):
                pe.sem_inc(s, 2)
            with pe.Fori(0, T // 2) as trip_no:
                t = trip_no * 2
                for u in range(2):
                    pe.wait_ge(c_ready, t + u + 1)
                    pe.wait_ge(ct_ready, t + u + 1)
                    for g in range(4):
                        last = pe.transpose(p_t[u][:, g * P:(g + 1) * P], cst[u][:, g * P:(g + 1) * P], ident[:, :])
                    last.then_inc(ct_mm, 1)
                    pe.wait_ge(ct_ready, t + u + 3)
                    pe.wait_ge(y_used, t + u + 1)
                    for g in range(4):
                        last = pe.matmul(p_y[u][:, :], ctb[u][:, g * P:(g + 1) * P], wov[:, g * D:(g + 1) * D],
                                         start=(g == 0), stop=(g == 3))
                    last.then_inc(y_mm, 1)


def route(nc, a, x, ident, mod, mv, rstd, hall, weight, slot, slot_out, tile_expert, slots_dram):
    st = ExitStack()
    with st:
        def sb(name, cols, dt=F32):
            return st.enter_context(nc.sbuf_tensor(name, [P, cols], dt))

        def sem(name):
            return st.enter_context(nc.semaphore(name))

        PADG = 16
        PADE = E + 8
        gate = sb("gate", DK * E)
        lower = sb("lower", P)
        ones = sb("ones2", P)
        thresholds = sb("thresholds", T)
        numbers = sb("numbers", SLOT_TILES)
        hb = [sb("hb0", D), sb("hb1", D)]
        h2T = [sb("h2T0", D), sb("h2T1", D)]
        sc = sb("sc", T * E)
        tmp = sb("tmp", T * E)
        gpad = sb("gpad", T * PADG)
        gtop = sb("gtop", T * 8)
        gkey = sb("gkey", T * 8)
        grep = sb("grep", T * PADG)
        gmask = sb("gmask", T * GROUPS)
        gpen = sb("gpen", T * GROUPS)
        epad = sb("epad", T * PADE)
        etop = sb("etop", T * 8)
        ekey = sb("ekey", T * 8)
        erep = sb("erep", T * PADE)
        chosen = sb("chosen", T * E)
        wn = sb("wn", T * E)
        wsum = sb("wsum", T)
        before = sb("before", (T + 1) * E)
        cmp = sb("cmp", E * T)
        ntiles = sb("ntiles", E)
        scan = [sb("scan0", E), sb("scan1", E)]
        first = sb("first", E)
        val = sb("val", T * E)
        vtop = sb("vtop", T * 8)
        texp = sb("texp", SLOT_TILES * E)
        tsum = sb("tsum", TILES)
        p_t = [st.enter_context(nc.psum_tensor(f"p_tn{n}", [P, D], F32)) for n in range(2)]
        p_l = [st.enter_context(nc.psum_tensor(f"p_l{n}", [P, E], F32)) for n in range(2)]
        p_pos = st.enter_context(nc.psum_tensor("p_pos", [P, T * E], F32))
        p_cnt = st.enter_context(nc.psum_tensor("p_cnt", [P, E], F32))
        ld = sem("ld3")
        h_ready = sem("h_ready3")
        t_mm = sem("t_mm3")
        t_ready = sem("t_ready3")
        l_mm = sem("l_mm3")
        l_used = sem("l_used3")
        kept = sem("kept3")
        exped = sem("exped3")
        pads = sem("pads3")
        pool = sem("pool3")
        chosen_ready = sem("chosen_ready3")
        cum_ready = sem("cum_ready3")
        pos_mm = sem("pos_mm3")
        vec = sem("vec3")
        stored = sem("stored3")
        block = st.enter_context(nc.Block())

        @block.sync
        def _(sp):
            for k in range(DK):
                sp.dma_start(gate[:, k * E:(k + 1) * E], a["gate"][k * P:(k + 1) * P, :]).then_inc(ld, 16)
            sp.dma_start(lower[:, :], a["lower"]).then_inc(ld, 16)
            sp.dma_start(thresholds[:, :], a["thresholds"]).then_inc(ld, 16)
            sp.dma_start(numbers[:, :], a["numbers"]).then_inc(ld, 16)
            sp.wait_ge(kept, T + 2)
            sp.dma_start(slots_dram[SLOT_TILES * P:SLOT_TILES * P + S, :].rearrange("(t p) d -> p t d", p=P),
                         hall[:, :].rearrange("p (t d) -> p t d", t=T)).then_inc(stored, 16)
            sp.wait_ge(stored, 16)

        @block.gpsimd
        def _(gp):
            step = Chain(gp, pool)
            step(gp.memset(ones[:, :], 1.0))
            step(gp.memset(gpad[:, :].rearrange("p (t n) -> p t n", t=T)[:, :, GROUPS:8], -1.0))
            step(gp.memset(gpad[:, :].rearrange("p (t n) -> p t n", t=T)[:, :, 8:PADG], 2.0))
            step(gp.memset(gkey[:, :], 2.0))
            step(gp.memset(ekey[:, :], 2.0))
            step(gp.memset(tsum[:, 0:T], float(E)))
            step(gp.memset(tsum[:, T:2 * T], float(E + 1)))
            step(gp.memset(before[:, 0:E], 0.0))
            gp.memset(epad[:, :].rearrange("p (t n) -> p t n", t=T)[:, :, E:PADE], 2.0).then_inc(pads, 1)
            gp.wait_ge(pads, 1)
            with gp.Fori(0, T // 2) as trip_no:
                t = trip_no * 2
                for u in range(2):
                    gp.wait_ge(h_ready, t + u + 1)
                    gp.tensor_copy(hall[:, ds((t + u) * D, D)], hb[u][:, :]).then_inc(kept, 1)

        @block.scalar
        def _(act):
            with act.Fori(0, T // 2) as trip_no:
                t = trip_no * 2
                for u in range(2):
                    act.wait_ge(t_mm, t + u + 3)
                    act.wait_ge(l_mm, t + u + 1)
                    act.copy(h2T[u][:, :], p_t[u][:, :]).then_inc(t_ready, 1)
                    act.wait_ge(l_mm, t + u + 3)
                    act.activation(sc[:, ds((t + u) * E, E)], p_l[u][:, :], ACT.Exp, scale=-1.0).then_inc(l_used, 1)

        @block.vector
        def _(v):
            step = Chain(v, vec)

            def t3(tensor, n=E):
                return tensor[:, :].rearrange("p (t n) -> p t n", n=n)

            with v.Fori(0, T // 2) as trip_no:
                t = trip_no * 2
                step.enter(t, 2)
                for u in range(2):
                    v.wait_ge(t_mm, t + u + 1)
                    v.wait_ge(kept, t + u + 1)
                    step(v.tensor_scalar(hb[u][:, :], x[:, ds((t + u) * D, D)], mv[:, ds((t + u) * 2, 1)],
                                         rstd[:, ds(t + u, 1)], ALU.subtract, ALU.mult))
                    step(v.tensor_tensor(hb[u][:, :], hb[u][:, :], mod[:, 4 * D:5 * D], ALU.mult))
                    v.tensor_tensor(hb[u][:, :], hb[u][:, :], mod[:, 3 * D:4 * D], ALU.add).then_inc(h_ready, 1)
            step.leave(T, 2)
            v.wait_ge(l_used, T + 2)
            v.wait_ge(pads, 1)
            v.wait_ge(ld, 16 * (DK + 3))
            step(v.tensor_scalar(sc[:, :], sc[:, :], 1.0, None, ALU.add))
            step(v.reciprocal(sc[:, :], sc[:, :]))
            step(v.tensor_reduce(t3(gpad, PADG)[:, :, 0:GROUPS],
                                 sc[:, :].rearrange("p (t g n) -> p t g n", t=T, g=GROUPS), AX.X, ALU.max))
            for t in range(T):
                last = v.max(gtop[:, t * 8:(t + 1) * 8], gpad[:, t * PADG:t * PADG + 8])
            step(last)
            step(v.tensor_copy(t3(gkey, 8)[:, :, 0:2], t3(gtop, 8)[:, :, 0:2]))
            for t in range(T):
                last = v.match_replace(grep[:, t * PADG:(t + 1) * PADG], gkey[:, t * 8:(t + 1) * 8],
                                       gpad[:, t * PADG:(t + 1) * PADG], -5.0)
            step(last)
            step(v.tensor_scalar(t3(gmask, GROUPS), t3(grep, PADG)[:, :, 0:GROUPS], -5.0, None, ALU.is_equal))
            step(v.tensor_scalar(gpen[:, :], gmask[:, :], -1.0, None, ALU.add))
            by_group = lambda z: z.rearrange("p (t g n) -> p t g n", t=T, g=GROUPS)
            wide = lambda z: z[:, :].rearrange("p (t g n) -> p t g n", t=T, n=1).to_broadcast([P, T, GROUPS, EPG])
            step(v.tensor_tensor(by_group(tmp[:, :]), by_group(sc[:, :]), wide(gmask), ALU.mult))
            step(v.tensor_tensor(by_group(tmp[:, :]), by_group(tmp[:, :]), wide(gpen), ALU.add))
            step(v.tensor_copy(t3(epad, PADE)[:, :, 0:E], t3(tmp)))
            for t in range(T):
                last = v.max(etop[:, t * 8:(t + 1) * 8], epad[:, t * PADE:t * PADE + E])
            step(last)
            step(v.tensor_copy(t3(ekey, 8)[:, :, 0:TOPK], t3(etop, 8)[:, :, 0:TOPK]))
            for t in range(T):
                last = v.match_replace(erep[:, t * PADE:(t + 1) * PADE], ekey[:, t * 8:(t + 1) * 8],
                                       epad[:, t * PADE:(t + 1) * PADE], -5.0)
            step(last)
            v.tensor_scalar(t3(chosen), t3(erep, PADE)[:, :, 0:E], -5.0, None, ALU.is_equal).then_inc(chosen_ready, 1)
            v.wait_ge(chosen_ready, 1)
            with v.Fori(0, T) as t:
                step.enter(t, 1)
                step(v.tensor_tensor(before[:, ds((t + 1) * E, E)], before[:, ds(t * E, E)], chosen[:, ds(t * E, E)],
                                     ALU.add))
            step.leave(T)
            v.tensor_copy(first[:, :], before[:, T * E:(T + 1) * E]).then_inc(cum_ready, 1)
            step(v.tensor_tensor(wn[:, :], sc[:, :], chosen[:, :], ALU.mult))
            step(v.tensor_reduce(wsum[:, :], t3(wn), AX.X, ALU.add))
            step(v.reciprocal(wsum[:, :], wsum[:, :]))
            step(v.tensor_tensor(t3(wn), t3(wn), wsum[:, :].rearrange("p (t n) -> p t n", n=1).to_broadcast([P, T, E]),
                                 ALU.mult))
            v.wait_ge(pos_mm, 2)
            step(v.tensor_tensor(cmp[:, :].rearrange("p (e n) -> p e n", n=T),
                                 p_cnt[:, :].rearrange("p (e n) -> p e n", n=1).to_broadcast([P, E, T]),
                                 thresholds[:, :].rearrange("p (e n) -> p e n", e=1).to_broadcast([P, E, T]),
                                 ALU.is_gt))
            step(v.tensor_reduce(ntiles[:, :], cmp[:, :].rearrange("p (e n) -> p e n", n=T), AX.X, ALU.add))
            step(v.tensor_copy(scan[0][:, :], ntiles[:, :]))
            src = 0
            for d in (1, 2, 4, 8, 16):
                step(v.tensor_copy(scan[1 - src][:, 0:d], scan[src][:, 0:d]))
                step(v.tensor_tensor(scan[1 - src][:, d:E], scan[src][:, d:E], scan[src][:, 0:E - d], ALU.add))
                src = 1 - src
            ends = scan[src]
            step(v.tensor_tensor(first[:, :], ends[:, :], ntiles[:, :], ALU.subtract))
            step(v.tensor_scalar(first[:, :], first[:, :], float(P), 1.0, ALU.mult, ALU.add))
            step(v.tensor_tensor(t3(val), p_pos[:, :].rearrange("p (t n) -> p t n", n=E),
                                 first[:, :].rearrange("p (t n) -> p t n", t=1).to_broadcast([P, T, E]), ALU.add))
            step(v.tensor_tensor(val[:, :], val[:, :], chosen[:, :], ALU.mult))
            for t in range(T):
                last = v.max(vtop[:, t * 8:(t + 1) * 8], val[:, t * E:(t + 1) * E])
            step(last)
            step(v.tensor_scalar(t3(slot, 8)[:, :, 0:TOPK], t3(vtop, 8)[:, :, 0:TOPK], -1.0, None, ALU.add))
            step(v.tensor_scalar(t3(slot_out, 8)[:, :, 0:TOPK], t3(vtop, 8)[:, :, 0:TOPK], float(2 * S - 1), None,
                                 ALU.add))
            for j in range(TOPK):
                step(v.tensor_tensor(t3(tmp), t3(val), t3(vtop, 8)[:, :, j:j + 1].to_broadcast([P, T, E]),
                                     ALU.is_equal))
                step(v.tensor_tensor(tmp[:, :], tmp[:, :], wn[:, :], ALU.mult))
                step(v.tensor_reduce(t3(weight, 8)[:, :, j], t3(tmp), AX.X, ALU.add))
            te = texp[0:1, :].rearrange("p (t n) -> p t n", n=E)
            step(v.tensor_tensor(te, ends[0:1, :].rearrange("p (t n) -> p t n", t=1).to_broadcast([1, SLOT_TILES, E]),
                                 numbers[0:1, :].rearrange("p (t n) -> p t n", n=1).to_broadcast([1, SLOT_TILES, E]),
                                 ALU.is_le))
            step(v.tensor_reduce(tsum[0:1, 2 * T:TILES], te, AX.X, ALU.add))
            step(v.tensor_scalar(tsum[0:1, 2 * T:TILES], tsum[0:1, 2 * T:TILES], float(E - 1), None, ALU.min))
            step(v.tensor_copy(tile_expert[0:1, :], tsum[0:1, :]))

        @block.tensor
        def _(pe):
            for s in (t_mm, t_ready, l_mm, l_used, kept):
                pe.sem_inc(s, 2)
            pe.wait_ge(ld, 16 * (DK + 3))
            with pe.Fori(0, T // 2) as trip_no:
                t = trip_no * 2
                for u in range(2):
                    pe.wait_ge(h_ready, t + u + 1)
                    pe.wait_ge(t_ready, t + u + 1)
                    for k in range(DK):
                        last = pe.transpose(p_t[u][:, k * P:(k + 1) * P], hb[u][:, k * P:(k + 1) * P], ident[:, :])
                    last.then_inc(t_mm, 1)
                    pe.wait_ge(t_ready, t + u + 3)
                    pe.wait_ge(l_used, t + u + 1)
                    for k in range(DK):
                        last = pe.matmul(p_l[u][:, :], h2T[u][:, k * P:(k + 1) * P], gate[:, k * E:(k + 1) * E],
                                         start=(k == 0), stop=(k == DK - 1))
                    last.then_inc(l_mm, 1)
            pe.wait_ge(pads, 1)
            pe.wait_ge(chosen_ready, 1)
            pe.matmul(p_pos[:, :], lower[:, :], chosen[:, :], start=True, stop=False)
            pe.wait_ge(cum_ready, 1)
            pe.matmul(p_pos[:, :], ones[:, :], before[:, 0:T * E], start=False, stop=True).then_inc(pos_mm, 1)
            pe.matmul(p_cnt[:, :], ones[:, :], before[:, T * E:(T + 1) * E], start=True, stop=True).then_inc(pos_mm, 1)


def experts(nc, a, ident, hall, slot, tile_expert, slots_dram, done_dram):
    st = ExitStack()
    with st:
        def sb(name, cols, dt=F32, parts=P):
            return st.enter_context(nc.sbuf_tensor(name, [parts, cols], dt))

        def pb(name):
            return st.enter_context(nc.psum_tensor(name, [P, 512], F32))

        def sem(name):
            return st.enter_context(nc.semaphore(name))

        U = 4
        rows = [sb(f"rows{n}", D) for n in range(U)]
        w_in = [sb(f"w_in{n}", DK * 2 * M) for n in range(U)]
        w_out = [sb(f"w_out{n}", 2 * D, parts=MH) for n in range(U)]
        rT = [sb("rT0", D), sb("rT1", D)]
        ex = [sb("ex0", M), sb("ex1", M)]
        hid = [sb("hid0", M), sb("hid1", M)]
        hidT = [sb("hidT0", 2 * P, parts=MH), sb("hidT1", 2 * P, parts=MH)]
        y = [sb(f"y{n}", D) for n in range(U)]
        stage = [sb("stage0", D), sb("stage1", D)]
        stage_slot = [sb("stage_slot0", 8, U32), sb("stage_slot1", 8, U32)]
        p_r = pb("p_r")
        p_g = [pb(f"p_g{n}") for n in range(U)]
        p_h = pb("p_h")
        p_y = [pb("p_d0"), pb("p_d1")]
        staged = sem("staged")
        issued = sem("issued")
        scattered = [sem("scattered0"), sem("scattered1")]
        row_ld = [sem(f"row_ld{n}") for n in range(U)]
        w_ld = [sem(f"w_ld{n}") for n in range(U)]
        r_mm = sem("r_mm")
        r_used = sem("r_used")
        g_mm = sem("g_mm")
        silued = sem("silued")
        hid_ready = sem("hid_ready")
        h_mm = sem("h_mm")
        h_used = sem("h_used")
        y_mm = sem("y_mm4")
        y_ready = sem("y_ready")
        y_out = [sem(f"y_out{n}") for n in range(U)]
        block = st.enter_context(nc.Block())
        CREDIT = {r_mm: U, r_used: 1, g_mm: 2, silued: 0, hid_ready: U, h_mm: 2, h_used: 1, y_mm: U, y_ready: 2}

        w_in_dram = a["w_in"]
        w_out_dram = a["w_out"]

        @block.gpsimd
        def _(gp):
            gp.sem_inc(staged, 1)
            def scatter(t, u):
                gp.tensor_copy(stage[u][:, :], hall[:, ds((t + u) * D, D)])
                gp.tensor_copy(stage_slot[u][:, 0:TOPK], slot[:, ds((t + u) * 8, TOPK)]).then_inc(staged, 1)
                gp.wait_ge(staged, t + u + 2)
                gp.sem_inc(issued, 1)
                for j in range(TOPK):
                    gp.indirect_dma_start(
                        out=slots_dram[0:SLOT_TILES * P, :],
                        out_offset=bass.IndirectOffsetOnAxis(ap=stage_slot[u][:, j:j + 1], axis=0),
                        in_=stage[u][:, :], in_offset=None).then_inc(scattered[u], 16)

            for u in range(2):
                scatter(0, u)
            with gp.Fori(0, T // 2 - 1) as trip_no:
                t = 2 + trip_no * 2
                for u in range(2):
                    gp.wait_ge(scattered[u], 8 * TOPK * t)
                    scatter(t, u)

        @block.sync
        def _(sp):
            for s, n in CREDIT.items():
                if n:
                    sp.sem_inc(s, n)

            def load(i, u, row):
                e = sp.value_load(tile_expert[0:1, ds(i + u, 1)], min_val=0, max_val=E + 1)
                sp.wait_ge(r_mm, i + u + 1)
                sp.dma_start(rows[u][:, :], slots_dram[ds(row, P), :]).then_inc(row_ld[u], 16)
                sp.wait_ge(y_mm, i + u + 1)
                sp.dma_start(w_in[u][:, :].rearrange("p (k n) -> p k n", k=DK),
                             w_in_dram[ds(e, 1), :, :].rearrange("a (k p) n -> p (a k) n", p=P)).then_inc(w_ld[u], 16)
                sp.dma_start(w_out[u][:, :].rearrange("p (k n) -> p k n", k=2),
                             w_out_dram[ds(e, 1), :, :].rearrange("a (k p) n -> p (a k) n", p=MH)).then_inc(w_ld[u], 16)

            def store(n, u):
                sp.wait_ge(y_ready, n + 3)
                sp.dma_start(done_dram[ds(n * P, P), :], y[u][:, :]).then_inc(y_out[u], 16)

            for u in range(U):
                load(0, u, (u + SLOT_TILES) * P)
            with sp.Fori(1, T // U) as trip_no:
                i = trip_no * U
                for u in range(U):
                    load(i, u, (i + u + SLOT_TILES) * P)
                    store(i + u - U, u)
            with sp.Fori(0, T // U) as trip_no:
                i = T + trip_no * U
                for u in range(U):
                    load(i, u, (i + u + SLOT_TILES - T) * P)
                    store(i + u - U, u)
            for s in scattered:
                sp.wait_ge(s, 16 * TOPK * T // 2)
            with sp.Fori(0, (TILES - 2 * T) // U) as trip_no:
                i = 2 * T + trip_no * U
                for u in range(U):
                    load(i, u, (i + u - 2 * T) * P)
                    store(i + u - U, u)
            for u in range(U):
                store(TILES - U + u, u)
            for s in y_out:
                sp.wait_ge(s, 16 * TILES // U + 16)

        @block.scalar
        def _(act):
            def copy_rows(n, u):
                act.wait_ge(r_mm, n + U + 1)
                act.wait_ge(g_mm, n + 1)
                act.copy(rT[u % 2][:, :], p_r[:, 0:D]).then_inc(r_used, 1)

            def silu_gate(n, u):
                act.wait_ge(g_mm, n + 3)
                act.wait_ge(hid_ready, n + U - 1)
                act.activation(ex[u % 2][:, :], p_g[u % U][:, 0:M], ACT.Silu).then_inc(silued, 1)

            def copy_hidden(n, u):
                act.wait_ge(h_mm, n + 3)
                act.wait_ge(y_mm, n + U - 1)
                act.copy(hidT[u % 2][:, :], p_h[0:MH, 0:2 * P]).then_inc(h_used, 1)

            def trip(i, u, ahead=2):
                n = i + u
                copy_hidden(n, u)
                if ahead == 2:
                    copy_rows(n + 2, u + 2)
                    silu_gate(n + 2, u + 2)

            act.preload_act_table(ACT.Silu)
            for n in range(2):
                copy_rows(n, n)
                silu_gate(n, n)
            with act.Fori(0, (TILES - U) // U) as trip_no:
                i = trip_no * U
                for u in range(U):
                    trip(i, u)
            for u in range(U):
                trip(TILES - U, u, 2 if u < U - 2 else 0)

        @block.vector
        def _(v):
            def silu(n, u):
                up = p_g[u % U][:, M:2 * M]
                v.wait_ge(silued, n + 1)
                v.wait_ge(h_mm, n + 1)
                v.tensor_tensor(hid[u % 2][:, :], ex[u % 2][:, :], up, ALU.mult).then_inc(hid_ready, 1)

            def copy_y(n, u):
                v.wait_ge(y_mm, n + U + 1)
                v.wait_ge(y_out[u], (n - u) * (16 // U) + 16)
                v.tensor_copy(y[u][:, :], p_y[u % 2][:, 0:D]).then_inc(y_ready, 1)

            for s in y_out:
                v.sem_inc(s, 16)
            for n in range(2):
                silu(n, n)
            with v.Fori(0, (TILES - U) // U) as trip_no:
                i = trip_no * U
                for u in range(U):
                    silu(i + u + 2, u + 2)
                    copy_y(i + u, u)
            for u in range(U):
                if u < U - 2:
                    silu(TILES - U + u + 2, u + 2)
                copy_y(TILES - U + u, u)

        @block.tensor
        def _(pe):
            def turn_rows(n, u, ring):
                pe.wait_ge(row_ld[u % U], ring)
                pe.wait_ge(r_used, n + 1)
                for k in range(DK):
                    last = pe.transpose(p_r[:, k * P:(k + 1) * P], rows[u % U][:, k * P:(k + 1) * P], ident[:, :])
                last.then_inc(r_mm, 1)

            def gate_up(n, u, ring):
                pe.wait_ge(r_used, n + 2)
                pe.wait_ge(w_ld[u % U], 2 * ring)
                pe.wait_ge(hid_ready, n + 1)
                for k in range(DK):
                    last = pe.matmul(p_g[u % U][:, 0:2 * M], rT[u % 2][:, k * P:(k + 1) * P],
                                     w_in[u % U][:, k * 2 * M:(k + 1) * 2 * M], start=(k == 0), stop=(k == DK - 1))
                last.then_inc(g_mm, 1)

            def turn_hidden(n, u):
                pe.wait_ge(hid_ready, n + U + 1)
                pe.wait_ge(h_used, n + 1)
                for k in range(2):
                    last = pe.transpose(p_h[0:MH, k * P:(k + 1) * P], hid[u % 2][:, k * MH:(k + 1) * MH], ident[:, :])
                last.then_inc(h_mm, 1)

            def down(n, u):
                pe.wait_ge(h_used, n + 2)
                pe.wait_ge(y_ready, n + 1)
                for k in range(2):
                    last = pe.matmul(p_y[u % 2][:, 0:D], hidT[u % 2][:, k * P:(k + 1) * P],
                                     w_out[u % U][:, k * D:(k + 1) * D], start=(k == 0), stop=(k == 1))
                last.then_inc(y_mm, 1)

            def trip(i, u, ring, ahead=2):
                n = i + u
                turn_hidden(n, u)
                if ahead == 2:
                    late = ring + (16 if u + 2 >= U else 0)
                    turn_rows(n + 2, u + 2, late)
                    gate_up(n + 2, u + 2, late)
                down(n, u)

            for n in range(2):
                turn_rows(n, n, 16)
                gate_up(n, n, 16)
            with pe.Fori(0, (TILES - U) // U) as trip_no:
                i = trip_no * U
                for u in range(U):
                    trip(i, u, i * (16 // U) + 16)
            for u in range(U):
                trip(TILES - U, u, 16 * (TILES // U), 2 if u < U - 2 else 0)


def combine(nc, x, mod, weight, slot_out, done_dram, out):
    st = ExitStack()
    with st:
        def sb(name, cols, dt=F32):
            return st.enter_context(nc.sbuf_tensor(name, [P, cols], dt))

        def sem(name):
            return st.enter_context(nc.semaphore(name))

        PARTS = TOPK + 2
        got = [sb("got0", PARTS * D), sb("got1", PARTS * D)]
        slot_now = [sb("slot_now0", 8, U32), sb("slot_now1", 8, U32)]
        acc = [sb("acc0", D), sb("acc1", D)]
        slot_ready = sem("slot_ready")
        issued = sem("issued5")
        gathered = [sem("gathered0"), sem("gathered1")]
        shared = [sem("shared0"), sem("shared1")]
        used = sem("used5")
        done = sem("done5")
        written = [sem("written0"), sem("written1")]
        vec = sem("vec5")
        block = st.enter_context(nc.Block())

        @block.gpsimd
        def _(gp):
            with gp.Fori(0, T // 2) as trip_no:
                t = trip_no * 2
                for u in range(2):
                    gp.wait_ge(used, t + u + 1)
                    gp.tensor_copy(slot_now[u][:, 0:TOPK], slot_out[:, ds((t + u) * 8, TOPK)]).then_inc(slot_ready, 1)
                    gp.wait_ge(slot_ready, t + u + 1)
                    gp.sem_inc(issued, 1)
                    for j in range(TOPK):
                        gp.indirect_dma_start(
                            out=got[u][:, j * D:(j + 1) * D], out_offset=None,
                            in_=done_dram,
                            in_offset=bass.IndirectOffsetOnAxis(ap=slot_now[u][:, j:j + 1], axis=0)
                        ).then_inc(gathered[u], 16)

        @block.sync
        def _(sp):
            sp.sem_inc(used, 2)
            for s in written:
                sp.sem_inc(s, 16)
            with sp.Fori(0, T // 2) as trip_no:
                t = trip_no * 2
                for u in range(2):
                    sp.wait_ge(used, t + u + 1)
                    for part in range(2):
                        sp.dma_start(got[u][:, (TOPK + part) * D:(TOPK + part + 1) * D],
                                     done_dram[ds((t + u + T * part) * P, P), :]).then_inc(shared[u], 16)

        @block.scalar
        def _(act):
            with act.Fori(0, T // 2) as trip_no:
                t = trip_no * 2
                for u in range(2):
                    act.wait_ge(done, t + u + 1)
                    act.dma_start(out[ds((t + u) * P, P), :], acc[u][:, :]).then_inc(written[u], 16)
            for s in written:
                act.wait_ge(s, 16 * T // 2 + 16)

        @block.vector
        def _(v):
            step = Chain(v, vec)
            with v.Fori(0, T // 2) as trip_no:
                t = trip_no * 2
                step.enter(t, TOPK + 1)
                for u in range(2):
                    g = got[u]
                    v.wait_ge(shared[u], 16 * t + 32)
                    v.wait_ge(gathered[u], 16 * TOPK // 2 * t + 16 * TOPK)
                    v.wait_ge(written[u], 8 * t + 16)
                    step(v.tensor_tensor(acc[u][:, :], g[:, TOPK * D:(TOPK + 1) * D], g[:, (TOPK + 1) * D:PARTS * D],
                                         ALU.add))
                    for j in range(TOPK):
                        ins = v.scalar_tensor_tensor(out=acc[u][:, :], in0=g[:, j * D:(j + 1) * D],
                                                     scalar=weight[:, ds((t + u) * 8 + j, 1)], in1=acc[u][:, :],
                                                     op0=ALU.mult, op1=ALU.add)
                        if j < TOPK - 1:
                            step(ins)
                        else:
                            ins.then_inc(used, 1)
                            v.wait_ge(used, t + u + 3)
                    step(v.tensor_tensor(acc[u][:, :], acc[u][:, :], mod[:, 5 * D:6 * D], ALU.mult))
                    v.tensor_tensor(acc[u][:, :], acc[u][:, :], x[:, ds((t + u) * D, D)], ALU.add).then_inc(done, 1)
            step.leave(T, 2)


def kernel(**inputs):
    import concourse.bacc as bacc
    from concourse.bass_utils import run_bass_kernel_spmd

    given = {n: np.asarray(v) for n, v in inputs.items()}
    f32 = np.float32
    pairs = np.concatenate([np.arange(0, ROPE, 2), np.arange(1, ROPE, 2)])
    qb = given["L0_attn_q_b_w"].reshape(H, QK, QR)
    qb = np.concatenate([qb[:, QK - ROPE:][:, pairs], qb[:, :QK - ROPE]], axis=1)
    kva = given["L0_attn_kv_a_w"]
    kva = np.concatenate([kva[C:][pairs], kva[:C]], axis=0)
    kvb = given["L0_attn_kv_b_w"].reshape(H, QK - ROPE + V, C)
    lnq = np.zeros((RT * P,), f32)
    lnq[:QR] = given["L0_attn_q_a_ln"]
    inv = (f32(1.0) / (f32(128000.0) ** (np.arange(0, ROPE, 2, dtype=f32) / f32(ROPE)))).astype(f32)
    angle = (inv[:, None] * np.arange(S, dtype=f32)[None, :]).astype(f32).astype(np.float64)
    cos, sin = np.cos(angle).astype(f32), np.sin(angle).astype(f32)
    sw_gate, sw_up, sw_down = (given[f"L0_ffn_sw_{n}"] for n in ("gate", "up", "down"))
    w_in = np.concatenate([given["L0_ffn_w_gate"], given["L0_ffn_w_up"]], axis=2)
    shared_in = np.stack([np.concatenate([sw_gate[:, i * M:(i + 1) * M], sw_up[:, i * M:(i + 1) * M]], axis=1)
                          for i in range(2)])
    arrays = {
        "x": given["L0_attn_x"].reshape(S, D),
        "c": given["L0_c"].reshape(DK, P).T,
        "wmod": given["L0_wmod"],
        "wqaT": given["L0_attn_q_a_w"].T,
        "wqa": given["L0_attn_q_a_w"],
        "lnq": lnq.reshape(RT, P).T,
        "wqb": qb.transpose(1, 0, 2).reshape(P, H * QR),
        "wkvT": kva.T,
        "lnkv": np.broadcast_to(given["L0_attn_kv_a_ln"], (P, C)),
        "wk": kvb[:, :QK - ROPE].transpose(1, 0, 2).reshape(QK - ROPE, H * C),
        "wv": kvb[:, QK - ROPE:].transpose(1, 0, 2).reshape(V, H * C),
        "woT": given["L0_attn_o_w"].T.reshape(H, V, D).transpose(1, 0, 2).reshape(V, H * D),
        "cos": np.concatenate([cos, cos]),
        "sin": np.concatenate([sin, -sin]),
        "gate": given["L0_ffn_gate_w"],
        "w_in": np.concatenate([w_in, shared_in]),
        "w_out": np.concatenate([given["L0_ffn_w_down"], sw_down.reshape(2, M, D)]),
        "lower": np.triu(np.ones((P, P), f32), 1),
        "thresholds": np.broadcast_to(np.arange(T, dtype=f32) * P, (P, T)),
        "numbers": np.broadcast_to(np.arange(SLOT_TILES, dtype=f32), (P, SLOT_TILES)),
    }
    nc = bacc.Bacc("TRN2", target_bir_lowering=False, num_devices=1)
    feed, aps = {}, {}
    for name, array in arrays.items():
        array = np.ascontiguousarray(array)
        feed[f"in_{name}"] = array
        aps[name] = nc.dram_tensor(f"in_{name}", array.shape, mybir.dt.from_np(array.dtype), kind="ExternalInput").ap()
    out = nc.dram_tensor("out", [S, D], F32, kind="ExternalOutput").ap()
    program(nc, aps, out)
    result = run_bass_kernel_spmd(nc, [feed], core_ids=[0])
    return result.results[0]["out"].reshape(1, S, D)
```

```python
from contextlib import ExitStack

import numpy as np

import concourse.bass as bass
from concourse import mybir

F32 = mybir.dt.float32
F32R = mybir.dt.float32r
F16 = mybir.dt.float16
I32 = mybir.dt.int32
U32 = mybir.dt.uint32
ALU = mybir.AluOpType
ACT = mybir.ActivationFunctionType
AX = mybir.AxisListType
ds = bass.ds

P = 128
S = 2048
D = 256
T = S // P
DK = D // P
H = 16
ROPE = 64
HALF = ROPE // 2
C = 32
QK = 128
V = 128
KA = ROPE + C
KS = KA + 1
QR = 682
RT = -(-QR // P)
RL = QR - (RT - 1) * P
HC = H * C
QC = 512
E = 32
TOPK = 6
GROUPS = 4
EPG = E // GROUPS
M = 176
MH = M // 2
WIN = DK * 2 * M
WOUT = 2 * D
SLOT_TILES = S * TOPK // P + E
TILES = SLOT_TILES + 2 * T
STEPS_V = 4 * 4 + 2
SCALE = float(1.0 / np.sqrt(np.float32(QK)))
STEPS = 32
P_SCALE = 2.0 ** 14
C_SCALE = 16.0
CP = 64


class Chain:

    def __init__(self, engine, semaphore):
        self.engine, self.semaphore, self.before, self.now = engine, semaphore, 0, 0

    def __call__(self, instruction):
        instruction.then_inc(self.semaphore, 1)
        self.now += 1
        self.engine.wait_ge(self.semaphore, self.before + self.now)

    def enter(self, i, each):
        self.start, self.each = self.before + self.now, each
        self.before, self.now = self.start + i * each, 0

    def leave(self, end, unit=1):
        assert self.now == self.each * unit, (self.now, self.each, unit)
        self.before, self.now = self.start + end * self.each, 0


def program(nc, a, out):
    top = ExitStack()
    with top:
        def sb(stack, name, cols, dt=F32, parts=P):
            return stack.enter_context(nc.sbuf_tensor(name, [parts, cols], dt))

        x = sb(top, "x", T * D)
        ident = sb(top, "ident", P)
        ones = sb(top, "ones", P)
        mod = sb(top, "mod", 6 * D)
        wov = sb(top, "wov", 4 * D)
        cbar = sb(top, "cbar", T * HC)
        slots_dram = nc.dram_tensor("expert_rows", [SLOT_TILES * P + S, D], F32, kind="Internal").ap()
        done_dram = nc.dram_tensor("expert_out", [TILES * P, D], F32, kind="Internal").ap()

        att = ExitStack()
        with att:
            hT = sb(att, "hT", DK * S)
            weff = sb(att, "weff", DK * H * KA)
            caug = sb(att, "caug", T * CP)
            cosq = sb(att, "cosq", S)
            sinq = sb(att, "sinq", S)
            k_hi = sb(att, "k_hi", S, F32R)
            k_lo = sb(att, "k_lo", S, F32R)
            mods_and_weights(nc, a, x, ident, ones, mod, wov, hT, weff, caug, cosq, sinq, k_hi, k_lo, slots_dram, cbar)
            attention(nc, hT, weff, caug, cosq, sinq, k_hi, k_lo, ident, cbar)
        ffn(nc, a, x, ident, mod, wov, cbar, slots_dram, done_dram, out)


def mods_and_weights(nc, a, x, ident, ones, mod, wov, hT, weff, caug, cosq, sinq, k_hi, k_lo, slots_dram, cbar):
    st = ExitStack()
    with st:
        def sb(name, cols, dt=F32):
            return st.enter_context(nc.sbuf_tensor(name, [P, cols], dt))

        def pb(name, banks=1):
            return st.enter_context(nc.psum_tensor(name, [P, 512 * banks], F32))

        def sem(name):
            return st.enter_context(nc.semaphore(name))

        ccol = sb("ccol", 3 * DK)
        cwide = sb("cwide", DK * P)
        gate_sign = sb("gate_sign", D)
        wqaT = sb("wqaT", DK * QR)
        wqa = sb("wqa", RT * D)
        lnq = sb("lnq", RT)
        wkvT = sb("wkvT", DK * KA)
        lnkv = sb("lnkv", C)
        fold = sb("fold", H * KA)
        wv = cbar[:, H * D:H * D + H * C]
        woT = cbar[:, 0:H * D]
        wqb = sb("wqb", 2 * QR)
        afold = sb("afold", RT * H * KA)
        wmod = afold[:, 0:DK * 6 * D]
        hbuf = sb("hbuf", 2 * D)
        hTb = sb("hTb", 2 * D)
        stats = sb("stats", T * 6)
        mv = sb("mv", T * 2)
        rstd = sb("rstd", T)
        ckv = cbar[:, 5120:5120 + T * KA]
        junk = sb("junk", 512)
        ssq = sb("ssq", T * 3)
        rq = sb("rq", T)
        rc = sb("rc", T)
        tmp16 = sb("tmp16", T * 4)
        diag = sb("diag", 2 * P)
        kbuf = sb("kbuf", 4 * KA)
        rot_a = sb("rot_a", QC)
        rot_b = sb("rot_b", QC)
        kraw = sb("kraw", QC)
        zeros = cbar[:, 7168:7168 + 2 * D]

        pw = [pb("pw0", 2), pb("pw1", 2)]
        pt = [pb("pt0"), pb("pt1")]
        pk = [pb("pk0"), pb("pk1")]

        ld_x = sem("ld_x")
        ld_mod = sem("ld_mod")
        ld_w = sem("ld_w")
        ld_qb = [sem("ld_qb0"), sem("ld_qb1")]
        zeroed = sem("zeroed")
        consts = sem("consts")
        exp_c = sem("exp_c")
        silu_c = sem("silu_c")
        mod_mm = sem("mod_mm")
        mod_used = sem("mod_used")
        mod_copied = sem("mod_copied")
        dve = sem("dve")
        pool = sem("pool")
        var_ready = sem("var_ready")
        stats_ready = sem("stats_ready")
        rstd_ready = sem("rstd_ready")
        h_ready = sem("h_ready")
        ht_mm = sem("ht_mm")
        ht_ready = sem("ht_ready")
        kv_mm = sem("kv_mm")
        kv_ready = sem("kv_ready")
        squares_ready = sem("squares_ready")
        sums_ready = sem("sums_ready")
        roots_ready = sem("roots_ready")
        k_ready = sem("k_ready")
        k_mm = sem("k_mm")
        k_used = sem("k_used")
        diag_ready = sem("diag_ready")
        rq_mm = sem("rq_mm")
        rq_used = sem("rq_used")
        fold_ready = sem("fold_ready")
        a_mm = sem("a_mm")
        a_used = sem("a_used")
        w_mm = sem("w_mm")
        w_used = sem("w_used")
        ov_mm = sem("ov_mm")
        ov_used = sem("ov_used")

        block = st.enter_context(nc.Block())

        NLW = 9

        @block.sync
        def _(sp):
            sp.sem_inc(a_mm, 2)
            sp.dma_start(x[:, :].rearrange("p (t d) -> p t d", t=T),
                         a["x"].rearrange("(t p) d -> p t d", p=P)).then_inc(ld_x, 16)
            sp.dma_start(ccol[:, 0:DK], a["c"]).then_inc(ld_mod, 16)
            sp.dma_start(wmod.rearrange("p (k n) -> p k n", k=DK),
                         a["wmod"].rearrange("(k p) n -> p k n", p=P)).then_inc(ld_mod, 16)
            sp.dma_start(wqaT[:, :].rearrange("p (k n) -> p k n", k=DK),
                         a["wqaT"].rearrange("(k p) n -> p k n", p=P)).then_inc(ld_w, 16)
            sp.dma_start(wkvT[:, :].rearrange("p (k n) -> p k n", k=DK),
                         a["wkvT"].rearrange("(k p) n -> p k n", p=P)).then_inc(ld_w, 16)
            sp.dma_start(lnkv[:, :], a["lnkv"]).then_inc(ld_w, 16)
            sp.dma_start(cosq[0:ROPE, :], a["cos"]).then_inc(ld_w, 16)
            sp.dma_start(sinq[0:ROPE, :], a["sin"]).then_inc(ld_w, 16)
            sp.dma_start(wqa[:, 0:(RT - 1) * D].rearrange("p (k n) -> p k n", n=D),
                         a["wqa"][0:(RT - 1) * P, :].rearrange("(k p) n -> p k n", p=P)).then_inc(ld_w, 16)
            sp.dma_start(wqa[0:RL, (RT - 1) * D:RT * D], a["wqa"][(RT - 1) * P:QR, :]).then_inc(ld_w, 16)
            sp.dma_start(lnq[:, :], a["lnq"]).then_inc(ld_w, 16)
            sp.dma_start(woT, a["woT"]).then_inc(ld_w, 16)
            sp.dma_start(wv, a["wv"]).then_inc(fold_ready, 16)
            sp.wait_ge(consts, 4)
            sp.dma_start(fold[ROPE:P, :].rearrange("p (h n) -> p h n", h=H)[:, :, ROPE:KA],
                         a["wk"].rearrange("p (h n) -> p h n", h=H)).then_inc(fold_ready, 16)
            with sp.Fori(0, H // 2) as trip_no:
                h = trip_no * 2
                for u in range(2):
                    sp.wait_ge(a_mm, h + u + 1)
                    sp.dma_start(wqb[:, u * QR:(u + 1) * QR],
                                 a["wqb"][:, ds((h + u) * QR, QR)]).then_inc(ld_qb[u], 16)

        @block.gpsimd
        def _(gp):
            step = Chain(gp, pool)
            step(gp.memset(ident[:, :], 0.0))
            step(gp.affine_select(out=ident[:, :], in_=ident[:, :], compare_op=ALU.not_equal, fill=1.0,
                                  base=0, pattern=[[-1, P]], channel_multiplier=1))
            step(gp.memset(ones[:, :], 1.0))
            step(gp.memset(zeros, 0.0))
            step(gp.memset(k_hi[KA:KS, :].bitcast(F32), 1.0))
            step(gp.memset(k_lo[KA:KS, :].bitcast(F32), 0.0))
            step(gp.memset(fold[:, :], 0.0))
            step(gp.memset(caug[:, :], 0.0))
            step(gp.memset(caug[:, :].rearrange("p (t n) -> p t n", t=T)[:, :, C:C + 1], 1.0))
            step(gp.tensor_copy(fold[0:ROPE, :].rearrange("p (h n) -> p h n", h=H)[:, :, 0:ROPE],
                                ident[0:ROPE, 0:ROPE].rearrange("p (h n) -> p h n", h=1).to_broadcast([ROPE, H, ROPE])))
            gp.sem_inc(consts, 4)
            rows = slots_dram.rearrange("(n p r) d -> n p (r d)", p=P, r=2)
            with gp.Fori(0, SLOT_TILES // 2) as n:
                gp.dma_start(rows[ds(n, 1), :, :].rearrange("a p n -> (a p) n"), zeros).then_inc(zeroed, 16)
            gp.wait_ge(zeroed, 16 * (SLOT_TILES // 2))

        @block.scalar
        def _(act):
            act.wait_ge(ld_mod, 32)
            act.activation(ccol[:, DK:2 * DK], ccol[:, 0:DK], ACT.Exp, scale=-1.0).then_inc(exp_c, 1)
            act.wait_ge(var_ready, 1)
            act.activation(rstd[:, :], tmp16[:, 0:T], ACT.Sqrt).then_inc(rstd_ready, 1)
            with act.Fori(0, T // 2) as trip_no:
                t = trip_no * 2
                for u in range(2):
                    act.wait_ge(ht_mm, t + u + 3)
                    act.wait_ge(kv_mm, t + u + 1)
                    act.copy(hTb[:, u * D:(u + 1) * D], pt[u][:, 0:D]).then_inc(ht_ready, 1)
                    act.copy(hT[:, :].rearrange("p (k s) -> p k s", k=DK)[:, :, ds((t + u) * P, P)],
                             pt[u][:, 0:D].rearrange("p (k s) -> p k s", k=DK)).then_inc(ht_ready, 1)
                    act.wait_ge(kv_mm, t + u + 3)
                    for c in range(2):
                        act.activation(pw[u][:, c * 512:c * 512 + 341], pw[u][:, c * 512:c * 512 + 341], ACT.Square,
                                       accum_out=ssq[:, ds((t + u) * 3 + c, 1)])
                    act.wait_ge(kv_ready, t + u + 3)
                    act.activation(junk[:, ds((t + u) * C, C)], ckv[:, ds((t + u) * KA + ROPE, C)], ACT.Square,
                                   accum_out=ssq[:, ds((t + u) * 3 + 2, 1)]).then_inc(squares_ready, 1)
            act.wait_ge(sums_ready, 2)
            act.activation(rq[:, :], tmp16[:, 0:T], ACT.Sqrt).then_inc(roots_ready, 1)
            act.activation(rc[:, :], tmp16[:, T:2 * T], ACT.Sqrt).then_inc(roots_ready, 1)

        @block.vector
        def _(v):
            step = Chain(v, dve)
            v.wait_ge(exp_c, 1)
            v.wait_ge(consts, 4)
            step(v.tensor_scalar(ccol[:, DK:2 * DK], ccol[:, DK:2 * DK], 1.0, None, ALU.add))
            step(v.reciprocal(ccol[:, 2 * DK:3 * DK], ccol[:, DK:2 * DK]))
            step(v.tensor_tensor(ccol[:, 2 * DK:3 * DK], ccol[:, 2 * DK:3 * DK], ccol[:, 0:DK], ALU.mult))
            for k in range(DK):
                v.tensor_scalar(cwide[:, k * P:(k + 1) * P], ones[:, :], ccol[:, 2 * DK + k:2 * DK + k + 1], None,
                                ALU.mult).then_inc(silu_c, 1)
            v.wait_ge(ld_x, 16)
            with v.Fori(0, T) as t:
                v.bn_stats(stats[:, ds(t * 6, 6)], x[:, ds(t * D, D)]).then_inc(stats_ready, 1)
            v.wait_ge(stats_ready, T)
            for t in range(T):
                last = v.bn_aggr(mv[:, t * 2:(t + 1) * 2], stats[:, t * 6:(t + 1) * 6])
            step(last)
            var = mv[:, :].rearrange("p (t n) -> p t n", n=2)[:, :, 1]
            v.tensor_scalar(tmp16[:, 0:T], var, 1e-5, None, ALU.add).then_inc(var_ready, 1)
            for c in range(3):
                v.wait_ge(mod_mm, c + 1)
                v.tensor_copy(mod[:, c * 512:(c + 1) * 512], pw[c % 2][:, 0:512]).then_inc(mod_used, 1)
            v.wait_ge(mod_used, 3)
            for part in (1, 4):
                step(v.tensor_scalar(mod[:, part * D:(part + 1) * D], mod[:, part * D:(part + 1) * D], 1.0, None,
                                     ALU.add))
            for part in (2, 5):
                g = mod[:, part * D:(part + 1) * D]
                step(v.tensor_scalar(gate_sign[:, :], g, 0.0, 2.0, ALU.is_ge, ALU.mult))
                step(v.tensor_scalar(gate_sign[:, :], gate_sign[:, :], -1.0, None, ALU.add))
                step(v.tensor_tensor(g, g, gate_sign[:, :], ALU.mult))
                step(v.scalar_tensor_tensor(out=g, in0=g, scalar=0.25, in1=gate_sign[:, :], op0=ALU.max,
                                            op1=ALU.mult))
            v.wait_ge(rstd_ready, 1)
            step(v.reciprocal(rstd[:, :], rstd[:, :]))
            with v.Fori(0, T // 2) as trip_no:
                t = trip_no * 2
                step.enter(t, 2)
                for u in range(2):
                    hb = hbuf[:, u * D:(u + 1) * D]
                    v.wait_ge(ht_mm, t + u + 1)
                    step(v.tensor_scalar(hb, x[:, ds((t + u) * D, D)], mv[:, ds((t + u) * 2, 1)],
                                         rstd[:, ds(t + u, 1)], ALU.subtract, ALU.mult))
                    step(v.tensor_tensor(hb, hb, mod[:, D:2 * D], ALU.mult))
                    v.tensor_tensor(hb, hb, mod[:, 0:D], ALU.add).then_inc(h_ready, 1)
                for u in range(2):
                    v.wait_ge(kv_mm, t + u + 3)
                    v.tensor_copy(ckv[:, ds((t + u) * KA, KA)], pk[u][:, 0:KA]).then_inc(kv_ready, 1)
            step.leave(T, 2)
            v.wait_ge(squares_ready, T + 2)
            s3 = ssq[:, :].rearrange("p (t n) -> p t n", n=3)
            step(v.tensor_tensor(tmp16[:, 0:T], s3[:, :, 0], s3[:, :, 1], ALU.add))
            v.tensor_scalar(tmp16[:, 0:T], tmp16[:, 0:T], 1.0 / QR, 1e-6, ALU.mult, ALU.add).then_inc(sums_ready, 1)
            v.tensor_scalar(tmp16[:, T:2 * T], s3[:, :, 2], 1.0 / C, 1e-6, ALU.mult, ALU.add).then_inc(sums_ready, 1)
            v.wait_ge(roots_ready, 2)
            step(v.reciprocal(rq[:, :], rq[:, :]))
            step(v.reciprocal(rc[:, :], rc[:, :]))
            v.wait_ge(ld_w, 16 * NLW)
            v.wait_ge(kv_ready, T + 2)
            with v.Fori(0, T // 4) as q:
                step.enter(q, 6)
                for j in range(4):
                    t = q * 4 + j
                    if j == 0:
                        v.wait_ge(k_used, q + 1)
                    v.tensor_copy(kbuf[:, j * KA:j * KA + ROPE], ckv[:, ds(t * KA, ROPE)]).then_inc(k_ready, 1)
                    v.scalar_tensor_tensor(out=kbuf[:, j * KA + ROPE:(j + 1) * KA], in0=ckv[:, ds(t * KA + ROPE, C)],
                                           scalar=rc[:, ds(t, 1)], in1=lnkv[:, :], op0=ALU.mult,
                                           op1=ALU.mult).then_inc(k_ready, 1)
                    v.scalar_tensor_tensor(out=caug[:, ds(t * CP, C)], in0=ckv[:, ds(t * KA + ROPE, C)],
                                           scalar=rc[:, ds(t, 1)], in1=lnkv[:, :], op0=ALU.mult,
                                           op1=ALU.mult).then_inc(k_ready, 1)
                v.wait_ge(k_mm, q + 1)
                step(v.tensor_tensor(rot_a[0:ROPE, :], pk[0][0:ROPE, :], cosq[0:ROPE, ds(q * QC, QC)], ALU.mult))
                step(v.tensor_tensor(rot_b[HALF:ROPE, :], pk[0][0:HALF, :], sinq[0:HALF, ds(q * QC, QC)], ALU.mult))
                step(v.tensor_tensor(rot_b[0:HALF, :], pk[0][HALF:ROPE, :], sinq[HALF:ROPE, ds(q * QC, QC)], ALU.mult))
                step(v.tensor_tensor(kraw[0:ROPE, :], rot_a[0:ROPE, :], rot_b[0:ROPE, :], ALU.add))
                step(v.tensor_copy(kraw[ROPE:KA, :], pk[0][ROPE:KA, :]))
                step(v.tensor_copy(k_hi[0:KA, ds(q * QC, QC)], kraw[0:KA, :]))
                v.tensor_tensor(k_lo[0:KA, ds(q * QC, QC)], kraw[0:KA, :],
                                k_hi[0:KA, ds(q * QC, QC)].bitcast(F32), ALU.subtract).then_inc(k_used, 1)
                v.wait_ge(k_used, q + 2)
            step.leave(T // 4)
            with v.Fori(0, T // 2) as trip_no:
                t = trip_no * 2
                for u in range(2):
                    v.wait_ge(rq_used, t + u + 1)
                    v.tensor_scalar(diag[:, u * P:(u + 1) * P], ident[:, :], rq[:, ds(t + u, 1)], None,
                                    ALU.mult).then_inc(diag_ready, 1)
                for u in range(2):
                    v.wait_ge(rq_mm, t + u + 1)
                    tok = ds((t + u) * P, P)
                    v.tensor_tensor(cosq[0:ROPE, tok], cosq[0:ROPE, tok], pt[u][0:ROPE, 0:P], ALU.mult)
                    v.tensor_tensor(sinq[0:ROPE, tok], sinq[0:ROPE, tok], pt[u][0:ROPE, 0:P], ALU.mult)
                    v.tensor_copy(cosq[ROPE:KA, tok], pt[u][ROPE:KA, 0:P]).then_inc(rq_used, 1)
            with v.Fori(0, H // 2) as trip_no:
                h = trip_no * 2
                for u in range(2):
                    v.wait_ge(a_mm, h + u + 3)
                    for r in range(RT):
                        n = P if r < RT - 1 else RL
                        src = pw[u][0:n, (r // 3) * 512 + (r % 3) * KA:(r // 3) * 512 + (r % 3 + 1) * KA]
                        last = v.tensor_scalar(afold[0:n, ds((h + u) * KA + r * H * KA, KA)], src, lnq[0:n, r:r + 1],
                                               None, ALU.mult)
                    last.then_inc(a_used, 1)
            for c in range(3):
                for k in range(DK):
                    n = c * DK + k
                    v.wait_ge(w_mm, n + 1)
                    v.tensor_copy(weff[:, k * H * KA + c * 512:k * H * KA + (c + 1) * 512],
                                  pt[n % 2][:, :]).then_inc(w_used, 1)
            for g in range(4):
                v.wait_ge(ov_mm, g + 1)
                v.tensor_copy(wov[:, g * D:(g + 1) * D], pk[g % 2][:, 0:D]).then_inc(ov_used, 1)

        @block.tensor
        def _(pe):
            pe.wait_ge(silu_c, DK)
            for c in range(3):
                if c == 2:
                    pe.wait_ge(mod_used, 1)
                for k in range(DK):
                    last = pe.matmul(pw[c % 2][:, 0:512], cwide[:, k * P:(k + 1) * P],
                                     wmod[:, k * 6 * D + c * 512:k * 6 * D + (c + 1) * 512],
                                     start=(k == 0), stop=(k == DK - 1))
                last.then_inc(mod_mm, 1)
            pe.wait_ge(mod_used, 3)
            pe.wait_ge(ld_w, 16 * NLW)
            for s in (ht_mm, kv_mm, squares_ready, kv_ready):
                pe.sem_inc(s, 2)
            with pe.Fori(0, T // 2) as trip_no:
                t = trip_no * 2
                for u in range(2):
                    pe.wait_ge(h_ready, t + u + 1)
                    for k in range(DK):
                        last = pe.transpose(pt[u][:, k * P:(k + 1) * P], hbuf[:, u * D + k * P:u * D + (k + 1) * P],
                                            ident[:, :])
                    last.then_inc(ht_mm, 1)
                    pe.wait_ge(ht_ready, 2 * (t + u) + 2)
                    pe.wait_ge(squares_ready, t + u + 1)
                    pe.wait_ge(kv_ready, t + u + 1)
                    for c in range(2):
                        for k in range(DK):
                            last = pe.matmul(pw[u][:, c * 512:c * 512 + 341], hTb[:, u * D + k * P:u * D + (k + 1) * P],
                                             wqaT[:, k * QR + c * 341:k * QR + (c + 1) * 341],
                                             start=(k == 0), stop=(k == DK - 1))
                    for k in range(DK):
                        last = pe.matmul(pk[u][:, 0:KA], hTb[:, u * D + k * P:u * D + (k + 1) * P],
                                         wkvT[:, k * KA:(k + 1) * KA], start=(k == 0), stop=(k == DK - 1))
                    last.then_inc(kv_mm, 1)
            pe.wait_ge(kv_ready, T + 2)
            pe.wait_ge(squares_ready, T + 2)
            pe.sem_inc(k_used, 1)
            with pe.Fori(0, T // 4) as q:
                pe.wait_ge(k_ready, 12 * q + 12)
                pe.wait_ge(k_used, q + 1)
                for j in range(4):
                    last = pe.transpose(pk[0][0:KA, j * P:(j + 1) * P], kbuf[:, j * KA:(j + 1) * KA], ident[:, :])
                last.then_inc(k_mm, 1)
            pe.sem_inc(rq_used, 2)
            with pe.Fori(0, T // 2) as trip_no:
                t = trip_no * 2
                for u in range(2):
                    pe.wait_ge(diag_ready, t + u + 1)
                    pe.wait_ge(rq_used, t + u + 1)
                    pe.matmul(pt[u][:, 0:P], ones[:, :], diag[:, u * P:(u + 1) * P], start=True,
                              stop=True).then_inc(rq_mm, 1)
            pe.wait_ge(rq_used, T + 2)
            pe.sem_inc(a_used, 2)
            pe.wait_ge(fold_ready, 32)
            with pe.Fori(0, H // 2) as trip_no:
                h = trip_no * 2
                for u in range(2):
                    pe.wait_ge(ld_qb[u], 8 * h + 16)
                    pe.wait_ge(a_used, h + u + 1)
                    for r in range(RT):
                        n = P if r < RT - 1 else RL
                        last = pe.matmul(pw[u][0:n, (r // 3) * 512 + (r % 3) * KA:(r // 3) * 512 + (r % 3 + 1) * KA],
                                         wqb[:, u * QR + r * P:u * QR + r * P + n],
                                         fold[:, ds((h + u) * KA, KA)], start=(r % 3 == 0), stop=True,
                                         skip_group_check=True)
                    last.then_inc(a_mm, 1)
            pe.wait_ge(a_used, H + 2)
            for c in range(3):
                for k in range(DK):
                    n = c * DK + k
                    if n >= 2:
                        pe.wait_ge(w_used, n - 1)
                    for r in range(RT):
                        m = P if r < RT - 1 else RL
                        last = pe.matmul(pt[n % 2][:, :], wqa[0:m, r * D + k * P:r * D + (k + 1) * P],
                                         afold[0:m, r * H * KA + c * 512:r * H * KA + (c + 1) * 512],
                                         start=(r == 0), stop=(r == RT - 1))
                    last.then_inc(w_mm, 1)
            pe.wait_ge(k_used, T // 4 + 1)
            for g in range(4):
                if g >= 2:
                    pe.wait_ge(ov_used, g - 1)
                for j in range(4):
                    h = 4 * g + j
                    last = pe.matmul(pk[g % 2][C * j:C * (j + 1), 0:D], wv[:, h * C:(h + 1) * C],
                                     woT[:, h * D:(h + 1) * D], start=True, stop=True)
                last.then_inc(ov_mm, 1)


def attention(nc, hT, weff, caug, cosq, sinq, k_hi, k_lo, ident, cbar):
    st = ExitStack()
    with st:
        def sb(name, cols, dt=F32):
            return st.enter_context(nc.sbuf_tensor(name, [P, cols], dt))

        def pb(name, cols=QC):
            return st.enter_context(nc.psum_tensor(name, [P, cols], F32))

        def sem(name):
            return st.enter_context(nc.semaphore(name))

        q_hi = [sb("q_hi0", S, F32R), sb("q_hi1", S, F32R)]
        q_lo = [sb("q_lo0", S, F32R), sb("q_lo1", S, F32R)]
        wq = [sb("wq0", DK * KA), sb("wq1", DK * KA)]
        prob = [sb(f"prob{n}", 2 * QC) for n in range(2)]
        prob_hi = [sb(f"prob_hi{n}", 2 * QC, F16) for n in range(4)]
        prob_lo = [sb(f"prob_lo{n}", 2 * QC, F16) for n in range(4)]
        c_hi = sb("c_hi", T * CP, F16)
        c_lo = sb("c_lo", T * CP, F16)
        prob_scale = sb("prob_scale", 1)
        q_raw = sb("q_raw", QC)
        rot = sb("rot", QC)
        maxes = sb("maxes", 4 * T)
        maxneg = sb("maxneg", T)
        att_t = sb("att_t", QC)
        recip = sb("recip", 8)

        p_s = [pb("p_s0", 2 * QC), pb("p_s1", 2 * QC)]
        p_m = [pb("p_m0"), pb("p_m1")]
        p_o = pb("p_o")
        p_x = pb("p_x")

        wq_ready = sem("wq_ready")
        x_mm = sem("x_mm")
        x_used = sem("x_used")
        q_ready = sem("q_ready")
        max_mm = sem("max_mm")
        max_used = sem("max_used")
        neg_ready = sem("neg_ready")
        s_mm = sem("s_mm")
        p_ready = sem("p_ready")
        lo_ready = sem("lo_ready")
        o_mm = sem("o_mm")
        o_copied = sem("o_copied")
        zero_rows = sem("zero_rows")
        c_ready = sem("c_ready2")
        vec = sem("vec")

        MAXIMA = (0, 0, 0, 0, 3, 3, 0, 3, 3, 3, 3, 3, 0, 3, 3, 4, 0, 3, 3, 3, 3, 3, 3, 3, 3, 3, 3, 3, 0, 0, 0, 0)
        PROJECT = (1, 5, 11, 15)
        assert sum(MAXIMA) == 4 * T and all(sum(MAXIMA[:s + 2]) <= 16 * c for c, s in enumerate(PROJECT))

        def beside(first, last):
            at = {}
            for s in range(STEPS):
                copy, turn, others, maxima = [], [], [], []
                if s == 17 or (s == 1 and not first):
                    copy = [("copy", 0 if s == 17 else 1)]
                if s == 19 or (s == 3 and not first):
                    turn = [("turn", 0 if s == 19 else 1)]
                if not last:
                    maxima = [("max", n) for n in range(sum(MAXIMA[:s]), sum(MAXIMA[:s + 1]))]
                    others = [("project", c) for c in range(4) if PROJECT[c] == s]
                    others += [("row", c) for c in range(4) if 28 + c == s]
                at[s] = maxima[:2] + copy + maxima[2:] + turn + others
            return at

        ALONE = [("project", c) for c in range(4)] + [("max", n) for n in range(4 * T)] + [("row", c) for c in range(4)]

        def x_base(h, first=False):
            return 8 if first else 10 * h + 7

        def x_use(h, what, first=False, last=False):
            if h is None:
                return {"project": 0, "row": 4}[what[0]] + what[1]
            uses = [w for todo in beside(first, last).values() for w in todo if w[0] in ("project", "row", "turn")]
            return x_base(h, first) + uses.index(what)

        block = st.enter_context(nc.Block())

        @block.gpsimd
        def _(gp):
            gp.memset(prob_scale[:, :], float(np.log(P_SCALE))).then_inc(zero_rows, 1)
            gp.wait_ge(zero_rows, 1)
            for u in range(2):
                gp.memset(q_lo[u][KA:KS, :].bitcast(F32), 0.0).then_inc(zero_rows, 1)
                gp.wait_ge(zero_rows, u + 2)
            with gp.Fori(0, H) as h:
                for s in range(STEPS):
                    n = h * STEPS + s
                    gp.wait_ge(p_ready, n + 3)
                    gp.wait_ge(o_mm, n + 1)
                    gp.tensor_tensor(prob_lo[s % 4][:, :], prob[s % 2][:, :], prob_hi[s % 4][:, :],
                                     ALU.subtract).then_inc(lo_ready, 1)

        @block.scalar
        def _(act):
            w3 = weff[:, :].rearrange("p (k n) -> p k n", k=DK)

            def copy_wq(h, u):
                act.wait_ge(q_ready, 4 * h + 1)
                act.copy(wq[u][:, :].rearrange("p (k n) -> p k n", k=DK), w3[:, :, ds(h * KA, KA)]).then_inc(wq_ready, 1)

            def head(h, u, more=True):
                for s in range(STEPS):
                    n = h * STEPS + s
                    act.wait_ge(s_mm, n + 1)
                    act.wait_ge(lo_ready, n + 1)
                    act.wait_ge(o_mm, n + 1)
                    act.activation(prob[s % 2][:, :], p_s[s % 2][:, :], ACT.Exp, bias=prob_scale[:, :],
                                   scale=SCALE)
                    act.activation(prob_hi[s % 4][:, :], p_s[s % 2][:, :], ACT.Exp, bias=prob_scale[:, :],
                                   scale=SCALE).then_inc(p_ready, 1)
                    if s == 24 and more:
                        copy_wq(h + 2, u)

            act.preload_act_table(ACT.Exp)
            for u in range(2):
                copy_wq(u, u)
            with act.Fori(0, (H - 2) // 2) as trip_no:
                h = trip_no * 2
                for u in range(2):
                    head(h + u, u)
            for u in range(2):
                head(H - 2 + u, u, more=False)

        @block.vector
        def _(v):
            step = Chain(v, vec)

            def project(c, g, u, use):
                tok = slice(c * QC, (c + 1) * QC)
                v.wait_ge(x_mm, use + 1)
                v.wait_ge(q_ready, 4 * g + c + 5)
                step(v.tensor_tensor(q_raw[0:KA, :], p_x[0:KA, :], cosq[0:KA, tok], ALU.mult))
                step(v.tensor_tensor(rot[HALF:ROPE, :], p_x[0:HALF, :], sinq[0:HALF, tok], ALU.mult))
                v.tensor_tensor(rot[0:HALF, :], p_x[HALF:ROPE, :], sinq[HALF:ROPE, tok], ALU.mult).then_inc(x_used, 1)
                v.wait_ge(x_used, use + 2)
                step(v.tensor_tensor(q_raw[0:ROPE, :], q_raw[0:ROPE, :], rot[0:ROPE, :], ALU.add))
                step(v.tensor_copy(q_hi[u][0:KA, tok], q_raw[0:KA, :]))
                v.tensor_tensor(q_lo[u][0:KA, tok], q_raw[0:KA, :], q_hi[u][0:KA, tok].bitcast(F32),
                                ALU.subtract).then_inc(q_ready, 1)

            def maximum(n, g):
                v.wait_ge(max_mm, 64 * g + n + 1)
                v.tensor_reduce(maxes[:, n:n + 1], p_m[n % 2][:, :], AX.X, ALU.max).then_inc(max_used, 1)
                if n == 4 * T - 1:
                    v.wait_ge(max_used, 64 * g + n + 3)
                    v.tensor_reduce(maxneg[:, :], maxes[:, :].rearrange("p (t c) -> p t c", c=4), AX.X, ALU.max,
                                    negate=True).then_inc(neg_ready, 1)
                    v.wait_ge(neg_ready, g + 1)

            def row(c, u, use):
                v.wait_ge(x_mm, use + 1)
                v.tensor_copy(q_hi[u][KA:KS, c * QC:(c + 1) * QC], p_x[KA:KS, :]).then_inc(x_used, 1)

            def copy_out(half, h):
                v.wait_ge(o_mm, STEPS * h + 16 * half + 16 + 4)
                v.tensor_copy(att_t[:, :], p_o[:, :]).then_inc(o_copied, 1)

            def turn(half, h, use):
                v.wait_ge(x_mm, use + 1)
                src = p_x[:, :].rearrange("p (b s n) -> p b s n", b=4, s=2)
                r = recip[:, :].rearrange("p (b s n) -> p b s n", b=4, s=2)
                step(v.reciprocal(r, src[:, :, :, C:C + 1]))
                dst = cbar[:, half * 8 * HC:(half + 1) * 8 * HC].rearrange("p (s b n) -> p b s n", s=2, b=4)
                v.tensor_tensor(dst[:, :, :, ds(h * C, C)], src[:, :, :, 0:C], r.to_broadcast([P, 4, 2, C]),
                                ALU.mult).then_inc(x_used, 1)
                v.wait_ge(x_used, use + 2)

            def head(h, u, first=False, last=False):
                for s, todo in beside(first, last).items():
                    for what in todo:
                        kind, c = what
                        if kind == "project":
                            project(c, h + 1, 1 - u, x_use(h, what, first, last))
                        elif kind == "max":
                            maximum(c, h + 1)
                        elif kind == "row":
                            row(c, 1 - u, x_use(h, what, first, last))
                        elif kind == "copy":
                            copy_out(c, h - c)
                        else:
                            turn(c, h - c, x_use(h, what, first, last))

            v.tensor_scalar(c_hi[:, :], caug[:, :], C_SCALE, None, ALU.mult).then_inc(c_ready, 1)
            v.wait_ge(c_ready, 1)
            v.scalar_tensor_tensor(out=c_lo[:, :], in0=caug[:, :], scalar=C_SCALE, in1=c_hi[:, :], op0=ALU.mult,
                                   op1=ALU.subtract).then_inc(c_ready, 1)
            for kind, c in ALONE:
                if kind == "project":
                    project(c, 0, 0, x_use(None, (kind, c)))
                elif kind == "max":
                    maximum(c, 0)
                else:
                    row(c, 0, x_use(None, (kind, c)))
            head(0, 0, first=True)
            start = step.now
            with v.Fori(0, (H - 2) // 2) as trip_no:
                h = 1 + trip_no * 2
                step.before, step.now = start + (h - 1) * STEPS_V, 0
                head(h, 1)
                head(h + 1, 0)
                assert step.now == 2 * STEPS_V
            step.before, step.now = start + (H - 2) * STEPS_V, 0
            head(H - 1, 1, last=True)
            copy_out(1, H - 1)
            turn(1, H - 1, x_base(H - 1) + 2)

        @block.tensor
        def _(pe):
            for s, n in ((x_used, 1), (q_ready, 5), (max_used, 2), (p_ready, 2), (lo_ready, 2), (o_mm, 4), (o_copied, 1)):
                pe.sem_inc(s, n)

            def project(c, g, u, use):
                pe.wait_ge(wq_ready, g + 1)
                pe.wait_ge(x_used, use + 1)
                for k in range(DK):
                    last = pe.matmul(p_x[0:KA, :], wq[u][:, k * KA:(k + 1) * KA],
                                     hT[:, k * S + c * QC:k * S + (c + 1) * QC], start=(k == 0), stop=(k == DK - 1))
                last.then_inc(x_mm, 1)

            def maximum(n, g, u):
                j, kc = n // 4, n % 4
                if kc == 0:
                    pe.wait_ge(q_ready, 4 * g + j // 4 + 6)
                pe.wait_ge(max_used, 64 * g + n + 1)
                pe.matmul(p_m[n % 2][:, :], q_hi[u][0:KA, j * P:(j + 1) * P], k_hi[0:KA, kc * QC:(kc + 1) * QC],
                          start=True, stop=True).then_inc(max_mm, 1)

            def row(c, g, use):
                pe.wait_ge(neg_ready, g + 1)
                pe.wait_ge(x_used, use + 1)
                for j in range(4):
                    last = pe.matmul(p_x[KA:KS, j * P:(j + 1) * P], maxneg[:, 4 * c + j:4 * c + j + 1], ident[:, :],
                                     start=True, stop=True)
                last.then_inc(x_mm, 1)

            def turn(half, h, use):
                pe.wait_ge(o_copied, 2 * h + half + 2)
                pe.wait_ge(x_used, use + 1)
                for b in range(4):
                    last = pe.transpose(p_x[:, b * P:(b + 1) * P], att_t[:, b * P:(b + 1) * P], ident[:, :])
                last.then_inc(x_mm, 1)

            def scores(s, h, u, first, between):
                half, kt = s // 16, s % 16
                n = STEPS * h + s
                if kt == 0:
                    pe.wait_ge(x_used, x_base(h, first) + 2 * half - 1)
                pe.wait_ge(p_ready, n + 1)
                keys = slice(kt * P, (kt + 1) * P)
                for part, (kk, qq) in enumerate(((k_hi, q_hi), (k_hi, q_lo), (k_lo, q_hi))):
                    if part and between:
                        between.pop(0)()
                    for j in range(2):
                        c = 2 * half + j
                        last = pe.matmul(p_s[s % 2][:, j * QC:(j + 1) * QC], kk[0:KS, keys],
                                         qq[u][0:KS, c * QC:(c + 1) * QC], start=(part == 0), stop=(part == 2))
                last.then_inc(s_mm, 1)

            def weigh(s, h):
                half, kt = s // 16, s % 16
                n = STEPS * h + s
                pe.wait_ge(lo_ready, n + 3)
                if kt == 0:
                    pe.wait_ge(o_copied, 2 * h + half + 1)
                for part, (cc, pp) in enumerate(((c_hi, prob_hi[s % 4]), (c_lo, prob_hi[s % 4]),
                                              (c_hi, prob_lo[s % 4]))):
                    for j in range(2):
                        last = pe.matmul(p_o[j * CP:(j + 1) * CP, :], cc[:, kt * CP:(kt + 1) * CP],
                                         pp[:, j * QC:(j + 1) * QC], start=(kt == 0 and part == 0),
                                         stop=(kt == 15 and part == 2))
                last.then_inc(o_mm, 1)

            def head(h, u, first=False, last=False):
                for s, todo in beside(first, last).items():
                    maxima = [(lambda c=c: maximum(c, h + 1, 1 - u)) for kind, c in todo if kind == "max"]
                    scores(s, h, u, first, maxima)
                    if s >= 2:
                        weigh(s - 2, h)
                    elif not first:
                        weigh(STEPS - 2 + s, h - 1)
                    for m in maxima:
                        m()
                    for what in todo:
                        kind, c = what
                        if kind == "project":
                            project(c, h + 1, 1 - u, x_use(h, what, first, last))
                        elif kind == "row":
                            row(c, h + 1, x_use(h, what, first, last))
                        elif kind == "turn":
                            turn(c, h - c, x_use(h, what, first, last))

            pe.wait_ge(zero_rows, 3)
            for kind, c in ALONE:
                if kind == "project":
                    project(c, 0, 0, x_use(None, (kind, c)))
                elif kind == "max":
                    maximum(c, 0, 0)
                else:
                    row(c, 0, x_use(None, (kind, c)))
            pe.wait_ge(c_ready, 2)
            head(0, 0, first=True)
            with pe.Fori(0, (H - 2) // 2) as trip_no:
                h = 1 + trip_no * 2
                head(h, 1)
                head(h + 1, 0)
            head(H - 1, 1, last=True)
            weigh(STEPS - 2, H - 1)
            weigh(STEPS - 1, H - 1)
            turn(1, H - 1, x_base(H - 1) + 2)


def ffn(nc, a, x, ident, mod, wov, cbar, slots_dram, done_dram, out):
    outer = ExitStack()
    with outer:
        def keep(name, cols, dt=F32):
            return outer.enter_context(nc.sbuf_tensor(name, [P, cols], dt))

        hall = keep("hall", T * D)
        mv = keep("mv2", T * 2)
        rstd = keep("rstd2", T)
        weight = keep("weight", T * 8)
        slot = keep("slot", T * 8, U32)
        slot_out = keep("slot_out", T * 8, U32)
        tile_expert = keep("tile_expert", TILES, I32)
        project_out(nc, x, ident, mod, wov, cbar, mv, rstd)
        route(nc, a, x, ident, mod, mv, rstd, hall, weight, slot, slot_out, tile_expert, slots_dram)
        experts(nc, a, ident, hall, slot, tile_expert, slots_dram, done_dram)
        combine(nc, x, mod, weight, slot_out, done_dram, out)


def project_out(nc, x, ident, mod, wov, cbar, mv, rstd):
    st = ExitStack()
    with st:
        def sb(name, cols, dt=F32):
            return st.enter_context(nc.sbuf_tensor(name, [P, cols], dt))

        def sem(name):
            return st.enter_context(nc.semaphore(name))

        cst = [sb("cst0", HC), sb("cst1", HC)]
        ctb = [sb("ctb0", HC), sb("ctb1", HC)]
        gated = sb("gated", D)
        stats = sb("stats2", T * 6)
        var = sb("var2", T)
        p_t = [st.enter_context(nc.psum_tensor(f"p_t{n}", [P, HC], F32)) for n in range(2)]
        p_y = [st.enter_context(nc.psum_tensor(f"p_y{n}", [P, D], F32)) for n in range(2)]
        c_ready = sem("c_ready")
        ct_mm = sem("ct_mm")
        ct_ready = sem("ct_ready")
        y_mm = sem("y_mm")
        y_used = sem("y_used")
        vec = sem("vec2")
        var_ready = sem("var_ready2")
        stats_ready = sem("stats_ready2")
        root_ready = sem("root_ready2")
        block = st.enter_context(nc.Block())

        @block.gpsimd
        def _(gp):
            with gp.Fori(0, T // 2) as trip_no:
                t = trip_no * 2
                for u in range(2):
                    gp.wait_ge(ct_mm, t + u + 1)
                    gp.tensor_copy(cst[u][:, :], cbar[:, ds((t + u) * HC, HC)]).then_inc(c_ready, 1)

        @block.scalar
        def _(act):
            with act.Fori(0, T // 2) as trip_no:
                t = trip_no * 2
                for u in range(2):
                    act.wait_ge(ct_mm, t + u + 3)
                    act.wait_ge(y_mm, t + u + 1)
                    act.copy(ctb[u][:, :], p_t[u][:, :]).then_inc(ct_ready, 1)
            act.wait_ge(var_ready, 1)
            act.activation(rstd[:, :], var[:, :], ACT.Sqrt).then_inc(root_ready, 1)

        @block.vector
        def _(v):
            step = Chain(v, vec)
            with v.Fori(0, T // 2) as trip_no:
                t = trip_no * 2
                step.enter(t, 1)
                for u in range(2):
                    xt = x[:, ds((t + u) * D, D)]
                    v.wait_ge(y_mm, t + u + 3)
                    v.tensor_tensor(gated[:, :], p_y[u][:, :], mod[:, 2 * D:3 * D], ALU.mult).then_inc(y_used, 1)
                    v.wait_ge(y_used, t + u + 3)
                    step(v.tensor_tensor(xt, xt, gated[:, :], ALU.add))
            step.leave(T, 2)
            with v.Fori(0, T) as t:
                v.bn_stats(stats[:, ds(t * 6, 6)], x[:, ds(t * D, D)]).then_inc(stats_ready, 1)
            v.wait_ge(stats_ready, T)
            for t in range(T):
                last = v.bn_aggr(mv[:, t * 2:(t + 1) * 2], stats[:, t * 6:(t + 1) * 6])
            step(last)
            v.tensor_scalar(var[:, :], mv[:, :].rearrange("p (t n) -> p t n", n=2)[:, :, 1], 1e-5, None,
                            ALU.add).then_inc(var_ready, 1)
            v.wait_ge(root_ready, 1)
            step(v.reciprocal(rstd[:, :], rstd[:, :]))

        @block.tensor
        def _(pe):
            for s in (ct_mm, ct_ready, y_mm, y_used):
                pe.sem_inc(s, 2)
            with pe.Fori(0, T // 2) as trip_no:
                t = trip_no * 2
                for u in range(2):
                    pe.wait_ge(c_ready, t + u + 1)
                    pe.wait_ge(ct_ready, t + u + 1)
                    for g in range(4):
                        last = pe.transpose(p_t[u][:, g * P:(g + 1) * P], cst[u][:, g * P:(g + 1) * P], ident[:, :])
                    last.then_inc(ct_mm, 1)
                    pe.wait_ge(ct_ready, t + u + 3)
                    pe.wait_ge(y_used, t + u + 1)
                    for g in range(4):
                        last = pe.matmul(p_y[u][:, :], ctb[u][:, g * P:(g + 1) * P], wov[:, g * D:(g + 1) * D],
                                         start=(g == 0), stop=(g == 3))
                    last.then_inc(y_mm, 1)


def route(nc, a, x, ident, mod, mv, rstd, hall, weight, slot, slot_out, tile_expert, slots_dram):
    st = ExitStack()
    with st:
        def sb(name, cols, dt=F32):
            return st.enter_context(nc.sbuf_tensor(name, [P, cols], dt))

        def sem(name):
            return st.enter_context(nc.semaphore(name))

        PADG = 16
        PADE = E + 8
        gate = sb("gate", DK * E)
        lower = sb("lower", P)
        ones = sb("ones2", P)
        thresholds = sb("thresholds", T)
        numbers = sb("numbers", SLOT_TILES)
        hb = [sb("hb0", D), sb("hb1", D)]
        h2T = [sb("h2T0", D), sb("h2T1", D)]
        sc = sb("sc", T * E)
        tmp = sb("tmp", T * E)
        gpad = sb("gpad", T * PADG)
        gtop = sb("gtop", T * 8)
        gkey = sb("gkey", T * 8)
        grep = sb("grep", T * PADG)
        gmask = sb("gmask", T * GROUPS)
        gpen = sb("gpen", T * GROUPS)
        epad = sb("epad", T * PADE)
        etop = sb("etop", T * 8)
        ekey = sb("ekey", T * 8)
        erep = sb("erep", T * PADE)
        chosen = sb("chosen", T * E)
        wn = sb("wn", T * E)
        wsum = sb("wsum", T)
        before = sb("before", (T + 1) * E)
        cmp = sb("cmp", E * T)
        ntiles = sb("ntiles", E)
        scan = [sb("scan0", E), sb("scan1", E)]
        first = sb("first", E)
        val = sb("val", T * E)
        vtop = sb("vtop", T * 8)
        texp = sb("texp", SLOT_TILES * E)
        tsum = sb("tsum", TILES)
        p_t = [st.enter_context(nc.psum_tensor(f"p_tn{n}", [P, D], F32)) for n in range(2)]
        p_l = [st.enter_context(nc.psum_tensor(f"p_l{n}", [P, E], F32)) for n in range(2)]
        p_pos = st.enter_context(nc.psum_tensor("p_pos", [P, T * E], F32))
        p_cnt = st.enter_context(nc.psum_tensor("p_cnt", [P, E], F32))
        ld = sem("ld3")
        h_ready = sem("h_ready3")
        t_mm = sem("t_mm3")
        t_ready = sem("t_ready3")
        l_mm = sem("l_mm3")
        l_used = sem("l_used3")
        kept = sem("kept3")
        exped = sem("exped3")
        pads = sem("pads3")
        pool = sem("pool3")
        chosen_ready = sem("chosen_ready3")
        cum_ready = sem("cum_ready3")
        pos_mm = sem("pos_mm3")
        vec = sem("vec3")
        stored = sem("stored3")
        block = st.enter_context(nc.Block())

        @block.sync
        def _(sp):
            for k in range(DK):
                sp.dma_start(gate[:, k * E:(k + 1) * E], a["gate"][k * P:(k + 1) * P, :]).then_inc(ld, 16)
            sp.dma_start(lower[:, :], a["lower"]).then_inc(ld, 16)
            sp.dma_start(thresholds[:, :], a["thresholds"]).then_inc(ld, 16)
            sp.dma_start(numbers[:, :], a["numbers"]).then_inc(ld, 16)
            sp.wait_ge(kept, T + 2)
            sp.dma_start(slots_dram[SLOT_TILES * P:SLOT_TILES * P + S, :].rearrange("(t p) d -> p t d", p=P),
                         hall[:, :].rearrange("p (t d) -> p t d", t=T)).then_inc(stored, 16)
            sp.wait_ge(stored, 16)

        @block.gpsimd
        def _(gp):
            step = Chain(gp, pool)
            step(gp.memset(ones[:, :], 1.0))
            step(gp.memset(gpad[:, :].rearrange("p (t n) -> p t n", t=T)[:, :, GROUPS:8], -1.0))
            step(gp.memset(gpad[:, :].rearrange("p (t n) -> p t n", t=T)[:, :, 8:PADG], 2.0))
            step(gp.memset(gkey[:, :], 2.0))
            step(gp.memset(ekey[:, :], 2.0))
            step(gp.memset(tsum[:, 0:T], float(E)))
            step(gp.memset(tsum[:, T:2 * T], float(E + 1)))
            step(gp.memset(before[:, 0:E], 0.0))
            gp.memset(epad[:, :].rearrange("p (t n) -> p t n", t=T)[:, :, E:PADE], 2.0).then_inc(pads, 1)
            gp.wait_ge(pads, 1)
            with gp.Fori(0, T // 2) as trip_no:
                t = trip_no * 2
                for u in range(2):
                    gp.wait_ge(h_ready, t + u + 1)
                    gp.tensor_copy(hall[:, ds((t + u) * D, D)], hb[u][:, :]).then_inc(kept, 1)

        @block.scalar
        def _(act):
            with act.Fori(0, T // 2) as trip_no:
                t = trip_no * 2
                for u in range(2):
                    act.wait_ge(t_mm, t + u + 3)
                    act.wait_ge(l_mm, t + u + 1)
                    act.copy(h2T[u][:, :], p_t[u][:, :]).then_inc(t_ready, 1)
                    act.wait_ge(l_mm, t + u + 3)
                    act.activation(sc[:, ds((t + u) * E, E)], p_l[u][:, :], ACT.Exp, scale=-1.0).then_inc(l_used, 1)

        @block.vector
        def _(v):
            step = Chain(v, vec)

            def t3(tensor, n=E):
                return tensor[:, :].rearrange("p (t n) -> p t n", n=n)

            with v.Fori(0, T // 2) as trip_no:
                t = trip_no * 2
                step.enter(t, 2)
                for u in range(2):
                    v.wait_ge(t_mm, t + u + 1)
                    v.wait_ge(kept, t + u + 1)
                    step(v.tensor_scalar(hb[u][:, :], x[:, ds((t + u) * D, D)], mv[:, ds((t + u) * 2, 1)],
                                         rstd[:, ds(t + u, 1)], ALU.subtract, ALU.mult))
                    step(v.tensor_tensor(hb[u][:, :], hb[u][:, :], mod[:, 4 * D:5 * D], ALU.mult))
                    v.tensor_tensor(hb[u][:, :], hb[u][:, :], mod[:, 3 * D:4 * D], ALU.add).then_inc(h_ready, 1)
            step.leave(T, 2)
            v.wait_ge(l_used, T + 2)
            v.wait_ge(pads, 1)
            v.wait_ge(ld, 16 * (DK + 3))
            step(v.tensor_scalar(sc[:, :], sc[:, :], 1.0, None, ALU.add))
            step(v.reciprocal(sc[:, :], sc[:, :]))
            step(v.tensor_reduce(t3(gpad, PADG)[:, :, 0:GROUPS],
                                 sc[:, :].rearrange("p (t g n) -> p t g n", t=T, g=GROUPS), AX.X, ALU.max))
            for t in range(T):
                last = v.max(gtop[:, t * 8:(t + 1) * 8], gpad[:, t * PADG:t * PADG + 8])
            step(last)
            step(v.tensor_copy(t3(gkey, 8)[:, :, 0:2], t3(gtop, 8)[:, :, 0:2]))
            for t in range(T):
                last = v.match_replace(grep[:, t * PADG:(t + 1) * PADG], gkey[:, t * 8:(t + 1) * 8],
                                       gpad[:, t * PADG:(t + 1) * PADG], -5.0)
            step(last)
            step(v.tensor_scalar(t3(gmask, GROUPS), t3(grep, PADG)[:, :, 0:GROUPS], -5.0, None, ALU.is_equal))
            step(v.tensor_scalar(gpen[:, :], gmask[:, :], -1.0, None, ALU.add))
            by_group = lambda z: z.rearrange("p (t g n) -> p t g n", t=T, g=GROUPS)
            wide = lambda z: z[:, :].rearrange("p (t g n) -> p t g n", t=T, n=1).to_broadcast([P, T, GROUPS, EPG])
            step(v.tensor_tensor(by_group(tmp[:, :]), by_group(sc[:, :]), wide(gmask), ALU.mult))
            step(v.tensor_tensor(by_group(tmp[:, :]), by_group(tmp[:, :]), wide(gpen), ALU.add))
            step(v.tensor_copy(t3(epad, PADE)[:, :, 0:E], t3(tmp)))
            for t in range(T):
                last = v.max(etop[:, t * 8:(t + 1) * 8], epad[:, t * PADE:t * PADE + E])
            step(last)
            step(v.tensor_copy(t3(ekey, 8)[:, :, 0:TOPK], t3(etop, 8)[:, :, 0:TOPK]))
            for t in range(T):
                last = v.match_replace(erep[:, t * PADE:(t + 1) * PADE], ekey[:, t * 8:(t + 1) * 8],
                                       epad[:, t * PADE:(t + 1) * PADE], -5.0)
            step(last)
            v.tensor_scalar(t3(chosen), t3(erep, PADE)[:, :, 0:E], -5.0, None, ALU.is_equal).then_inc(chosen_ready, 1)
            v.wait_ge(chosen_ready, 1)
            with v.Fori(0, T) as t:
                step.enter(t, 1)
                step(v.tensor_tensor(before[:, ds((t + 1) * E, E)], before[:, ds(t * E, E)], chosen[:, ds(t * E, E)],
                                     ALU.add))
            step.leave(T)
            v.tensor_copy(first[:, :], before[:, T * E:(T + 1) * E]).then_inc(cum_ready, 1)
            step(v.tensor_tensor(wn[:, :], sc[:, :], chosen[:, :], ALU.mult))
            step(v.tensor_reduce(wsum[:, :], t3(wn), AX.X, ALU.add))
            step(v.reciprocal(wsum[:, :], wsum[:, :]))
            step(v.tensor_tensor(t3(wn), t3(wn), wsum[:, :].rearrange("p (t n) -> p t n", n=1).to_broadcast([P, T, E]),
                                 ALU.mult))
            v.wait_ge(pos_mm, 2)
            step(v.tensor_tensor(cmp[:, :].rearrange("p (e n) -> p e n", n=T),
                                 p_cnt[:, :].rearrange("p (e n) -> p e n", n=1).to_broadcast([P, E, T]),
                                 thresholds[:, :].rearrange("p (e n) -> p e n", e=1).to_broadcast([P, E, T]),
                                 ALU.is_gt))
            step(v.tensor_reduce(ntiles[:, :], cmp[:, :].rearrange("p (e n) -> p e n", n=T), AX.X, ALU.add))
            step(v.tensor_copy(scan[0][:, :], ntiles[:, :]))
            src = 0
            for d in (1, 2, 4, 8, 16):
                step(v.tensor_copy(scan[1 - src][:, 0:d], scan[src][:, 0:d]))
                step(v.tensor_tensor(scan[1 - src][:, d:E], scan[src][:, d:E], scan[src][:, 0:E - d], ALU.add))
                src = 1 - src
            ends = scan[src]
            step(v.tensor_tensor(first[:, :], ends[:, :], ntiles[:, :], ALU.subtract))
            step(v.tensor_scalar(first[:, :], first[:, :], float(P), 1.0, ALU.mult, ALU.add))
            step(v.tensor_tensor(t3(val), p_pos[:, :].rearrange("p (t n) -> p t n", n=E),
                                 first[:, :].rearrange("p (t n) -> p t n", t=1).to_broadcast([P, T, E]), ALU.add))
            step(v.tensor_tensor(val[:, :], val[:, :], chosen[:, :], ALU.mult))
            for t in range(T):
                last = v.max(vtop[:, t * 8:(t + 1) * 8], val[:, t * E:(t + 1) * E])
            step(last)
            step(v.tensor_scalar(t3(slot, 8)[:, :, 0:TOPK], t3(vtop, 8)[:, :, 0:TOPK], -1.0, None, ALU.add))
            step(v.tensor_scalar(t3(slot_out, 8)[:, :, 0:TOPK], t3(vtop, 8)[:, :, 0:TOPK], float(2 * S - 1), None,
                                 ALU.add))
            for j in range(TOPK):
                step(v.tensor_tensor(t3(tmp), t3(val), t3(vtop, 8)[:, :, j:j + 1].to_broadcast([P, T, E]),
                                     ALU.is_equal))
                step(v.tensor_tensor(tmp[:, :], tmp[:, :], wn[:, :], ALU.mult))
                step(v.tensor_reduce(t3(weight, 8)[:, :, j], t3(tmp), AX.X, ALU.add))
            te = texp[0:1, :].rearrange("p (t n) -> p t n", n=E)
            step(v.tensor_tensor(te, ends[0:1, :].rearrange("p (t n) -> p t n", t=1).to_broadcast([1, SLOT_TILES, E]),
                                 numbers[0:1, :].rearrange("p (t n) -> p t n", n=1).to_broadcast([1, SLOT_TILES, E]),
                                 ALU.is_le))
            step(v.tensor_reduce(tsum[0:1, 2 * T:TILES], te, AX.X, ALU.add))
            step(v.tensor_scalar(tsum[0:1, 2 * T:TILES], tsum[0:1, 2 * T:TILES], float(E - 1), None, ALU.min))
            step(v.tensor_copy(tile_expert[0:1, :], tsum[0:1, :]))

        @block.tensor
        def _(pe):
            for s in (t_mm, t_ready, l_mm, l_used, kept):
                pe.sem_inc(s, 2)
            pe.wait_ge(ld, 16 * (DK + 3))
            with pe.Fori(0, T // 2) as trip_no:
                t = trip_no * 2
                for u in range(2):
                    pe.wait_ge(h_ready, t + u + 1)
                    pe.wait_ge(t_ready, t + u + 1)
                    for k in range(DK):
                        last = pe.transpose(p_t[u][:, k * P:(k + 1) * P], hb[u][:, k * P:(k + 1) * P], ident[:, :])
                    last.then_inc(t_mm, 1)
                    pe.wait_ge(t_ready, t + u + 3)
                    pe.wait_ge(l_used, t + u + 1)
                    for k in range(DK):
                        last = pe.matmul(p_l[u][:, :], h2T[u][:, k * P:(k + 1) * P], gate[:, k * E:(k + 1) * E],
                                         start=(k == 0), stop=(k == DK - 1))
                    last.then_inc(l_mm, 1)
            pe.wait_ge(pads, 1)
            pe.wait_ge(chosen_ready, 1)
            pe.matmul(p_pos[:, :], lower[:, :], chosen[:, :], start=True, stop=False)
            pe.wait_ge(cum_ready, 1)
            pe.matmul(p_pos[:, :], ones[:, :], before[:, 0:T * E], start=False, stop=True).then_inc(pos_mm, 1)
            pe.matmul(p_cnt[:, :], ones[:, :], before[:, T * E:(T + 1) * E], start=True, stop=True).then_inc(pos_mm, 1)


def experts(nc, a, ident, hall, slot, tile_expert, slots_dram, done_dram):
    st = ExitStack()
    with st:
        def sb(name, cols, dt=F32, parts=P):
            return st.enter_context(nc.sbuf_tensor(name, [parts, cols], dt))

        def pb(name):
            return st.enter_context(nc.psum_tensor(name, [P, 512], F32))

        def sem(name):
            return st.enter_context(nc.semaphore(name))

        U = 8
        rows = [sb(f"rows{n}", D) for n in range(U)]
        w = [sb(f"w{n}", WIN + WOUT) for n in range(U)]
        rT = [sb("rT0", D), sb("rT1", D)]
        ex = [sb("ex0", M), sb("ex1", M)]
        hid = [sb("hid0", M), sb("hid1", M)]
        hidT = [sb("hidT0", 2 * P, parts=MH), sb("hidT1", 2 * P, parts=MH)]
        y = [sb(f"y{n}", D) for n in range(U)]
        ST = 4
        stage = [sb(f"stage{n}", D) for n in range(ST)]
        stage_slot = [sb(f"stage_slot{n}", 8, U32) for n in range(ST)]
        p_r = [pb("p_r0"), pb("p_r1")]
        p_g = [pb("p_g0"), pb("p_g1")]
        p_h = [pb("p_h0"), pb("p_h1")]
        p_y = [pb("p_d0"), pb("p_d1")]
        staged = sem("staged")
        issued = sem("issued")
        scattered = [sem(f"scattered{n}") for n in range(ST)]
        row_ld = [sem(f"row_ld{n}") for n in range(U)]
        w_ld = [sem(f"w_ld{n}") for n in range(U)]
        r_mm = sem("r_mm")
        r_used = sem("r_used")
        g_mm = sem("g_mm")
        silued = sem("silued")
        hid_ready = sem("hid_ready")
        h_mm = sem("h_mm")
        h_used = sem("h_used")
        y_mm = sem("y_mm4")
        y_ready = sem("y_ready")
        y_out = [sem(f"y_out{n}") for n in range(U)]
        block = st.enter_context(nc.Block())
        CREDIT = {r_mm: U, r_used: 2, g_mm: 2, hid_ready: 2, h_mm: 2, h_used: 2, y_mm: U, y_ready: 2}


        @block.gpsimd
        def _(gp):
            with gp.Fori(0, T // ST) as trip_no:
                for u in range(ST):
                    gp.wait_ge(staged, trip_no * ST + u + 1)
                    gp.sem_inc(issued, 1)
                    for j in range(TOPK):
                        gp.indirect_dma_start(
                            out=slots_dram[0:SLOT_TILES * P, :],
                            out_offset=bass.IndirectOffsetOnAxis(ap=stage_slot[u][:, j:j + 1], axis=0),
                            in_=stage[u][:, :], in_offset=None).then_inc(scattered[u], 16)

        @block.sync
        def _(sp):
            for s, n in CREDIT.items():
                sp.sem_inc(s, n)

            def load(i, u, row, weights=True):
                if weights:
                    e = sp.value_load(tile_expert[0:1, ds(i + u, 1)], min_val=0, max_val=E + 1)
                sp.wait_ge(r_mm, i + u + 1)
                sp.dma_start(rows[u][:, :], slots_dram[ds(row, P), :]).then_inc(row_ld[u], 16)
                sp.wait_ge(y_mm, i + u + 1)
                if not weights:
                    sp.sem_inc(w_ld[u], 16)
                    return
                sp.dma_start(w[u][:, :], a["experts"][ds(e, 1), :, :].rearrange("a p n -> (a p) n")).then_inc(w_ld[u], 16)

            def store(n, u):
                sp.wait_ge(y_ready, n + 3)
                sp.dma_start(done_dram[ds(n * P, P), :], y[u][:, :]).then_inc(y_out[u], 16)

            assert T == 2 * U
            for half in range(2):
                for group in range(2):
                    i = half * T + group * U
                    for u in range(U):
                        load(i, u, (group * U + u + SLOT_TILES) * P, weights=group == 0)
                        if i:
                            store(i + u - U, u)
            for s in scattered:
                sp.wait_ge(s, 16 * TOPK * T // ST)
            with sp.Fori(0, (TILES - 2 * T) // U) as trip_no:
                i = 2 * T + trip_no * U
                for u in range(U):
                    load(i, u, (i + u - 2 * T) * P)
                    store(i + u - U, u)
            for u in range(U):
                store(TILES - U + u, u)
            for s in y_out:
                sp.wait_ge(s, 16 * TILES // U + 16)

        @block.scalar
        def _(act):
            def copy_rows(n, u):
                act.wait_ge(r_mm, n + U + 1)
                act.wait_ge(g_mm, n + 1)
                act.copy(rT[u % 2][:, :], p_r[u % 2][:, 0:D]).then_inc(r_used, 1)

            def silu_gate(n, u):
                act.wait_ge(g_mm, n + 3)
                act.wait_ge(hid_ready, n + 1)
                act.activation(ex[u % 2][:, :], p_g[u % 2][:, 0:M], ACT.Silu).then_inc(silued, 1)

            def copy_hidden(n, u):
                act.wait_ge(h_mm, n + 3)
                act.wait_ge(y_mm, n + U - 1)
                act.copy(hidT[u % 2][:, :], p_h[u % 2][0:MH, 0:2 * P]).then_inc(h_used, 1)

            def trip(n, u, left=U):
                copy_hidden(n, u)
                if left >= 2:
                    silu_gate(n + 2, u + 2)
                if left >= 3:
                    copy_rows(n + 3, u + 3)

            act.preload_act_table(ACT.Silu)
            copy_rows(0, 0)
            for n in range(2):
                silu_gate(n, n)
                copy_rows(n + 1, n + 1)
            with act.Fori(0, (TILES - U) // U) as trip_no:
                i = trip_no * U
                for u in range(U):
                    trip(i + u, u)
            for u in range(U):
                trip(TILES - U + u, u, U - 1 - u)

        @block.vector
        def _(v):
            def silu(n, u):
                up = p_g[u % 2][:, M:2 * M]
                v.wait_ge(silued, n + 1)
                v.wait_ge(h_mm, n + 1)
                v.tensor_tensor(hid[u % 2][:, :], ex[u % 2][:, :], up, ALU.mult).then_inc(hid_ready, 1)

            def copy_y(n, u):
                v.wait_ge(y_mm, n + U + 1)
                v.wait_ge(y_out[u], (n - u) * (16 // U) + 16)
                v.tensor_copy(y[u][:, :], p_y[u % 2][:, 0:D]).then_inc(y_ready, 1)

            for s in y_out:
                v.sem_inc(s, 16)
            for n in range(2):
                silu(n, n)
            def stage_tile(t, u, again):
                if again:
                    v.wait_ge(scattered[u], t * (16 * TOPK // ST))
                v.tensor_copy(stage[u][:, :], hall[:, ds((t + u) * D, D)])
                v.tensor_copy(stage_slot[u][:, 0:TOPK], slot[:, ds((t + u) * 8, TOPK)]).then_inc(staged, 1)

            def shared_tiles(i, t, again=True):
                for u in range(U):
                    if u in (0, 1, 3, 5):
                        stage_tile(t, (u + 1) // 2, again)
                    silu(i + u + 2, u + 2)
                    copy_y(i + u, u)

            shared_tiles(0, 0, again=False)
            with v.Fori(1, T // ST) as trip_no:
                shared_tiles(trip_no * U, trip_no * ST)
            with v.Fori(T // ST, (TILES - U) // U) as trip_no:
                i = trip_no * U
                for u in range(U):
                    silu(i + u + 2, u + 2)
                    copy_y(i + u, u)
            for u in range(U):
                if u < U - 2:
                    silu(TILES - U + u + 2, u + 2)
                copy_y(TILES - U + u, u)

        @block.tensor
        def _(pe):
            def turn_rows(n, u, ring):
                pe.wait_ge(row_ld[u % U], ring)
                pe.wait_ge(r_used, n + 1)
                for k in range(DK):
                    last = pe.transpose(p_r[u % 2][:, k * P:(k + 1) * P], rows[u % U][:, k * P:(k + 1) * P], ident[:, :])
                last.then_inc(r_mm, 1)

            def gate_up(n, u, ring):
                pe.wait_ge(r_used, n + 3)
                pe.wait_ge(w_ld[u % U], ring)
                pe.wait_ge(hid_ready, n + 1)
                for k in range(DK):
                    last = pe.matmul(p_g[u % 2][:, 0:2 * M], rT[u % 2][:, k * P:(k + 1) * P],
                                     w[u % U][:, k * 2 * M:(k + 1) * 2 * M], start=(k == 0), stop=(k == DK - 1))
                last.then_inc(g_mm, 1)

            def turn_hidden(n, u):
                pe.wait_ge(hid_ready, n + 3)
                pe.wait_ge(h_used, n + 1)
                for k in range(2):
                    last = pe.transpose(p_h[u % 2][0:MH, k * P:(k + 1) * P], hid[u % 2][:, k * MH:(k + 1) * MH], ident[:, :])
                last.then_inc(h_mm, 1)

            def down(n, u):
                pe.wait_ge(h_used, n + 3)
                pe.wait_ge(y_ready, n + 1)
                for k in range(2):
                    last = pe.matmul(p_y[u % 2][:, 0:D], hidT[u % 2][:, k * P:(k + 1) * P],
                                     w[u % U][0:MH, WIN + k * D:WIN + (k + 1) * D], start=(k == 0), stop=(k == 1))
                last.then_inc(y_mm, 1)

            def trip(i, u, ring, left=U):
                n = i + u
                turn_hidden(n, u)
                if left >= 2:
                    gate_up(n + 2, u + 2, ring + (16 if u + 2 >= U else 0))
                if left >= 3:
                    turn_rows(n + 3, u + 3, ring + (16 if u + 3 >= U else 0))
                down(n, u)

            turn_rows(0, 0, 16)
            for n in range(2):
                gate_up(n, n, 16)
                turn_rows(n + 1, n + 1, 16)
            with pe.Fori(0, (TILES - U) // U) as trip_no:
                i = trip_no * U
                for u in range(U):
                    trip(i, u, i * (16 // U) + 16)
            for u in range(U):
                trip(TILES - U, u, 16 * (TILES // U), U - 1 - u)


def combine(nc, x, mod, weight, slot_out, done_dram, out):
    st = ExitStack()
    with st:
        def sb(name, cols, dt=F32):
            return st.enter_context(nc.sbuf_tensor(name, [P, cols], dt))

        def sem(name):
            return st.enter_context(nc.semaphore(name))

        PARTS = TOPK + 2
        got = [sb("got0", PARTS * D), sb("got1", PARTS * D)]
        slot_now = [sb("slot_now0", 8, U32), sb("slot_now1", 8, U32)]
        acc = [sb("acc0", D), sb("acc1", D)]
        slot_ready = sem("slot_ready")
        issued = sem("issued5")
        gathered = [sem("gathered0"), sem("gathered1")]
        shared = [sem("shared0"), sem("shared1")]
        used = sem("used5")
        done = sem("done5")
        written = [sem("written0"), sem("written1")]
        vec = sem("vec5")
        block = st.enter_context(nc.Block())

        @block.gpsimd
        def _(gp):
            with gp.Fori(0, T // 2) as trip_no:
                t = trip_no * 2
                for u in range(2):
                    gp.wait_ge(used, t + u + 1)
                    gp.tensor_copy(slot_now[u][:, 0:TOPK], slot_out[:, ds((t + u) * 8, TOPK)]).then_inc(slot_ready, 1)
                    gp.wait_ge(slot_ready, t + u + 1)
                    gp.sem_inc(issued, 1)
                    for j in range(TOPK):
                        gp.indirect_dma_start(
                            out=got[u][:, j * D:(j + 1) * D], out_offset=None,
                            in_=done_dram,
                            in_offset=bass.IndirectOffsetOnAxis(ap=slot_now[u][:, j:j + 1], axis=0)
                        ).then_inc(gathered[u], 16)

        @block.sync
        def _(sp):
            sp.sem_inc(used, 2)
            for s in written:
                sp.sem_inc(s, 16)
            with sp.Fori(0, T // 2) as trip_no:
                t = trip_no * 2
                for u in range(2):
                    sp.wait_ge(used, t + u + 1)
                    for part in range(2):
                        sp.dma_start(got[u][:, (TOPK + part) * D:(TOPK + part + 1) * D],
                                     done_dram[ds((t + u + T * part) * P, P), :]).then_inc(shared[u], 16)

        @block.scalar
        def _(act):
            with act.Fori(0, T // 2) as trip_no:
                t = trip_no * 2
                for u in range(2):
                    act.wait_ge(done, t + u + 1)
                    act.dma_start(out[ds((t + u) * P, P), :], acc[u][:, :]).then_inc(written[u], 16)
            for s in written:
                act.wait_ge(s, 16 * T // 2 + 16)

        @block.vector
        def _(v):
            step = Chain(v, vec)
            with v.Fori(0, T // 2) as trip_no:
                t = trip_no * 2
                step.enter(t, TOPK + 1)
                for u in range(2):
                    g = got[u]
                    v.wait_ge(shared[u], 16 * t + 32)
                    v.wait_ge(gathered[u], 16 * TOPK // 2 * t + 16 * TOPK)
                    v.wait_ge(written[u], 8 * t + 16)
                    step(v.tensor_tensor(acc[u][:, :], g[:, TOPK * D:(TOPK + 1) * D], g[:, (TOPK + 1) * D:PARTS * D],
                                         ALU.add))
                    for j in range(TOPK):
                        ins = v.scalar_tensor_tensor(out=acc[u][:, :], in0=g[:, j * D:(j + 1) * D],
                                                     scalar=weight[:, ds((t + u) * 8 + j, 1)], in1=acc[u][:, :],
                                                     op0=ALU.mult, op1=ALU.add)
                        if j < TOPK - 1:
                            step(ins)
                        else:
                            ins.then_inc(used, 1)
                            v.wait_ge(used, t + u + 3)
                    step(v.tensor_tensor(acc[u][:, :], acc[u][:, :], mod[:, 5 * D:6 * D], ALU.mult))
                    v.tensor_tensor(acc[u][:, :], acc[u][:, :], x[:, ds((t + u) * D, D)], ALU.add).then_inc(done, 1)
            step.leave(T, 2)


def kernel(**inputs):
    import concourse.bacc as bacc
    from concourse.bass_utils import run_bass_kernel_spmd

    given = {n: np.asarray(v) for n, v in inputs.items()}
    f32 = np.float32
    pairs = np.concatenate([np.arange(0, ROPE, 2), np.arange(1, ROPE, 2)])
    qb = given["L0_attn_q_b_w"].reshape(H, QK, QR)
    qb = np.concatenate([qb[:, QK - ROPE:][:, pairs], qb[:, :QK - ROPE]], axis=1)
    kva = given["L0_attn_kv_a_w"]
    kva = np.concatenate([kva[C:][pairs], kva[:C]], axis=0)
    kvb = given["L0_attn_kv_b_w"].reshape(H, QK - ROPE + V, C)
    lnq = np.zeros((RT * P,), f32)
    lnq[:QR] = given["L0_attn_q_a_ln"]
    inv = (f32(1.0) / (f32(128000.0) ** (np.arange(0, ROPE, 2, dtype=f32) / f32(ROPE)))).astype(f32)
    angle = (inv[:, None] * np.arange(S, dtype=f32)[None, :]).astype(f32).astype(np.float64)
    cos, sin = np.cos(angle).astype(f32), np.sin(angle).astype(f32)
    sw_gate, sw_up, sw_down = (given[f"L0_ffn_sw_{n}"] for n in ("gate", "up", "down"))
    w_in = np.concatenate([given["L0_ffn_w_gate"], given["L0_ffn_w_up"]], axis=2)
    shared_in = np.stack([np.concatenate([sw_gate[:, i * M:(i + 1) * M], sw_up[:, i * M:(i + 1) * M]], axis=1)
                          for i in range(2)])
    w_in = np.concatenate([w_in, shared_in]).reshape(E + 2, DK, P, 2 * M).transpose(0, 2, 1, 3).reshape(E + 2, P, WIN)
    w_down = np.concatenate([given["L0_ffn_w_down"], sw_down.reshape(2, M, D)])
    w_out = np.zeros((E + 2, P, WOUT), f32)
    w_out[:, :MH] = w_down.reshape(E + 2, 2, MH, D).transpose(0, 2, 1, 3).reshape(E + 2, MH, WOUT)
    arrays = {
        "x": given["L0_attn_x"].reshape(S, D),
        "c": given["L0_c"].reshape(DK, P).T,
        "wmod": given["L0_wmod"],
        "wqaT": given["L0_attn_q_a_w"].T,
        "wqa": given["L0_attn_q_a_w"],
        "lnq": lnq.reshape(RT, P).T,
        "wqb": qb.transpose(1, 0, 2).reshape(P, H * QR),
        "wkvT": kva.T,
        "lnkv": np.broadcast_to(given["L0_attn_kv_a_ln"], (P, C)),
        "wk": kvb[:, :QK - ROPE].transpose(1, 0, 2).reshape(QK - ROPE, H * C),
        "wv": kvb[:, QK - ROPE:].transpose(1, 0, 2).reshape(V, H * C),
        "woT": given["L0_attn_o_w"].T.reshape(H, V, D).transpose(1, 0, 2).reshape(V, H * D),
        "cos": np.concatenate([cos, cos]),
        "sin": np.concatenate([sin, -sin]),
        "gate": given["L0_ffn_gate_w"],
        "experts": np.concatenate([w_in, w_out], axis=2),
        "lower": np.triu(np.ones((P, P), f32), 1),
        "thresholds": np.broadcast_to(np.arange(T, dtype=f32) * P, (P, T)),
        "numbers": np.broadcast_to(np.arange(SLOT_TILES, dtype=f32), (P, SLOT_TILES)),
    }
    nc = bacc.Bacc("TRN2", target_bir_lowering=False, num_devices=1)
    feed, aps = {}, {}
    for name, array in arrays.items():
        array = np.ascontiguousarray(array)
        feed[f"in_{name}"] = array
        aps[name] = nc.dram_tensor(f"in_{name}", array.shape, mybir.dt.from_np(array.dtype), kind="ExternalInput").ap()
    out = nc.dram_tensor("out", [S, D], F32, kind="ExternalOutput").ap()
    program(nc, aps, out)
    result = run_bass_kernel_spmd(nc, [feed], core_ids=[0])
    return result.results[0]["out"].reshape(1, S, D)
```

```python
from contextlib import ExitStack

import numpy as np

import concourse.bass as bass
from concourse import mybir

F32 = mybir.dt.float32
F32R = mybir.dt.float32r
F16 = mybir.dt.float16
I32 = mybir.dt.int32
U32 = mybir.dt.uint32
ALU = mybir.AluOpType
ACT = mybir.ActivationFunctionType
AX = mybir.AxisListType
ds = bass.ds

P = 128
S = 2048
D = 256
T = S // P
DK = D // P
H = 16
ROPE = 64
HALF = ROPE // 2
C = 32
QK = 128
V = 128
KA = ROPE + C
KS = KA + 1
QR = 682
RT = -(-QR // P)
RL = QR - (RT - 1) * P
HC = H * C
QC = 512
E = 32
TOPK = 6
GROUPS = 4
EPG = E // GROUPS
M = 176
MH = M // 2
RW = D + 1
WIN = DK * 2 * M
WOUT = 2 * D
SLOT_TILES = S * TOPK // P + E
TILES = SLOT_TILES + 2 * T
STEPS_V = 4 * 4 + 2
SCALE = float(1.0 / np.sqrt(np.float32(QK)))
STEPS = 32
P_SCALE = 2.0 ** 14
C_SCALE = 16.0
CP = 64


class Chain:

    def __init__(self, engine, semaphore):
        self.engine, self.semaphore, self.before, self.now = engine, semaphore, 0, 0

    def __call__(self, instruction):
        instruction.then_inc(self.semaphore, 1)
        self.now += 1
        self.engine.wait_ge(self.semaphore, self.before + self.now)

    def enter(self, i, each):
        self.start, self.each = self.before + self.now, each
        self.before, self.now = self.start + i * each, 0

    def leave(self, end, unit=1):
        assert self.now == self.each * unit, (self.now, self.each, unit)
        self.before, self.now = self.start + end * self.each, 0


def program(nc, a, out):
    top = ExitStack()
    with top:
        def sb(stack, name, cols, dt=F32, parts=P):
            return stack.enter_context(nc.sbuf_tensor(name, [parts, cols], dt))

        x = sb(top, "x", T * D)
        ident = sb(top, "ident", P)
        ones = sb(top, "ones", P)
        mod = sb(top, "mod", 6 * D)
        wov = sb(top, "wov", 4 * D)
        cbar = sb(top, "cbar", T * HC)
        slots_dram = nc.dram_tensor("expert_rows", [SLOT_TILES * P + S, RW], F32, kind="Internal").ap()
        ranked_dram = nc.dram_tensor("ranked_out", [SLOT_TILES * P + TOPK * S, D], F32, kind="Internal").ap()
        shared_dram = nc.dram_tensor("shared_out", [2 * S, D], F32, kind="Internal").ap()

        att = ExitStack()
        with att:
            hT = sb(att, "hT", DK * S)
            weff = sb(att, "weff", DK * H * KA)
            caug = sb(att, "caug", T * CP)
            cosq = sb(att, "cosq", S)
            sinq = sb(att, "sinq", S)
            k_hi = sb(att, "k_hi", S, F32R)
            k_lo = sb(att, "k_lo", S, F32R)
            mods_and_weights(nc, a, x, ident, ones, mod, wov, hT, weff, caug, cosq, sinq, k_hi, k_lo, cbar)
            attention(nc, hT, weff, caug, cosq, sinq, k_hi, k_lo, ident, slots_dram, cbar)
        ffn(nc, a, x, ident, mod, wov, cbar, slots_dram, ranked_dram, shared_dram, out)


def mods_and_weights(nc, a, x, ident, ones, mod, wov, hT, weff, caug, cosq, sinq, k_hi, k_lo, cbar):
    st = ExitStack()
    with st:
        def sb(name, cols, dt=F32):
            return st.enter_context(nc.sbuf_tensor(name, [P, cols], dt))

        def pb(name, banks=1):
            return st.enter_context(nc.psum_tensor(name, [P, 512 * banks], F32))

        def sem(name):
            return st.enter_context(nc.semaphore(name))

        ccol = sb("ccol", 3 * DK)
        cwide = sb("cwide", DK * P)
        gate_sign = sb("gate_sign", D)
        wqaT = sb("wqaT", DK * QR)
        wqa = sb("wqa", RT * D)
        lnq = sb("lnq", RT)
        wkvT = sb("wkvT", DK * KA)
        lnkv = sb("lnkv", C)
        fold = sb("fold", H * KA)
        wv = cbar[:, H * D:H * D + H * C]
        woT = cbar[:, 0:H * D]
        wqb = sb("wqb", 2 * QR)
        afold = sb("afold", RT * H * KA)
        wmod = afold[:, 0:DK * 6 * D]
        hbuf = sb("hbuf", 2 * D)
        hTb = sb("hTb", 2 * D)
        stats = sb("stats", T * 6)
        mv = sb("mv", T * 2)
        rstd = sb("rstd", T)
        ckv = cbar[:, 5120:5120 + T * KA]
        junk = sb("junk", 512)
        ssq = sb("ssq", T * 3)
        rq = sb("rq", T)
        rc = sb("rc", T)
        tmp16 = sb("tmp16", T * 4)
        kbuf = sb("kbuf", 4 * KA)
        rot_a = sb("rot_a", QC)
        rot_b = sb("rot_b", QC)
        kraw = sb("kraw", QC)

        pw = [pb("pw0", 2), pb("pw1", 2)]
        pt = [pb("pt0"), pb("pt1")]
        pk = [pb("pk0"), pb("pk1")]

        ld_x = sem("ld_x")
        ld_mod = sem("ld_mod")
        ld_w = sem("ld_w")
        ld_qb = [sem("ld_qb0"), sem("ld_qb1")]
        consts = sem("consts")
        exp_c = sem("exp_c")
        silu_c = sem("silu_c")
        mod_mm = sem("mod_mm")
        mod_used = sem("mod_used")
        dve = sem("dve")
        pool = sem("pool")
        var_ready = sem("var_ready")
        stats_ready = sem("stats_ready")
        rstd_ready = sem("rstd_ready")
        h_ready = sem("h_ready")
        ht_mm = sem("ht_mm")
        ht_ready = sem("ht_ready")
        kv_mm = sem("kv_mm")
        kv_ready = sem("kv_ready")
        squares_ready = sem("squares_ready")
        sums_ready = sem("sums_ready")
        roots_ready = sem("roots_ready")
        k_ready = sem("k_ready")
        k_mm = sem("k_mm")
        k_used = sem("k_used")
        diag_ready = sem("diag_ready")
        rq_mm = sem("rq_mm")
        rq_used = sem("rq_used")
        fold_ready = sem("fold_ready")
        a_mm = sem("a_mm")
        a_used = sem("a_used")
        w_mm = sem("w_mm")
        w_used = sem("w_used")
        ov_mm = sem("ov_mm")
        ov_used = sem("ov_used")

        block = st.enter_context(nc.Block())

        NLW = 9

        @block.sync
        def _(sp):
            sp.sem_inc(a_mm, 2)
            sp.dma_start(ccol[:, 0:DK], a["c"]).then_inc(ld_mod, 16)
            sp.dma_start(x[:, :].rearrange("p (t d) -> p t d", t=T),
                         a["x"].rearrange("(t p) d -> p t d", p=P)).then_inc(ld_x, 16)
            sp.dma_start(wmod.rearrange("p (k n) -> p k n", k=DK),
                         a["wmod"].rearrange("(k p) n -> p k n", p=P)).then_inc(ld_mod, 16)
            sp.dma_start(wqaT[:, :].rearrange("p (k n) -> p k n", k=DK),
                         a["wqaT"].rearrange("(k p) n -> p k n", p=P)).then_inc(ld_w, 16)
            sp.dma_start(wkvT[:, :].rearrange("p (k n) -> p k n", k=DK),
                         a["wkvT"].rearrange("(k p) n -> p k n", p=P)).then_inc(ld_w, 16)
            sp.dma_start(lnkv[:, :], a["lnkv"]).then_inc(ld_w, 16)
            sp.dma_start(cosq[0:ROPE, :], a["cos"]).then_inc(ld_w, 16)
            sp.dma_start(sinq[0:ROPE, :], a["sin"]).then_inc(ld_w, 16)
            sp.dma_start(wqa[:, 0:(RT - 1) * D].rearrange("p (k n) -> p k n", n=D),
                         a["wqa"][0:(RT - 1) * P, :].rearrange("(k p) n -> p k n", p=P)).then_inc(ld_w, 16)
            sp.dma_start(wqa[0:RL, (RT - 1) * D:RT * D], a["wqa"][(RT - 1) * P:QR, :]).then_inc(ld_w, 16)
            sp.dma_start(lnq[:, :], a["lnq"]).then_inc(ld_w, 16)
            sp.dma_start(woT, a["woT"]).then_inc(ld_w, 16)
            sp.dma_start(wv, a["wv"]).then_inc(fold_ready, 16)
            sp.wait_ge(consts, 4)
            sp.dma_start(fold[ROPE:P, :].rearrange("p (h n) -> p h n", h=H)[:, :, ROPE:KA],
                         a["wk"].rearrange("p (h n) -> p h n", h=H)).then_inc(fold_ready, 16)
            with sp.Fori(0, H // 2) as trip_no:
                h = trip_no * 2
                for u in range(2):
                    sp.wait_ge(a_mm, h + u + 1)
                    sp.dma_start(wqb[:, u * QR:(u + 1) * QR],
                                 a["wqb"][:, ds((h + u) * QR, QR)]).then_inc(ld_qb[u], 16)

        @block.gpsimd
        def _(gp):
            step = Chain(gp, pool)
            step(gp.memset(ident[:, :], 0.0))
            step(gp.affine_select(out=ident[:, :], in_=ident[:, :], compare_op=ALU.not_equal, fill=1.0,
                                  base=0, pattern=[[-1, P]], channel_multiplier=1))
            step(gp.memset(ones[:, :], 1.0))
            step(gp.memset(k_hi[KA:KS, :].bitcast(F32), 1.0))
            step(gp.memset(k_lo[KA:KS, :].bitcast(F32), 0.0))
            step(gp.memset(fold[:, :], 0.0))
            step(gp.memset(caug[:, :], 0.0))
            step(gp.memset(caug[:, :].rearrange("p (t n) -> p t n", t=T)[:, :, C:C + 1], 1.0))
            step(gp.tensor_copy(fold[0:ROPE, :].rearrange("p (h n) -> p h n", h=H)[:, :, 0:ROPE],
                                ident[0:ROPE, 0:ROPE].rearrange("p (h n) -> p h n", h=1).to_broadcast([ROPE, H, ROPE])))
            gp.sem_inc(consts, 4)

        @block.scalar
        def _(act):
            act.wait_ge(ld_mod, 32)
            act.activation(ccol[:, DK:2 * DK], ccol[:, 0:DK], ACT.Exp, scale=-1.0).then_inc(exp_c, 1)
            act.wait_ge(var_ready, 1)
            act.activation(rstd[:, :], tmp16[:, 0:T], ACT.Sqrt).then_inc(rstd_ready, 1)
            def keep_turned(n, u):
                act.wait_ge(ht_mm, n + 3)
                act.wait_ge(kv_mm, n + 1)
                act.copy(hTb[:, u * D:(u + 1) * D], pt[u][:, 0:D]).then_inc(ht_ready, 1)
                act.copy(hT[:, :].rearrange("p (k s) -> p k s", k=DK)[:, :, ds(n * P, P)],
                         pt[u][:, 0:D].rearrange("p (k s) -> p k s", k=DK)).then_inc(ht_ready, 1)

            def squares(n, u):
                act.wait_ge(kv_mm, n + 3)
                for c in range(2):
                    act.activation(pw[u][:, c * 512:c * 512 + 341], pw[u][:, c * 512:c * 512 + 341], ACT.Square,
                                   accum_out=ssq[:, ds(n * 3 + c, 1)])
                act.wait_ge(kv_ready, n + 3)
                act.activation(junk[:, ds(n * C, C)], ckv[:, ds(n * KA + ROPE, C)], ACT.Square,
                               accum_out=ssq[:, ds(n * 3 + 2, 1)]).then_inc(squares_ready, 1)

            keep_turned(0, 0)
            with act.Fori(0, T // 2 - 1) as trip_no:
                t = trip_no * 2
                for u in range(2):
                    keep_turned(t + u + 1, 1 - u)
                    squares(t + u, u)
            keep_turned(T - 1, 1)
            for u in range(2):
                squares(T - 2 + u, u)
            act.wait_ge(sums_ready, 2)
            act.activation(rq[:, :], tmp16[:, 0:T], ACT.Sqrt).then_inc(roots_ready, 1)
            act.activation(rc[:, :], tmp16[:, T:2 * T], ACT.Sqrt).then_inc(roots_ready, 1)
            with act.Fori(0, H // 2) as trip_no:
                h = trip_no * 2
                for u in range(2):
                    act.wait_ge(a_mm, h + u + 3)
                    for r in range(RT):
                        n = P if r < RT - 1 else RL
                        src = pw[u][0:n, (r // 3) * 512 + (r % 3) * KA:(r // 3) * 512 + (r % 3 + 1) * KA]
                        last = act.activation(afold[0:n, ds((h + u) * KA + r * H * KA, KA)], src, ACT.Copy,
                                              scale=lnq[0:n, r:r + 1])
                    last.then_inc(a_used, 1)
            for c in range(3):
                for k in range(DK):
                    n = c * DK + k
                    act.wait_ge(w_mm, n + 1)
                    act.copy(weff[:, k * H * KA + c * 512:k * H * KA + (c + 1) * 512],
                             pw[n % 2][:, 0:512]).then_inc(w_used, 1)
            for g in range(4):
                act.wait_ge(ov_mm, g + 1)
                act.copy(wov[:, g * D:(g + 1) * D], pk[g % 2][:, 0:D]).then_inc(ov_used, 1)

        @block.vector
        def _(v):
            step = Chain(v, dve)
            v.wait_ge(exp_c, 1)
            v.wait_ge(consts, 4)
            step(v.tensor_scalar(ccol[:, DK:2 * DK], ccol[:, DK:2 * DK], 1.0, None, ALU.add))
            step(v.reciprocal(ccol[:, 2 * DK:3 * DK], ccol[:, DK:2 * DK]))
            step(v.tensor_tensor(ccol[:, 2 * DK:3 * DK], ccol[:, 2 * DK:3 * DK], ccol[:, 0:DK], ALU.mult))
            for k in range(DK):
                v.tensor_scalar(cwide[:, k * P:(k + 1) * P], ones[:, :], ccol[:, 2 * DK + k:2 * DK + k + 1], None,
                                ALU.mult).then_inc(silu_c, 1)
            v.wait_ge(ld_x, 16)
            with v.Fori(0, T) as t:
                v.bn_stats(stats[:, ds(t * 6, 6)], x[:, ds(t * D, D)]).then_inc(stats_ready, 1)
            v.wait_ge(stats_ready, T)
            for t in range(T):
                last = v.bn_aggr(mv[:, t * 2:(t + 1) * 2], stats[:, t * 6:(t + 1) * 6])
            step(last)
            var = mv[:, :].rearrange("p (t n) -> p t n", n=2)[:, :, 1]
            v.tensor_scalar(tmp16[:, 0:T], var, 1e-5, None, ALU.add).then_inc(var_ready, 1)
            for c in range(3):
                v.wait_ge(mod_mm, c + 1)
                v.tensor_copy(mod[:, c * 512:(c + 1) * 512], pw[c % 2][:, 0:512]).then_inc(mod_used, 1)
            v.wait_ge(mod_used, 3)
            for part in (1, 4):
                step(v.tensor_scalar(mod[:, part * D:(part + 1) * D], mod[:, part * D:(part + 1) * D], 1.0, None,
                                     ALU.add))
            for part in (2, 5):
                g = mod[:, part * D:(part + 1) * D]
                step(v.tensor_scalar(gate_sign[:, :], g, 0.0, 2.0, ALU.is_ge, ALU.mult))
                step(v.tensor_scalar(gate_sign[:, :], gate_sign[:, :], -1.0, None, ALU.add))
                step(v.tensor_tensor(g, g, gate_sign[:, :], ALU.mult))
                step(v.scalar_tensor_tensor(out=g, in0=g, scalar=0.25, in1=gate_sign[:, :], op0=ALU.max,
                                            op1=ALU.mult))
            v.wait_ge(rstd_ready, 1)
            step(v.reciprocal(rstd[:, :], rstd[:, :]))
            def norm(n, u):
                hb = hbuf[:, u * D:(u + 1) * D]
                v.wait_ge(ht_mm, n + 1)
                step(v.tensor_scalar(hb, x[:, ds(n * D, D)], mv[:, ds(n * 2, 1)], rstd[:, ds(n, 1)],
                                     ALU.subtract, ALU.mult))
                step(v.tensor_tensor(hb, hb, mod[:, D:2 * D], ALU.mult))
                v.tensor_tensor(hb, hb, mod[:, 0:D], ALU.add).then_inc(h_ready, 1)

            def keep_latent(n, u):
                v.wait_ge(kv_mm, n + 3)
                v.tensor_copy(ckv[:, ds(n * KA, KA)], pk[u][:, 0:KA]).then_inc(kv_ready, 1)

            for u in range(2):
                norm(u, u)
            with v.Fori(0, T // 2 - 1) as trip_no:
                t = trip_no * 2
                step.enter(t, 2)
                for u in range(2):
                    norm(t + u + 2, u)
                    keep_latent(t + u, u)
            step.leave(T - 2, 2)
            for u in range(2):
                keep_latent(T - 2 + u, u)
            v.wait_ge(squares_ready, T + 2)
            s3 = ssq[:, :].rearrange("p (t n) -> p t n", n=3)
            step(v.tensor_tensor(tmp16[:, 0:T], s3[:, :, 0], s3[:, :, 1], ALU.add))
            v.tensor_scalar(tmp16[:, 0:T], tmp16[:, 0:T], 1.0 / QR, 1e-6, ALU.mult, ALU.add).then_inc(sums_ready, 1)
            v.tensor_scalar(tmp16[:, T:2 * T], s3[:, :, 2], 1.0 / C, 1e-6, ALU.mult, ALU.add).then_inc(sums_ready, 1)
            v.wait_ge(roots_ready, 2)
            step(v.reciprocal(rq[:, :], rq[:, :]))
            step(v.reciprocal(rc[:, :], rc[:, :]))
            v.wait_ge(ld_w, 16 * NLW)
            v.wait_ge(kv_ready, T + 2)
            with v.Fori(0, T // 4) as q:
                step.enter(q, 6)
                for j in range(4):
                    t = q * 4 + j
                    if j == 0:
                        v.wait_ge(k_used, q + 1)
                    v.tensor_copy(kbuf[:, j * KA:j * KA + ROPE], ckv[:, ds(t * KA, ROPE)]).then_inc(k_ready, 1)
                    v.scalar_tensor_tensor(out=kbuf[:, j * KA + ROPE:(j + 1) * KA], in0=ckv[:, ds(t * KA + ROPE, C)],
                                           scalar=rc[:, ds(t, 1)], in1=lnkv[:, :], op0=ALU.mult,
                                           op1=ALU.mult).then_inc(k_ready, 1)
                    v.scalar_tensor_tensor(out=caug[:, ds(t * CP, C)], in0=ckv[:, ds(t * KA + ROPE, C)],
                                           scalar=rc[:, ds(t, 1)], in1=lnkv[:, :], op0=ALU.mult,
                                           op1=ALU.mult).then_inc(k_ready, 1)
                v.wait_ge(k_mm, q + 1)
                step(v.tensor_tensor(rot_a[0:ROPE, :], pk[0][0:ROPE, :], cosq[0:ROPE, ds(q * QC, QC)], ALU.mult))
                step(v.tensor_tensor(rot_b[HALF:ROPE, :], pk[0][0:HALF, :], sinq[0:HALF, ds(q * QC, QC)], ALU.mult))
                step(v.tensor_tensor(rot_b[0:HALF, :], pk[0][HALF:ROPE, :], sinq[HALF:ROPE, ds(q * QC, QC)], ALU.mult))
                step(v.tensor_tensor(kraw[0:ROPE, :], rot_a[0:ROPE, :], rot_b[0:ROPE, :], ALU.add))
                step(v.tensor_copy(kraw[ROPE:KA, :], pk[0][ROPE:KA, :]))
                step(v.tensor_copy(k_hi[0:KA, ds(q * QC, QC)], kraw[0:KA, :]))
                v.tensor_tensor(k_lo[0:KA, ds(q * QC, QC)], kraw[0:KA, :],
                                k_hi[0:KA, ds(q * QC, QC)].bitcast(F32), ALU.subtract).then_inc(k_used, 1)
                v.wait_ge(k_used, q + 2)
            step.leave(T // 4)
            diag = (rot_a, rot_b)

            def spread(g):
                for j in range(4):
                    last = v.tensor_scalar(diag[g % 2][:, j * P:(j + 1) * P], ident[:, :],
                                           rq[:, 4 * g + j:4 * g + j + 1], None, ALU.mult)
                last.then_inc(diag_ready, 1)

            for g in range(2):
                spread(g)
            for g in range(T // 4):
                v.wait_ge(rq_mm, g + 1)
                tok = slice(g * QC, (g + 1) * QC)
                v.tensor_tensor(cosq[0:ROPE, tok], cosq[0:ROPE, tok], pt[g % 2][0:ROPE, :], ALU.mult)
                v.tensor_tensor(sinq[0:ROPE, tok], sinq[0:ROPE, tok], pt[g % 2][0:ROPE, :], ALU.mult)
                v.tensor_copy(cosq[ROPE:KA, tok], pt[g % 2][ROPE:KA, :]).then_inc(rq_used, 1)
                if g + 2 < T // 4:
                    spread(g + 2)

        @block.tensor
        def _(pe):
            pe.wait_ge(silu_c, DK)
            for c in range(3):
                if c == 2:
                    pe.wait_ge(mod_used, 1)
                for k in range(DK):
                    last = pe.matmul(pw[c % 2][:, 0:512], cwide[:, k * P:(k + 1) * P],
                                     wmod[:, k * 6 * D + c * 512:k * 6 * D + (c + 1) * 512],
                                     start=(k == 0), stop=(k == DK - 1))
                last.then_inc(mod_mm, 1)
            pe.wait_ge(mod_used, 3)
            pe.wait_ge(ld_w, 16 * NLW)
            for s in (ht_mm, kv_mm, squares_ready, kv_ready):
                pe.sem_inc(s, 2)
            def turn(n, u):
                pe.wait_ge(h_ready, n + 1)
                for k in range(DK):
                    last = pe.transpose(pt[u][:, k * P:(k + 1) * P], hbuf[:, u * D + k * P:u * D + (k + 1) * P],
                                        ident[:, :])
                last.then_inc(ht_mm, 1)

            def latents(n, u):
                pe.wait_ge(ht_ready, 2 * n + 2)
                pe.wait_ge(squares_ready, n + 1)
                pe.wait_ge(kv_ready, n + 1)
                for c in range(2):
                    for k in range(DK):
                        pe.matmul(pw[u][:, c * 512:c * 512 + 341], hTb[:, u * D + k * P:u * D + (k + 1) * P],
                                  wqaT[:, k * QR + c * 341:k * QR + (c + 1) * 341], start=(k == 0), stop=(k == DK - 1))
                for k in range(DK):
                    last = pe.matmul(pk[u][:, 0:KA], hTb[:, u * D + k * P:u * D + (k + 1) * P],
                                     wkvT[:, k * KA:(k + 1) * KA], start=(k == 0), stop=(k == DK - 1))
                last.then_inc(kv_mm, 1)

            turn(0, 0)
            with pe.Fori(0, T // 2 - 1) as trip_no:
                t = trip_no * 2
                for u in range(2):
                    turn(t + u + 1, 1 - u)
                    latents(t + u, u)
            turn(T - 1, 1)
            for u in range(2):
                latents(T - 2 + u, u)
            pe.wait_ge(kv_ready, T + 2)
            pe.wait_ge(squares_ready, T + 2)
            pe.sem_inc(k_used, 1)
            pe.sem_inc(a_used, 2)
            pe.wait_ge(fold_ready, 32)
            with pe.Fori(0, T // 4) as q:
                pe.wait_ge(k_ready, 12 * q + 12)
                pe.wait_ge(k_used, q + 1)
                for j in range(4):
                    last = pe.transpose(pk[0][0:KA, j * P:(j + 1) * P], kbuf[:, j * KA:(j + 1) * KA], ident[:, :])
                last.then_inc(k_mm, 1)
                for j in range(4):
                    h, u = q * 4 + j, j % 2
                    pe.wait_ge(ld_qb[u], 8 * (h - u) + 16)
                    pe.wait_ge(a_used, h + 1)
                    for r in range(RT):
                        n = P if r < RT - 1 else RL
                        last = pe.matmul(pw[u][0:n, (r // 3) * 512 + (r % 3) * KA:(r // 3) * 512 + (r % 3 + 1) * KA],
                                         wqb[:, u * QR + r * P:u * QR + r * P + n],
                                         fold[:, ds(h * KA, KA)], start=(r % 3 == 0), stop=True,
                                         skip_group_check=True)
                    last.then_inc(a_mm, 1)
            pe.wait_ge(a_used, H + 2)
            for n in range(3 * DK):
                c, k = n // DK, n % DK
                if n < T // 4:
                    pe.wait_ge(diag_ready, n + 1)
                    if n >= 2:
                        pe.wait_ge(rq_used, n - 1)
                    pe.matmul(pt[n % 2][:, :], ones[:, :], (rot_a, rot_b)[n % 2][:, :], start=True,
                              stop=True).then_inc(rq_mm, 1)
                if n >= 2:
                    pe.wait_ge(w_used, n - 1)
                for r in range(RT):
                    m = P if r < RT - 1 else RL
                    last = pe.matmul(pw[n % 2][:, 0:512], wqa[0:m, r * D + k * P:r * D + (k + 1) * P],
                                     afold[0:m, r * H * KA + c * 512:r * H * KA + (c + 1) * 512],
                                     start=(r == 0), stop=(r == RT - 1))
                last.then_inc(w_mm, 1)
            pe.wait_ge(k_used, T // 4 + 1)
            for g in range(4):
                if g >= 2:
                    pe.wait_ge(ov_used, g - 1)
                for j in range(4):
                    h = 4 * g + j
                    last = pe.matmul(pk[g % 2][C * j:C * (j + 1), 0:D], wv[:, h * C:(h + 1) * C],
                                     woT[:, h * D:(h + 1) * D], start=True, stop=True)
                last.then_inc(ov_mm, 1)


def attention(nc, hT, weff, caug, cosq, sinq, k_hi, k_lo, ident, slots_dram, cbar):
    st = ExitStack()
    with st:
        def sb(name, cols, dt=F32):
            return st.enter_context(nc.sbuf_tensor(name, [P, cols], dt))

        def pb(name, cols=QC):
            return st.enter_context(nc.psum_tensor(name, [P, cols], F32))

        def sem(name):
            return st.enter_context(nc.semaphore(name))

        q_hi = [sb("q_hi0", S, F32R), sb("q_hi1", S, F32R)]
        q_lo = [sb("q_lo0", S, F32R), sb("q_lo1", S, F32R)]
        wq = [sb("wq0", DK * KA), sb("wq1", DK * KA)]
        prob = [sb(f"prob{n}", 2 * QC) for n in range(2)]
        prob_hi = [sb(f"prob_hi{n}", 2 * QC, F16) for n in range(4)]
        prob_lo = [sb(f"prob_lo{n}", 2 * QC, F16) for n in range(4)]
        c_hi = sb("c_hi", T * CP, F16)
        c_lo = sb("c_lo", T * CP, F16)
        prob_scale = sb("prob_scale", 1)
        q_raw = sb("q_raw", QC)
        rot = sb("rot", QC)
        maxes = sb("maxes", 4 * T)
        maxneg = sb("maxneg", T)
        att_t = sb("att_t", QC)
        recip = sb("recip", 8)
        zeros = sb("zeros", 2 * RW)

        p_s = [pb("p_s0", 2 * QC), pb("p_s1", 2 * QC)]
        p_m = [pb("p_m0"), pb("p_m1")]
        p_o = pb("p_o")
        p_x = pb("p_x")

        wq_ready = sem("wq_ready")
        x_mm = sem("x_mm")
        x_used = sem("x_used")
        q_ready = sem("q_ready")
        max_mm = sem("max_mm")
        max_used = sem("max_used")
        neg_ready = sem("neg_ready")
        s_mm = sem("s_mm")
        p_ready = sem("p_ready")
        lo_ready = sem("lo_ready")
        o_mm = sem("o_mm")
        o_copied = sem("o_copied")
        zero_rows = sem("zero_rows")
        zeroed = sem("zeroed")
        c_ready = sem("c_ready2")
        vec = sem("vec")

        MAXIMA = (0, 0, 0, 0, 3, 4, 0, 2, 3, 3, 3, 4, 0, 2, 3, 4, 0, 2, 3, 3, 3, 3, 3, 3, 3, 3, 3, 3, 1, 0, 0, 0)
        PROJECT = (1, 5, 11, 15)
        assert sum(MAXIMA) == 4 * T and all(sum(MAXIMA[:s + 2]) <= 16 * c for c, s in enumerate(PROJECT))

        def beside(first, last):
            at = {}
            for s in range(STEPS):
                copy, turn, others, maxima = [], [], [], []
                if s == 17 or (s == 1 and not first):
                    copy = [("copy", 0 if s == 17 else 1)]
                if s == 19 or (s == 3 and not first):
                    turn = [("turn", 0 if s == 19 else 1)]
                if not last:
                    maxima = [("max", n) for n in range(sum(MAXIMA[:s]), sum(MAXIMA[:s + 1]))]
                    others = [("project", c) for c in range(4) if PROJECT[c] == s]
                    others += [("row", c) for c in range(4) if 28 + c == s]
                at[s] = maxima[:2] + copy + maxima[2:] + turn + others
            return at

        ALONE = [("project", c) for c in range(4)] + [("max", n) for n in range(4 * T)] + [("row", c) for c in range(4)]

        def x_base(h, first=False):
            return 8 if first else 10 * h + 7

        def x_use(h, what, first=False, last=False):
            if h is None:
                return {"project": 0, "row": 4}[what[0]] + what[1]
            uses = [w for todo in beside(first, last).values() for w in todo if w[0] in ("project", "row", "turn")]
            return x_base(h, first) + uses.index(what)

        block = st.enter_context(nc.Block())

        @block.sync
        def _(sp):
            rows = slots_dram.rearrange("(n p r) d -> n p (r d)", p=P, r=2)
            sp.wait_ge(zero_rows, 4)
            with sp.Fori(0, SLOT_TILES // 2) as n:
                sp.dma_start(rows[ds(n, 1), :, :].rearrange("a p n -> (a p) n"), zeros[:, :]).then_inc(zeroed, 16)
            sp.wait_ge(zeroed, 16 * (SLOT_TILES // 2))

        @block.gpsimd
        def _(gp):
            gp.memset(prob_scale[:, :], float(np.log(P_SCALE))).then_inc(zero_rows, 1)
            gp.wait_ge(zero_rows, 1)
            for u in range(2):
                gp.memset(q_lo[u][KA:KS, :].bitcast(F32), 0.0).then_inc(zero_rows, 1)
                gp.wait_ge(zero_rows, u + 2)
            gp.memset(zeros[:, :], 0.0).then_inc(zero_rows, 1)
            with gp.Fori(0, H) as h:
                for s in range(STEPS):
                    n = h * STEPS + s
                    gp.wait_ge(p_ready, n + 3)
                    gp.wait_ge(o_mm, n + 1)
                    gp.tensor_tensor(prob_lo[s % 4][:, :], prob[s % 2][:, :], prob_hi[s % 4][:, :],
                                     ALU.subtract).then_inc(lo_ready, 1)

        @block.scalar
        def _(act):
            w3 = weff[:, :].rearrange("p (k n) -> p k n", k=DK)

            def copy_wq(h, u):
                act.wait_ge(q_ready, 4 * h + 1)
                act.copy(wq[u][:, :].rearrange("p (k n) -> p k n", k=DK), w3[:, :, ds(h * KA, KA)]).then_inc(wq_ready, 1)

            def head(h, u, more=True):
                for s in range(STEPS):
                    n = h * STEPS + s
                    act.wait_ge(s_mm, n + 1)
                    act.wait_ge(lo_ready, n + 1)
                    act.wait_ge(o_mm, n + 1)
                    act.activation(prob[s % 2][:, :], p_s[s % 2][:, :], ACT.Exp, bias=prob_scale[:, :],
                                   scale=SCALE)
                    act.activation(prob_hi[s % 4][:, :], p_s[s % 2][:, :], ACT.Exp, bias=prob_scale[:, :],
                                   scale=SCALE).then_inc(p_ready, 1)
                    if s == 24 and more:
                        copy_wq(h + 2, u)

            act.preload_act_table(ACT.Exp)
            for u in range(2):
                copy_wq(u, u)
            with act.Fori(0, (H - 2) // 2) as trip_no:
                h = trip_no * 2
                for u in range(2):
                    head(h + u, u)
            for u in range(2):
                head(H - 2 + u, u, more=False)

        @block.vector
        def _(v):
            step = Chain(v, vec)

            def project(c, g, u, use):
                tok = slice(c * QC, (c + 1) * QC)
                v.wait_ge(x_mm, use + 1)
                v.wait_ge(q_ready, 4 * g + c + 5)
                step(v.tensor_tensor(q_raw[0:KA, :], p_x[0:KA, :], cosq[0:KA, tok], ALU.mult))
                step(v.tensor_tensor(rot[HALF:ROPE, :], p_x[0:HALF, :], sinq[0:HALF, tok], ALU.mult))
                v.tensor_tensor(rot[0:HALF, :], p_x[HALF:ROPE, :], sinq[HALF:ROPE, tok], ALU.mult).then_inc(x_used, 1)
                v.wait_ge(x_used, use + 2)
                step(v.tensor_tensor(q_raw[0:ROPE, :], q_raw[0:ROPE, :], rot[0:ROPE, :], ALU.add))
                step(v.tensor_copy(q_hi[u][0:KA, tok], q_raw[0:KA, :]))
                v.tensor_tensor(q_lo[u][0:KA, tok], q_raw[0:KA, :], q_hi[u][0:KA, tok].bitcast(F32),
                                ALU.subtract).then_inc(q_ready, 1)

            def maximum(n, g):
                v.wait_ge(max_mm, 64 * g + n + 1)
                v.tensor_reduce(maxes[:, n:n + 1], p_m[n % 2][:, :], AX.X, ALU.max).then_inc(max_used, 1)
                if n == 4 * T - 1:
                    v.wait_ge(max_used, 64 * g + n + 3)
                    v.tensor_reduce(maxneg[:, :], maxes[:, :].rearrange("p (t c) -> p t c", c=4), AX.X, ALU.max,
                                    negate=True).then_inc(neg_ready, 1)
                    v.wait_ge(neg_ready, g + 1)

            def row(c, u, use):
                v.wait_ge(x_mm, use + 1)
                v.tensor_copy(q_hi[u][KA:KS, c * QC:(c + 1) * QC], p_x[KA:KS, :]).then_inc(x_used, 1)

            def copy_out(half, h):
                v.wait_ge(o_mm, STEPS * h + 16 * half + 16 + 4)
                v.tensor_copy(att_t[:, :], p_o[:, :]).then_inc(o_copied, 1)

            def turn(half, h, use):
                v.wait_ge(x_mm, use + 1)
                src = p_x[:, :].rearrange("p (b s n) -> p b s n", b=4, s=2)
                r = recip[:, :].rearrange("p (b s n) -> p b s n", b=4, s=2)
                step(v.reciprocal(r, src[:, :, :, C:C + 1]))
                dst = cbar[:, half * 8 * HC:(half + 1) * 8 * HC].rearrange("p (s b n) -> p b s n", s=2, b=4)
                v.tensor_tensor(dst[:, :, :, ds(h * C, C)], src[:, :, :, 0:C], r.to_broadcast([P, 4, 2, C]),
                                ALU.mult).then_inc(x_used, 1)
                v.wait_ge(x_used, use + 2)

            def head(h, u, first=False, last=False):
                for s, todo in beside(first, last).items():
                    for what in todo:
                        kind, c = what
                        if kind == "project":
                            project(c, h + 1, 1 - u, x_use(h, what, first, last))
                        elif kind == "max":
                            maximum(c, h + 1)
                        elif kind == "row":
                            row(c, 1 - u, x_use(h, what, first, last))
                        elif kind == "copy":
                            copy_out(c, h - c)
                        else:
                            turn(c, h - c, x_use(h, what, first, last))

            v.tensor_scalar(c_hi[:, :], caug[:, :], C_SCALE, None, ALU.mult).then_inc(c_ready, 1)
            v.wait_ge(c_ready, 1)
            v.scalar_tensor_tensor(out=c_lo[:, :], in0=caug[:, :], scalar=C_SCALE, in1=c_hi[:, :], op0=ALU.mult,
                                   op1=ALU.subtract).then_inc(c_ready, 1)
            for kind, c in ALONE:
                if kind == "project":
                    project(c, 0, 0, x_use(None, (kind, c)))
                elif kind == "max":
                    maximum(c, 0)
                else:
                    row(c, 0, x_use(None, (kind, c)))
            head(0, 0, first=True)
            start = step.now
            with v.Fori(0, (H - 2) // 2) as trip_no:
                h = 1 + trip_no * 2
                step.before, step.now = start + (h - 1) * STEPS_V, 0
                head(h, 1)
                head(h + 1, 0)
                assert step.now == 2 * STEPS_V
            step.before, step.now = start + (H - 2) * STEPS_V, 0
            head(H - 1, 1, last=True)
            copy_out(1, H - 1)
            turn(1, H - 1, x_base(H - 1) + 2)

        @block.tensor
        def _(pe):
            for s, n in ((x_used, 1), (q_ready, 5), (max_used, 2), (p_ready, 2), (lo_ready, 2), (o_mm, 4), (o_copied, 1)):
                pe.sem_inc(s, n)

            def project(c, g, u, use):
                pe.wait_ge(wq_ready, g + 1)
                pe.wait_ge(x_used, use + 1)
                for k in range(DK):
                    last = pe.matmul(p_x[0:KA, :], wq[u][:, k * KA:(k + 1) * KA],
                                     hT[:, k * S + c * QC:k * S + (c + 1) * QC], start=(k == 0), stop=(k == DK - 1))
                last.then_inc(x_mm, 1)

            def maximum(n, g, u):
                j, kc = n // 4, n % 4
                if kc == 0:
                    pe.wait_ge(q_ready, 4 * g + j // 4 + 6)
                pe.wait_ge(max_used, 64 * g + n + 1)
                pe.matmul(p_m[n % 2][:, :], q_hi[u][0:KA, j * P:(j + 1) * P], k_hi[0:KA, kc * QC:(kc + 1) * QC],
                          start=True, stop=True).then_inc(max_mm, 1)

            def row(c, g, use):
                pe.wait_ge(neg_ready, g + 1)
                pe.wait_ge(x_used, use + 1)
                for j in range(4):
                    last = pe.matmul(p_x[KA:KS, j * P:(j + 1) * P], maxneg[:, 4 * c + j:4 * c + j + 1], ident[:, :],
                                     start=True, stop=True)
                last.then_inc(x_mm, 1)

            def turn(half, h, use):
                pe.wait_ge(o_copied, 2 * h + half + 2)
                pe.wait_ge(x_used, use + 1)
                for b in range(4):
                    last = pe.transpose(p_x[:, b * P:(b + 1) * P], att_t[:, b * P:(b + 1) * P], ident[:, :])
                last.then_inc(x_mm, 1)

            def scores(s, h, u, first, between):
                half, kt = s // 16, s % 16
                n = STEPS * h + s
                if kt == 0:
                    pe.wait_ge(x_used, x_base(h, first) + 2 * half - 1)
                pe.wait_ge(p_ready, n + 1)
                keys = slice(kt * P, (kt + 1) * P)
                for part, (kk, qq) in enumerate(((k_hi, q_hi), (k_hi, q_lo), (k_lo, q_hi))):
                    if part and between:
                        between.pop(0)()
                    for j in range(2):
                        c = 2 * half + j
                        last = pe.matmul(p_s[s % 2][:, j * QC:(j + 1) * QC], kk[0:KS, keys],
                                         qq[u][0:KS, c * QC:(c + 1) * QC], start=(part == 0), stop=(part == 2))
                last.then_inc(s_mm, 1)

            def weigh(s, h):
                half, kt = s // 16, s % 16
                n = STEPS * h + s
                pe.wait_ge(lo_ready, n + 3)
                if kt == 0:
                    pe.wait_ge(o_copied, 2 * h + half + 1)
                for part, (cc, pp) in enumerate(((c_hi, prob_hi[s % 4]), (c_lo, prob_hi[s % 4]),
                                              (c_hi, prob_lo[s % 4]))):
                    for j in range(2):
                        last = pe.matmul(p_o[j * CP:(j + 1) * CP, :], cc[:, kt * CP:(kt + 1) * CP],
                                         pp[:, j * QC:(j + 1) * QC], start=(kt == 0 and part == 0),
                                         stop=(kt == 15 and part == 2))
                last.then_inc(o_mm, 1)

            def head(h, u, first=False, last=False):
                for s, todo in beside(first, last).items():
                    maxima = [(lambda c=c: maximum(c, h + 1, 1 - u)) for kind, c in todo if kind == "max"]
                    scores(s, h, u, first, maxima)
                    if s >= 2:
                        weigh(s - 2, h)
                    elif not first:
                        weigh(STEPS - 2 + s, h - 1)
                    for m in maxima:
                        m()
                    for what in todo:
                        kind, c = what
                        if kind == "project":
                            project(c, h + 1, 1 - u, x_use(h, what, first, last))
                        elif kind == "row":
                            row(c, h + 1, x_use(h, what, first, last))
                        elif kind == "turn":
                            turn(c, h - c, x_use(h, what, first, last))

            pe.wait_ge(zero_rows, 3)
            for kind, c in ALONE:
                if kind == "project":
                    project(c, 0, 0, x_use(None, (kind, c)))
                elif kind == "max":
                    maximum(c, 0, 0)
                else:
                    row(c, 0, x_use(None, (kind, c)))
            pe.wait_ge(c_ready, 2)
            head(0, 0, first=True)
            with pe.Fori(0, (H - 2) // 2) as trip_no:
                h = 1 + trip_no * 2
                head(h, 1)
                head(h + 1, 0)
            head(H - 1, 1, last=True)
            weigh(STEPS - 2, H - 1)
            weigh(STEPS - 1, H - 1)
            turn(1, H - 1, x_base(H - 1) + 2)


def ffn(nc, a, x, ident, mod, wov, cbar, slots_dram, ranked_dram, shared_dram, out):
    outer = ExitStack()
    with outer:
        def keep(name, cols, dt=F32):
            return outer.enter_context(nc.sbuf_tensor(name, [P, cols], dt))

        hall = keep("hall", T * D)
        mv = keep("mv2", T * 2)
        rstd = keep("rstd2", T)
        weight = keep("weight", T * 8)
        slot = keep("slot", T * 8, U32)
        tile_expert = keep("tile_expert", TILES, I32)
        sc = keep("sc", T * E)
        chosen = keep("chosen", T * E)
        val = keep("val", T * E)
        vtop = keep("vtop", T * 8)
        project_out(nc, x, ident, mod, wov, cbar, mv, rstd)
        route(nc, a, x, ident, mod, mv, rstd, hall, slot, tile_expert, sc, chosen, val, vtop, slots_dram)
        experts(nc, a, ident, hall, slot, tile_expert, sc, chosen, val, vtop, weight, slots_dram, ranked_dram, shared_dram)
        combine(nc, x, mod, weight, ranked_dram, shared_dram, out)


def project_out(nc, x, ident, mod, wov, cbar, mv, rstd):
    st = ExitStack()
    with st:
        def sb(name, cols, dt=F32):
            return st.enter_context(nc.sbuf_tensor(name, [P, cols], dt))

        def sem(name):
            return st.enter_context(nc.semaphore(name))

        cst = [sb("cst0", HC), sb("cst1", HC)]
        ctb = [sb("ctb0", HC), sb("ctb1", HC)]
        gated = sb("gated", D)
        stats = sb("stats2", T * 6)
        var = sb("var2", T)
        p_t = [st.enter_context(nc.psum_tensor(f"p_t{n}", [P, HC], F32)) for n in range(2)]
        p_y = [st.enter_context(nc.psum_tensor(f"p_y{n}", [P, D], F32)) for n in range(2)]
        c_ready = sem("c_ready")
        ct_mm = sem("ct_mm")
        ct_ready = sem("ct_ready")
        y_mm = sem("y_mm")
        y_used = sem("y_used")
        vec = sem("vec2")
        var_ready = sem("var_ready2")
        stats_ready = sem("stats_ready2")
        counted = sem("counted2")
        root_ready = sem("root_ready2")
        block = st.enter_context(nc.Block())

        @block.gpsimd
        def _(gp):
            with gp.Fori(0, T // 2) as trip_no:
                t = trip_no * 2
                for u in range(2):
                    gp.wait_ge(ct_mm, t + u + 1)
                    gp.tensor_copy(cst[u][:, :], cbar[:, ds((t + u) * HC, HC)]).then_inc(c_ready, 1)

        @block.scalar
        def _(act):
            with act.Fori(0, T // 2) as trip_no:
                t = trip_no * 2
                for u in range(2):
                    act.wait_ge(ct_mm, t + u + 3)
                    act.wait_ge(y_mm, t + u + 1)
                    act.copy(ctb[u][:, :], p_t[u][:, :]).then_inc(ct_ready, 1)
            act.wait_ge(var_ready, 1)
            act.activation(rstd[:, :], var[:, :], ACT.Sqrt).then_inc(root_ready, 1)

        @block.vector
        def _(v):
            step = Chain(v, vec)
            with v.Fori(0, T // 2) as trip_no:
                t = trip_no * 2
                step.enter(t, 1)
                for u in range(2):
                    xt = x[:, ds((t + u) * D, D)]
                    v.wait_ge(y_mm, t + u + 3)
                    v.tensor_tensor(gated[:, :], p_y[u][:, :], mod[:, 2 * D:3 * D], ALU.mult).then_inc(y_used, 1)
                    v.wait_ge(y_used, t + u + 3)
                    step(v.tensor_tensor(xt, xt, gated[:, :], ALU.add))
                    v.sem_inc(counted, 1)
                    v.bn_stats(stats[:, ds((t + u) * 6, 6)], xt).then_inc(stats_ready, 1)
            step.leave(T, 2)
            v.wait_ge(stats_ready, T)
            for t in range(T):
                last = v.bn_aggr(mv[:, t * 2:(t + 1) * 2], stats[:, t * 6:(t + 1) * 6])
            step(last)
            v.tensor_scalar(var[:, :], mv[:, :].rearrange("p (t n) -> p t n", n=2)[:, :, 1], 1e-5, None,
                            ALU.add).then_inc(var_ready, 1)
            v.wait_ge(root_ready, 1)
            step(v.reciprocal(rstd[:, :], rstd[:, :]))

        @block.tensor
        def _(pe):
            for s in (ct_mm, ct_ready, y_mm, y_used):
                pe.sem_inc(s, 2)

            def turn(n, u):
                pe.wait_ge(c_ready, n + 1)
                pe.wait_ge(ct_ready, n + 1)
                for g in range(4):
                    last = pe.transpose(p_t[u][:, g * P:(g + 1) * P], cst[u][:, g * P:(g + 1) * P], ident[:, :])
                last.then_inc(ct_mm, 1)

            def project(n, u):
                pe.wait_ge(ct_ready, n + 3)
                pe.wait_ge(y_used, n + 1)
                for g in range(4):
                    last = pe.matmul(p_y[u][:, :], ctb[u][:, g * P:(g + 1) * P], wov[:, g * D:(g + 1) * D],
                                     start=(g == 0), stop=(g == 3))
                last.then_inc(y_mm, 1)

            turn(0, 0)
            with pe.Fori(0, T // 2 - 1) as trip_no:
                t = trip_no * 2
                for u in range(2):
                    turn(t + u + 1, 1 - u)
                    project(t + u, u)
            turn(T - 1, 1)
            for u in range(2):
                project(T - 2 + u, u)


def route(nc, a, x, ident, mod, mv, rstd, hall, slot, tile_expert, sc, chosen, val, vtop, slots_dram):
    st = ExitStack()
    with st:
        def sb(name, cols, dt=F32):
            return st.enter_context(nc.sbuf_tensor(name, [P, cols], dt))

        def sem(name):
            return st.enter_context(nc.semaphore(name))

        PADG = 16
        PADE = E + 8
        gate = sb("gate", DK * E)
        lower = sb("lower", P)
        ones = sb("ones2", P)
        thresholds = sb("thresholds", T)
        numbers = sb("numbers", 1)
        hb = [sb("hb0", D), sb("hb1", D)]
        h2T = [sb("h2T0", D), sb("h2T1", D)]
        tmp = sb("tmp", T * E)
        gpad = sb("gpad", T * PADG)
        gtop = sb("gtop", T * 8)
        gkey = sb("gkey", T * 8)
        grep = sb("grep", T * PADG)
        gmask = sb("gmask", T * GROUPS)
        gpen = sb("gpen", T * GROUPS)
        epad = sb("epad", T * PADE)
        etop = sb("etop", T * 8)
        ekey = sb("ekey", T * 8)
        erep = sb("erep", T * PADE)
        before = sb("before", (T + 1) * E)
        cmp = sb("cmp", E * T)
        ntiles = sb("ntiles", E)
        scan = [sb("scan0", E), sb("scan1", E)]
        first = sb("first", E)
        texp = sb("texp", E)
        tcol = sb("tcol", 1)
        assert SLOT_TILES == P
        tsum = sb("tsum", TILES)
        p_t = [st.enter_context(nc.psum_tensor(f"p_tn{n}", [P, D], F32)) for n in range(2)]
        p_l = [st.enter_context(nc.psum_tensor(f"p_l{n}", [P, E], F32)) for n in range(2)]
        p_pos = st.enter_context(nc.psum_tensor("p_pos", [P, T * E], F32))
        p_cnt = st.enter_context(nc.psum_tensor("p_cnt", [P, E + P], F32))
        ld = sem("ld3")
        h_ready = sem("h_ready3")
        t_mm = sem("t_mm3")
        t_ready = sem("t_ready3")
        l_mm = sem("l_mm3")
        l_used = sem("l_used3")
        kept = sem("kept3")
        pads = sem("pads3")
        pool = sem("pool3")
        chosen_ready = sem("chosen_ready3")
        cum_ready = sem("cum_ready3")
        pos_mm = sem("pos_mm3")
        tcol_ready = sem("tcol_ready3")
        vec = sem("vec3")
        stored = sem("stored3")
        block = st.enter_context(nc.Block())

        @block.sync
        def _(sp):
            for k in range(DK):
                sp.dma_start(gate[:, k * E:(k + 1) * E], a["gate"][k * P:(k + 1) * P, :]).then_inc(ld, 16)
            sp.dma_start(lower[:, :], a["lower"]).then_inc(ld, 16)
            sp.dma_start(thresholds[:, :], a["thresholds"]).then_inc(ld, 16)
            sp.dma_start(numbers[:, :], a["numbers"]).then_inc(ld, 16)
            sp.wait_ge(kept, T + 2)
            sp.dma_start(slots_dram[SLOT_TILES * P:SLOT_TILES * P + S, 0:D].rearrange("(t p) d -> p t d", p=P),
                         hall[:, :].rearrange("p (t d) -> p t d", t=T)).then_inc(stored, 16)
            sp.wait_ge(stored, 16)

        @block.gpsimd
        def _(gp):
            step = Chain(gp, pool)
            step(gp.memset(ones[:, :], 1.0))
            step(gp.memset(gpad[:, :].rearrange("p (t n) -> p t n", t=T)[:, :, GROUPS:8], -1.0))
            step(gp.memset(gpad[:, :].rearrange("p (t n) -> p t n", t=T)[:, :, 8:PADG], 2.0))
            step(gp.memset(gkey[:, :], 2.0))
            step(gp.memset(ekey[:, :], 2.0))
            step(gp.memset(tsum[:, 0:T], float(E)))
            step(gp.memset(tsum[:, T:2 * T], float(E + 1)))
            step(gp.memset(before[:, 0:E], 0.0))
            gp.memset(epad[:, :].rearrange("p (t n) -> p t n", t=T)[:, :, E:PADE], 2.0).then_inc(pads, 1)
            gp.wait_ge(pads, 1)
            with gp.Fori(0, T // 2) as trip_no:
                t = trip_no * 2
                for u in range(2):
                    gp.wait_ge(h_ready, t + u + 1)
                    gp.tensor_copy(hall[:, ds((t + u) * D, D)], hb[u][:, :]).then_inc(kept, 1)

        @block.scalar
        def _(act):
            def keep_turned(n, u):
                act.wait_ge(t_mm, n + 3)
                act.wait_ge(l_mm, n + 1)
                act.copy(h2T[u][:, :], p_t[u][:, :]).then_inc(t_ready, 1)

            def expo(n, u):
                act.wait_ge(l_mm, n + 3)
                act.activation(sc[:, ds(n * E, E)], p_l[u][:, :], ACT.Exp, scale=-1.0).then_inc(l_used, 1)

            keep_turned(0, 0)
            with act.Fori(0, T // 2 - 1) as trip_no:
                t = trip_no * 2
                for u in range(2):
                    keep_turned(t + u + 1, 1 - u)
                    expo(t + u, u)
            keep_turned(T - 1, 1)
            for u in range(2):
                expo(T - 2 + u, u)

        @block.vector
        def _(v):
            step = Chain(v, vec)

            def t3(tensor, n=E):
                return tensor[:, :].rearrange("p (t n) -> p t n", n=n)

            with v.Fori(0, T // 2) as trip_no:
                t = trip_no * 2
                step.enter(t, 2)
                for u in range(2):
                    v.wait_ge(t_mm, t + u + 1)
                    v.wait_ge(kept, t + u + 1)
                    step(v.tensor_scalar(hb[u][:, :], x[:, ds((t + u) * D, D)], mv[:, ds((t + u) * 2, 1)],
                                         rstd[:, ds(t + u, 1)], ALU.subtract, ALU.mult))
                    step(v.tensor_tensor(hb[u][:, :], hb[u][:, :], mod[:, 4 * D:5 * D], ALU.mult))
                    v.tensor_tensor(hb[u][:, :], hb[u][:, :], mod[:, 3 * D:4 * D], ALU.add).then_inc(h_ready, 1)
            step.leave(T, 2)
            v.wait_ge(l_used, T + 2)
            v.wait_ge(pads, 1)
            v.wait_ge(ld, 16 * (DK + 3))
            step(v.tensor_scalar(sc[:, :], sc[:, :], 1.0, None, ALU.add))
            step(v.reciprocal(sc[:, :], sc[:, :]))
            step(v.tensor_reduce(t3(gpad, PADG)[:, :, 0:GROUPS],
                                 sc[:, :].rearrange("p (t g n) -> p t g n", t=T, g=GROUPS), AX.X, ALU.max))
            for t in range(T):
                last = v.max(gtop[:, t * 8:(t + 1) * 8], gpad[:, t * PADG:t * PADG + 8])
            step(last)
            step(v.tensor_copy(t3(gkey, 8)[:, :, 0:2], t3(gtop, 8)[:, :, 0:2]))
            for t in range(T):
                last = v.match_replace(grep[:, t * PADG:(t + 1) * PADG], gkey[:, t * 8:(t + 1) * 8],
                                       gpad[:, t * PADG:(t + 1) * PADG], -5.0)
            step(last)
            step(v.tensor_scalar(t3(gmask, GROUPS), t3(grep, PADG)[:, :, 0:GROUPS], -5.0, None, ALU.is_equal))
            step(v.tensor_scalar(gpen[:, :], gmask[:, :], -1.0, None, ALU.add))
            by_group = lambda z: z.rearrange("p (t g n) -> p t g n", t=T, g=GROUPS)
            wide = lambda z: z[:, :].rearrange("p (t g n) -> p t g n", t=T, n=1).to_broadcast([P, T, GROUPS, EPG])
            step(v.tensor_tensor(by_group(tmp[:, :]), by_group(sc[:, :]), wide(gmask), ALU.mult))
            step(v.tensor_tensor(by_group(tmp[:, :]), by_group(tmp[:, :]), wide(gpen), ALU.add))
            step(v.tensor_copy(t3(epad, PADE)[:, :, 0:E], t3(tmp)))
            for t in range(T):
                last = v.max(etop[:, t * 8:(t + 1) * 8], epad[:, t * PADE:t * PADE + E])
            step(last)
            step(v.tensor_copy(t3(ekey, 8)[:, :, 0:TOPK], t3(etop, 8)[:, :, 0:TOPK]))
            for t in range(T):
                last = v.match_replace(erep[:, t * PADE:(t + 1) * PADE], ekey[:, t * 8:(t + 1) * 8],
                                       epad[:, t * PADE:(t + 1) * PADE], -5.0)
            step(last)
            v.tensor_scalar(t3(chosen), t3(erep, PADE)[:, :, 0:E], -5.0, None, ALU.is_equal).then_inc(chosen_ready, 1)
            v.wait_ge(chosen_ready, 1)
            with v.Fori(0, T) as t:
                step.enter(t, 1)
                step(v.tensor_tensor(before[:, ds((t + 1) * E, E)], before[:, ds(t * E, E)], chosen[:, ds(t * E, E)],
                                     ALU.add))
            step.leave(T)
            v.tensor_copy(first[:, :], before[:, T * E:(T + 1) * E]).then_inc(cum_ready, 1)
            v.wait_ge(pos_mm, 2)
            step(v.tensor_tensor(cmp[:, :].rearrange("p (e n) -> p e n", n=T),
                                 p_cnt[:, 0:E].rearrange("p (e n) -> p e n", n=1).to_broadcast([P, E, T]),
                                 thresholds[:, :].rearrange("p (e n) -> p e n", e=1).to_broadcast([P, E, T]),
                                 ALU.is_gt))
            step(v.tensor_reduce(ntiles[:, :], cmp[:, :].rearrange("p (e n) -> p e n", n=T), AX.X, ALU.add))
            step(v.tensor_copy(scan[0][:, :], ntiles[:, :]))
            src = 0
            for d in (1, 2, 4, 8, 16):
                step(v.tensor_copy(scan[1 - src][:, 0:d], scan[src][:, 0:d]))
                step(v.tensor_tensor(scan[1 - src][:, d:E], scan[src][:, d:E], scan[src][:, 0:E - d], ALU.add))
                src = 1 - src
            ends = scan[src]
            step(v.tensor_tensor(first[:, :], ends[:, :], ntiles[:, :], ALU.subtract))
            step(v.tensor_scalar(first[:, :], first[:, :], float(P), 1.0, ALU.mult, ALU.add))
            step(v.tensor_tensor(t3(val), p_pos[:, :].rearrange("p (t n) -> p t n", n=E),
                                 first[:, :].rearrange("p (t n) -> p t n", t=1).to_broadcast([P, T, E]), ALU.add))
            step(v.tensor_tensor(val[:, :], val[:, :], chosen[:, :], ALU.mult))
            for t in range(T):
                last = v.max(vtop[:, t * 8:(t + 1) * 8], val[:, t * E:(t + 1) * E])
            step(last)
            step(v.tensor_scalar(t3(slot, 8)[:, :, 0:TOPK], t3(vtop, 8)[:, :, 0:TOPK], -1.0, None, ALU.add))
            step(v.tensor_scalar(texp[:, :], ends[:, :], numbers[:, 0:1], None, ALU.is_le))
            v.tensor_reduce(tcol[:, :], texp[:, :], AX.X, ALU.add).then_inc(tcol_ready, 1)
            v.wait_ge(pos_mm, 3)
            step(v.tensor_scalar(tsum[0:1, 2 * T:TILES], p_cnt[0:1, E:E + P], float(E - 1), None, ALU.min))
            step(v.tensor_copy(tile_expert[0:1, :], tsum[0:1, :]))

        @block.tensor
        def _(pe):
            for s in (t_mm, t_ready, l_mm, l_used, kept):
                pe.sem_inc(s, 2)
            pe.wait_ge(ld, 16 * (DK + 3))

            def turn(n, u):
                pe.wait_ge(h_ready, n + 1)
                pe.wait_ge(t_ready, n + 1)
                for k in range(DK):
                    last = pe.transpose(p_t[u][:, k * P:(k + 1) * P], hb[u][:, k * P:(k + 1) * P], ident[:, :])
                last.then_inc(t_mm, 1)

            def logits(n, u):
                pe.wait_ge(t_ready, n + 3)
                pe.wait_ge(l_used, n + 1)
                for k in range(DK):
                    last = pe.matmul(p_l[u][:, :], h2T[u][:, k * P:(k + 1) * P], gate[:, k * E:(k + 1) * E],
                                     start=(k == 0), stop=(k == DK - 1))
                last.then_inc(l_mm, 1)

            turn(0, 0)
            with pe.Fori(0, T // 2 - 1) as trip_no:
                t = trip_no * 2
                for u in range(2):
                    turn(t + u + 1, 1 - u)
                    logits(t + u, u)
            turn(T - 1, 1)
            for u in range(2):
                logits(T - 2 + u, u)
            pe.wait_ge(pads, 1)
            pe.wait_ge(chosen_ready, 1)
            pe.matmul(p_pos[:, :], lower[:, :], chosen[:, :], start=True, stop=False)
            pe.wait_ge(cum_ready, 1)
            pe.matmul(p_pos[:, :], ones[:, :], before[:, 0:T * E], start=False, stop=True).then_inc(pos_mm, 1)
            pe.matmul(p_cnt[:, 0:E], ones[:, :], before[:, T * E:(T + 1) * E], start=True, stop=True).then_inc(pos_mm, 1)
            pe.wait_ge(tcol_ready, 1)
            pe.matmul(p_cnt[0:1, E:E + P], tcol[:, :], ident[:, :], start=True, stop=True).then_inc(pos_mm, 1)


def experts(nc, a, ident, hall, slot, tile_expert, sc, chosen, val, vtop, weight, slots_dram, ranked_dram, shared_dram):
    st = ExitStack()
    with st:
        def sb(name, cols, dt=F32, parts=P):
            return st.enter_context(nc.sbuf_tensor(name, [parts, cols], dt))

        def pb(name):
            return st.enter_context(nc.psum_tensor(name, [P, 512], F32))

        def sem(name):
            return st.enter_context(nc.semaphore(name))

        U = 8
        rows = [sb(f"rows{n}", RW) for n in range(U)]
        dests = sb("dests", T * TOPK)
        own = sb("own", SLOT_TILES)
        dest = [sb(f"dest{n}", 1, U32) for n in range(U)]
        w = [sb(f"w{n}", WIN + WOUT) for n in range(U)]
        rT = [sb("rT0", D), sb("rT1", D)]
        ex = [sb("ex0", M), sb("ex1", M)]
        hid = [sb("hid0", M), sb("hid1", M)]
        hidT = [sb("hidT0", 2 * P, parts=MH), sb("hidT1", 2 * P, parts=MH)]
        y = [sb(f"y{n}", D) for n in range(U)]
        ST = 4
        stage = [sb(f"stage{n}", TOPK * RW) for n in range(ST)]
        stage_slot = [sb(f"stage_slot{n}", 8, U32) for n in range(ST)]
        wn = sb("wn", T * E)
        wsum = sb("wsum", T)
        tmp = sb("tmp_w", T * E)
        p_r = [pb("p_r0"), pb("p_r1")]
        p_g = [pb("p_g0"), pb("p_g1")]
        p_h = [pb("p_h0"), pb("p_h1")]
        p_y = [pb("p_d0"), pb("p_d1")]
        staged = sem("staged")
        issued = sem("issued")
        scattered = [sem(f"scattered{n}") for n in range(ST)]
        row_ld = [sem(f"row_ld{n}") for n in range(U)]
        w_ld = [sem(f"w_ld{n}") for n in range(U)]
        r_mm = sem("r_mm")
        r_used = sem("r_used")
        g_mm = sem("g_mm")
        silued = sem("silued")
        hid_ready = sem("hid_ready")
        h_mm = sem("h_mm")
        h_used = sem("h_used")
        vec = sem("vec4")
        y_mm = sem("y_mm4")
        y_ready = sem("y_ready")
        y_out = [sem(f"y_out{n}") for n in range(U)]
        ranked = [sem(f"ranked{n}") for n in range(U)]
        tables = sem("tables")
        block = st.enter_context(nc.Block())
        CREDIT = {r_mm: U, r_used: 2, g_mm: 2, hid_ready: 2, h_mm: 2, h_used: 2, y_mm: U, y_ready: 2}


        @block.gpsimd
        def _(gp):
            with gp.Fori(0, T // ST) as trip_no:
                for u in range(ST):
                    gp.wait_ge(staged, trip_no * ST + u + 1)
                    gp.sem_inc(issued, 1)
                    for j in range(TOPK):
                        gp.indirect_dma_start(
                            out=slots_dram[0:SLOT_TILES * P, :],
                            out_offset=bass.IndirectOffsetOnAxis(ap=stage_slot[u][:, j:j + 1], axis=0),
                            in_=stage[u][:, j * RW:(j + 1) * RW], in_offset=None).then_inc(scattered[u], 16)

            with gp.Fori(0, (TILES - 2 * T) // U) as trip_no:
                for u in range(U):
                    gp.wait_ge(y_ready, trip_no * U + 2 * T + u + 3)
                    gp.sem_inc(issued, 1)
                    gp.indirect_dma_start(
                        out=ranked_dram, out_offset=bass.IndirectOffsetOnAxis(ap=dest[u][:, :], axis=0),
                        in_=y[u][:, :], in_offset=None).then_inc(ranked[u], 16)
            for s in ranked:
                gp.wait_ge(s, 16 * (TILES - 2 * T) // U)

        @block.sync
        def _(sp):
            for s, n in CREDIT.items():
                sp.sem_inc(s, n)

            sp.dma_start(dests[:, :], a["dests"]).then_inc(tables, 16)
            sp.dma_start(own[:, :], a["own"]).then_inc(tables, 16)

            def load_rows(i, u, row, cols=RW):
                if cols == RW:
                    sp.wait_ge(y_ready, i + u - U + 3)
                else:
                    sp.wait_ge(r_mm, i + u + 1)
                sp.dma_start(rows[u][:, 0:cols], slots_dram[ds(row, P), 0:cols]).then_inc(row_ld[u], 16)

            def load_weights(i, u):
                e = sp.value_load(tile_expert[0:1, ds(i + u, 1)], min_val=0, max_val=E + 1)
                sp.wait_ge(y_mm, i + u + 1)
                sp.dma_start(w[u][:, :], a["experts"][ds(e, 1), :, :].rearrange("a p n -> (a p) n")).then_inc(w_ld[u], 16)

            def keep_weights(i, u):
                sp.wait_ge(y_mm, i + u + 1)
                sp.sem_inc(w_ld[u], 16)

            def store(n, u):
                sp.wait_ge(y_ready, n + 3)
                sp.dma_start(shared_dram[ds(n * P, P), :], y[u][:, :]).then_inc(y_out[u], 16)

            assert T == 2 * U
            for half in range(2):
                for group in range(2):
                    i = half * T + group * U
                    for u in range(U):
                        load_rows(i, u, (group * U + u + SLOT_TILES) * P, cols=D)
                        (keep_weights if group else load_weights)(i, u)
                        if i:
                            store(i + u - U, u)
            def next_weights(u):
                load_weights(2 * T, u)
                store(2 * T - U + u, u)

            for u in range(U - 3):
                next_weights(u)
            for s in scattered:
                sp.wait_ge(s, 16 * TOPK * T // ST)
            for u in range(U):
                load_rows(2 * T, u, u * P)
                if u >= U - 3:
                    next_weights(u)
            with sp.Fori(1, (TILES - 2 * T) // U) as trip_no:
                i = 2 * T + trip_no * U
                for u in range(U):
                    load_weights(i, u)
                    load_rows(i, u, (i + u - 2 * T) * P)
            for s in y_out:
                sp.wait_ge(s, 16 * 2 * T // U + 16)

        @block.scalar
        def _(act):
            def copy_rows(n, u):
                act.wait_ge(r_mm, n + U + 1)
                act.wait_ge(g_mm, n + 1)
                act.copy(rT[u % 2][:, :], p_r[u % 2][:, 0:D]).then_inc(r_used, 1)

            def silu_gate(n, u):
                act.wait_ge(g_mm, n + 3)
                act.wait_ge(hid_ready, n + 1)
                act.activation(ex[u % 2][:, :], p_g[u % 2][:, 0:M], ACT.Silu).then_inc(silued, 1)

            def copy_hidden(n, u):
                act.wait_ge(h_mm, n + 3)
                act.wait_ge(y_mm, n + U - 1)
                act.copy(hidT[u % 2][:, :], p_h[u % 2][0:MH, 0:2 * P]).then_inc(h_used, 1)

            def trip(n, u, left=U):
                copy_hidden(n, u)
                if left >= 2:
                    silu_gate(n + 2, u + 2)
                if left >= 3:
                    copy_rows(n + 3, u + 3)

            act.preload_act_table(ACT.Silu)
            copy_rows(0, 0)
            for n in range(2):
                silu_gate(n, n)
                copy_rows(n + 1, n + 1)
            with act.Fori(0, (TILES - U) // U) as trip_no:
                i = trip_no * U
                for u in range(U):
                    trip(i + u, u)
            for u in range(U):
                trip(TILES - U + u, u, U - 1 - u)

        @block.vector
        def _(v):
            def silu(n, u):
                up = p_g[u % 2][:, M:2 * M]
                v.wait_ge(silued, n + 1)
                v.wait_ge(h_mm, n + 1)
                v.tensor_tensor(hid[u % 2][:, :], ex[u % 2][:, :], up, ALU.mult).then_inc(hid_ready, 1)

            def copy_y(n, u):
                v.wait_ge(y_mm, n + U + 1)
                v.wait_ge(y_out[u], (n - u) * (16 // U) + 16)
                v.tensor_copy(y[u][:, :], p_y[u % 2][:, 0:D]).then_inc(y_ready, 1)

            def copy_routed(i, u, again=True):
                n = i + u + 2 * T
                if again:
                    v.wait_ge(ranked[u], i * (16 // U))
                else:
                    v.wait_ge(y_out[u], 16 * 2 * T // U + 16)
                v.tensor_tensor(dest[u][:, :], rows[u][:, D:RW], own[:, ds(i + u, 1)], ALU.max)
                v.wait_ge(y_mm, n + U + 1)
                v.tensor_copy(y[u][:, :], p_y[u % 2][:, 0:D]).then_inc(y_ready, 1)

            v.wait_ge(tables, 32)
            for s in y_out:
                v.sem_inc(s, 16)
            for n in range(2):
                silu(n, n)
            def token_weights():
                step = Chain(v, vec)
                t3 = lambda z, n=E: z[:, :].rearrange("p (t n) -> p t n", n=n)
                step(v.tensor_tensor(wn[:, :], sc[:, :], chosen[:, :], ALU.mult))
                step(v.tensor_reduce(wsum[:, :], t3(wn), AX.X, ALU.add))
                step(v.reciprocal(wsum[:, :], wsum[:, :]))
                step(v.tensor_tensor(t3(wn), t3(wn), wsum[:, :].rearrange("p (t n) -> p t n", n=1).to_broadcast([P, T, E]),
                                     ALU.mult))
                for j in range(TOPK):
                    step(v.tensor_tensor(t3(tmp), t3(val), t3(vtop, 8)[:, :, j:j + 1].to_broadcast([P, T, E]),
                                         ALU.is_equal))
                    step(v.tensor_tensor(tmp[:, :], tmp[:, :], wn[:, :], ALU.mult))
                    step(v.tensor_reduce(t3(weight, 8)[:, :, j], t3(tmp), AX.X, ALU.add))

            def stage_tile(t, u, again):
                if again:
                    v.wait_ge(scattered[u], t * (16 * TOPK // ST))
                at = stage[u][:, :].rearrange("p (j n) -> p j n", j=TOPK)
                v.tensor_copy(at[:, :, 0:D], hall[:, ds((t + u) * D, D)].rearrange("p (j n) -> p j n", j=1)
                              .to_broadcast([P, TOPK, D]))
                v.tensor_copy(at[:, :, D], dests[:, ds((t + u) * TOPK, TOPK)])
                v.tensor_copy(stage_slot[u][:, 0:TOPK], slot[:, ds((t + u) * 8, TOPK)]).then_inc(staged, 1)

            def shared_tiles(i, t, again=True, last=False):
                for u in range(U):
                    if u in (0, 1, 3, 5):
                        stage_tile(t, (u + 1) // 2, again)
                    silu(i + u + 2, u + 2)
                    if last and u == U - 3:
                        token_weights()
                    copy_y(i + u, u)

            shared_tiles(0, 0, again=False)
            with v.Fori(1, T // ST - 1) as trip_no:
                shared_tiles(trip_no * U, trip_no * ST)
            shared_tiles(2 * T - U, T - ST, last=True)
            def routed_tiles(i, again=True, left=U + 2):
                for u in range(U):
                    if left - u > 2:
                        silu(2 * T + i + u + 2, u + 2)
                    copy_routed(i, u, again)

            ROUTED = TILES - 2 * T
            routed_tiles(0, again=False)
            with v.Fori(1, ROUTED // U - 1) as trip_no:
                routed_tiles(trip_no * U)
            routed_tiles(ROUTED - U, left=U)

        @block.tensor
        def _(pe):
            def turn_rows(n, u, ring):
                pe.wait_ge(row_ld[u % U], ring)
                pe.wait_ge(r_used, n + 1)
                for k in range(DK):
                    last = pe.transpose(p_r[u % 2][:, k * P:(k + 1) * P], rows[u % U][:, k * P:(k + 1) * P], ident[:, :])
                last.then_inc(r_mm, 1)

            def gate_up(n, u, ring):
                pe.wait_ge(r_used, n + 3)
                pe.wait_ge(w_ld[u % U], ring)
                pe.wait_ge(hid_ready, n + 1)
                for k in range(DK):
                    last = pe.matmul(p_g[u % 2][:, 0:2 * M], rT[u % 2][:, k * P:(k + 1) * P],
                                     w[u % U][:, k * 2 * M:(k + 1) * 2 * M], start=(k == 0), stop=(k == DK - 1))
                last.then_inc(g_mm, 1)

            def turn_hidden(n, u):
                pe.wait_ge(hid_ready, n + 3)
                pe.wait_ge(h_used, n + 1)
                for k in range(2):
                    last = pe.transpose(p_h[u % 2][0:MH, k * P:(k + 1) * P], hid[u % 2][:, k * MH:(k + 1) * MH], ident[:, :])
                last.then_inc(h_mm, 1)

            def down(n, u):
                pe.wait_ge(h_used, n + 3)
                pe.wait_ge(y_ready, n + 1)
                for k in range(2):
                    last = pe.matmul(p_y[u % 2][:, 0:D], hidT[u % 2][:, k * P:(k + 1) * P],
                                     w[u % U][0:MH, WIN + k * D:WIN + (k + 1) * D], start=(k == 0), stop=(k == 1))
                last.then_inc(y_mm, 1)

            def trip(i, u, ring, left=U):
                n = i + u
                turn_hidden(n, u)
                if left >= 2:
                    gate_up(n + 2, u + 2, ring + (16 if u + 2 >= U else 0))
                if left >= 3:
                    turn_rows(n + 3, u + 3, ring + (16 if u + 3 >= U else 0))
                down(n, u)

            turn_rows(0, 0, 16)
            for n in range(2):
                gate_up(n, n, 16)
                turn_rows(n + 1, n + 1, 16)
            with pe.Fori(0, (TILES - U) // U) as trip_no:
                i = trip_no * U
                for u in range(U):
                    trip(i, u, i * (16 // U) + 16)
            for u in range(U):
                trip(TILES - U, u, 16 * (TILES // U), U - 1 - u)


def combine(nc, x, mod, weight, ranked_dram, shared_dram, out):
    st = ExitStack()
    with st:
        def sb(name, cols, dt=F32):
            return st.enter_context(nc.sbuf_tensor(name, [P, cols], dt))

        def sem(name):
            return st.enter_context(nc.semaphore(name))

        PARTS = TOPK + 2
        B = 4
        got = [sb(f"got{n}", PARTS * D) for n in range(B)]
        acc = sb("acc", D)
        loaded = [sem(f"loaded{n}") for n in range(B)]
        scaled = sem("scaled5")
        used = sem("used5")
        done = sem("done5")
        written = sem("written5")
        vec = sem("vec5")
        block = st.enter_context(nc.Block())

        @block.sync
        def _(sp):
            sp.sem_inc(used, B)
            ranks = ranked_dram[SLOT_TILES * P:SLOT_TILES * P + TOPK * S, :].rearrange("(j t p) d -> t p j d", j=TOPK, p=P)
            halves = shared_dram.rearrange("(j t p) d -> t p j d", j=2, p=P)
            with sp.Fori(0, T // B) as trip_no:
                t = trip_no * B
                for u in range(B):
                    sp.wait_ge(used, t + u + 1)
                    for first, n, src in ((0, TOPK, ranks), (TOPK, 2, halves)):
                        sp.dma_start(got[u][:, first * D:(first + n) * D].rearrange("p (j d) -> p j d", j=n),
                                     src[ds(t + u, 1), :, :, :].rearrange("a p j d -> (a p) j d")).then_inc(loaded[u], 16)

        @block.gpsimd
        def _(gp):
            with gp.Fori(0, T) as t:
                gp.wait_ge(done, t + 1)
                gp.dma_start(out[ds(t * P, P), :], x[:, ds(t * D, D)]).then_inc(written, 16)
            gp.wait_ge(written, 16 * T)

        @block.scalar
        def _(act):
            with act.Fori(0, T // B) as trip_no:
                t = trip_no * B
                for u in range(B):
                    act.wait_ge(loaded[u], t * (32 // B) + 32)
                    for j in range(TOPK):
                        part = got[u][:, j * D:(j + 1) * D]
                        last = act.activation(part, part, ACT.Copy, scale=weight[:, ds((t + u) * 8 + j, 1)])
                    last.then_inc(scaled, 1)

        @block.vector
        def _(v):
            step = Chain(v, vec)
            with v.Fori(0, T // B) as trip_no:
                t = trip_no * B
                step.enter(t, 3)
                for u in range(B):
                    g = got[u]
                    xt = x[:, ds((t + u) * D, D)]
                    v.wait_ge(scaled, t + u + 1)
                    step(v.tensor_tensor(g[:, 0:4 * D], g[:, 0:4 * D], g[:, 4 * D:8 * D], ALU.add))
                    step(v.tensor_tensor(g[:, 0:2 * D], g[:, 0:2 * D], g[:, 2 * D:4 * D], ALU.add))
                    v.tensor_tensor(acc[:, :], g[:, 0:D], g[:, D:2 * D], ALU.add).then_inc(used, 1)
                    v.wait_ge(used, t + u + B + 1)
                    step(v.tensor_tensor(acc[:, :], acc[:, :], mod[:, 5 * D:6 * D], ALU.mult))
                    v.tensor_tensor(xt, xt, acc[:, :], ALU.add).then_inc(done, 1)
            step.leave(T, B)


def kernel(**inputs):
    import concourse.bacc as bacc
    from concourse.bass_utils import run_bass_kernel_spmd

    given = {n: np.asarray(v) for n, v in inputs.items()}
    f32 = np.float32
    pairs = np.concatenate([np.arange(0, ROPE, 2), np.arange(1, ROPE, 2)])
    qb = given["L0_attn_q_b_w"].reshape(H, QK, QR)
    qb = np.concatenate([qb[:, QK - ROPE:][:, pairs], qb[:, :QK - ROPE]], axis=1)
    kva = given["L0_attn_kv_a_w"]
    kva = np.concatenate([kva[C:][pairs], kva[:C]], axis=0)
    kvb = given["L0_attn_kv_b_w"].reshape(H, QK - ROPE + V, C)
    lnq = np.zeros((RT * P,), f32)
    lnq[:QR] = given["L0_attn_q_a_ln"]
    inv = (f32(1.0) / (f32(128000.0) ** (np.arange(0, ROPE, 2, dtype=f32) / f32(ROPE)))).astype(f32)
    angle = (inv[:, None] * np.arange(S, dtype=f32)[None, :]).astype(f32).astype(np.float64)
    cos, sin = np.cos(angle).astype(f32), np.sin(angle).astype(f32)
    sw_gate, sw_up, sw_down = (given[f"L0_ffn_sw_{n}"] for n in ("gate", "up", "down"))
    w_in = np.concatenate([given["L0_ffn_w_gate"], given["L0_ffn_w_up"]], axis=2)
    shared_in = np.stack([np.concatenate([sw_gate[:, i * M:(i + 1) * M], sw_up[:, i * M:(i + 1) * M]], axis=1)
                          for i in range(2)])
    w_in = np.concatenate([w_in, shared_in]).reshape(E + 2, DK, P, 2 * M).transpose(0, 2, 1, 3).reshape(E + 2, P, WIN)
    w_down = np.concatenate([given["L0_ffn_w_down"], sw_down.reshape(2, M, D)])
    w_out = np.zeros((E + 2, P, WOUT), f32)
    w_out[:, :MH] = w_down.reshape(E + 2, 2, MH, D).transpose(0, 2, 1, 3).reshape(E + 2, MH, WOUT)
    arrays = {
        "x": given["L0_attn_x"].reshape(S, D),
        "c": given["L0_c"].reshape(DK, P).T,
        "wmod": given["L0_wmod"],
        "wqaT": given["L0_attn_q_a_w"].T,
        "wqa": given["L0_attn_q_a_w"],
        "lnq": lnq.reshape(RT, P).T,
        "wqb": qb.transpose(1, 0, 2).reshape(P, H * QR),
        "wkvT": kva.T,
        "lnkv": np.broadcast_to(given["L0_attn_kv_a_ln"], (P, C)),
        "wk": kvb[:, :QK - ROPE].transpose(1, 0, 2).reshape(QK - ROPE, H * C),
        "wv": kvb[:, QK - ROPE:].transpose(1, 0, 2).reshape(V, H * C),
        "woT": given["L0_attn_o_w"].T.reshape(H, V, D).transpose(1, 0, 2).reshape(V, H * D),
        "cos": np.concatenate([cos, cos]),
        "sin": np.concatenate([sin, -sin]),
        "gate": given["L0_ffn_gate_w"],
        "experts": np.concatenate([w_in, w_out], axis=2),
        "lower": np.triu(np.ones((P, P), f32), 1),
        "own": np.arange(SLOT_TILES * P, dtype=f32).reshape(SLOT_TILES, P).T,
        "dests": (SLOT_TILES * P + np.arange(TOPK * S, dtype=f32)).reshape(TOPK, T, P).transpose(2, 1, 0).reshape(P, -1),
        "thresholds": np.broadcast_to(np.arange(T, dtype=f32) * P, (P, T)),
        "numbers": np.arange(SLOT_TILES, dtype=f32)[:, None],
    }
    nc = bacc.Bacc("TRN2", target_bir_lowering=False, num_devices=1)
    feed, aps = {}, {}
    for name, array in arrays.items():
        array = np.ascontiguousarray(array)
        feed[f"in_{name}"] = array
        aps[name] = nc.dram_tensor(f"in_{name}", array.shape, mybir.dt.from_np(array.dtype), kind="ExternalInput").ap()
    out = nc.dram_tensor("out", [S, D], F32, kind="ExternalOutput").ap()
    program(nc, aps, out)
    result = run_bass_kernel_spmd(nc, [feed], core_ids=[0])
    return result.results[0]["out"].reshape(1, S, D)
```
